# Optimizing a Trainium2 kernel written in Bass

```python
import numpy as np
import jax
import jax.numpy as jnp

def _softmax(x, axis=-1):
    return jax.nn.softmax(x, axis=axis)

def _gelu(x):
    return jax.nn.gelu(x, approximate=True)

def _silu(x):
    return jax.nn.silu(x)

def _sigmoid(x):
    return jax.nn.sigmoid(x)

def _layernorm(x, axis=-1, eps=1e-05):
    m = jnp.mean(x, axis=axis, keepdims=True)
    v = jnp.var(x, axis=axis, keepdims=True)
    return (x - m) / jnp.sqrt(v + eps)

def _scatter_add(tgt, idx, src, axis=0):
    return tgt.at[idx].add(src)

def _segment_sum(src, seg, n):
    return jax.ops.segment_sum(src, seg, n)
kernel_name = 'mk_early_fusion_d1_tok_img768_r4_190a8d'

def setup_inputs(seed: int=0):
    np.random.seed(seed)
    _w = jnp.asarray

    def _rec_inputs():
        import jax
        import jax.numpy as jnp
        _rk = jax.random.key(seed)
        x = -0.00016672 + 0.999947 * jax.random.normal(jax.random.fold_in(_rk, 1), (32, 3, 96, 96), jnp.float32)
        txt = 0.00389224 + 1.14309 * jax.random.normal(jax.random.fold_in(_rk, 2), (32, 128, 192), jnp.float32)
        return (x, txt)
    x, txt = _rec_inputs()

    def _L0_tok_setup():
        import jax, jax.numpy as jnp
        import numpy as np
        P = 16

        def _patchify(x, p):
            B, C, H, W = x.shape
            gh, gw = (H // p, W // p)
            x = x.reshape(B, C, gh, p, gw, p)
            x = x.transpose(0, 2, 4, 1, 3, 5)
            return x.reshape(B, gh * gw, C * p * p)
        key = jax.random.key(seed)
        k1, k2, k3, k4, k5 = jax.random.split(key, 5)
        B, C, H, Wd = (64, 3, 96, 96)
        emb = 192
        L = H // P * (Wd // P)
        return {'x': jax.random.normal(k1, (B, C, H, Wd), dtype=jnp.float32), 'W': jax.random.normal(k2, (emb, C * P * P), dtype=jnp.float32) * 0.02, 'b': jax.random.normal(k3, (emb,), dtype=jnp.float32) * 0.02, 'cls_tok': jax.random.normal(k4, (1, 1, emb), dtype=jnp.float32), 'pos_emb': jax.random.normal(k5, (1, L + 1, emb), dtype=jnp.float32)}
    _L0_tok_all = _L0_tok_setup()
    _L0_tok_in = {k: v for k, v in _L0_tok_all.items() if k in ('W', 'b', 'cls_tok', 'pos_emb')}
    del _L0_tok_all

    def _L0_attn_setup():
        import jax, jax.numpy as jnp
        import numpy as np
        HIDDEN = 192
        HEADS = 8
        key = jax.random.key(seed)
        ks = jax.random.split(key, 5)
        b, n = (2, 256)
        x = jax.random.normal(ks[0], (b, n, HIDDEN), dtype=jnp.float32)
        W_qkv = jax.random.normal(ks[1], (HIDDEN, 3 * HIDDEN * HEADS), dtype=jnp.float32) * 0.02
        b_qkv = jnp.zeros((3 * HIDDEN * HEADS,), dtype=jnp.float32)
        W_proj = jax.random.normal(ks[2], (HEADS * HIDDEN, HIDDEN), dtype=jnp.float32) * 0.02
        b_proj = jnp.zeros((HIDDEN,), dtype=jnp.float32)
        return {'x': x, 'W_qkv': W_qkv, 'b_qkv': b_qkv, 'W_proj': W_proj, 'b_proj': b_proj}
    _L0_attn_all = _L0_attn_setup()
    _L0_attn_in = {k: v for k, v in _L0_attn_all.items() if k in ('W_qkv', 'b_qkv', 'W_proj', 'b_proj')}
    del _L0_attn_all

    def _L0_ffn_setup():
        import jax, jax.numpy as jnp
        import numpy as np
        import math
        B, S, D = (4, 1024, 192)
        E = 8
        TOP_K = 2
        H = 512
        CAP_F = 1.25
        EPS = 1e-06
        ALPHA = 1.0
        key = jax.random.key(seed)
        k0, k1, k2, k3 = jax.random.split(key, 4)
        x = jax.random.normal(k0, (B, S, D), jnp.float32)
        gate_w = jax.random.normal(k1, (E, D), jnp.float32) * 0.02
        w13 = jax.random.normal(k2, (E, 2 * H, D), jnp.float32) * 0.02
        w2 = jax.random.normal(k3, (E, D, H), jnp.float32) * 0.02
        norm_w = jnp.ones((E, D), jnp.float32)
        return {'x': x, 'gate_w': gate_w, 'w13': w13, 'w2': w2, 'norm_w': norm_w}
    _L0_ffn_all = _L0_ffn_setup()
    _L0_ffn_in = {k: v for k, v in _L0_ffn_all.items() if k in ('gate_w', 'w13', 'w2', 'norm_w')}
    del _L0_ffn_all
    return {'x': x, 'txt': txt, 'L0_tok_W': _L0_tok_in['W'], 'L0_tok_b': _L0_tok_in['b'], 'L0_tok_cls_tok': _L0_tok_in['cls_tok'], 'L0_tok_pos_emb': _L0_tok_in['pos_emb'], 'L0_attn_W_qkv': _L0_attn_in['W_qkv'], 'L0_attn_b_qkv': _L0_attn_in['b_qkv'], 'L0_attn_W_proj': _L0_attn_in['W_proj'], 'L0_attn_b_proj': _L0_attn_in['b_proj'], 'L0_ffn_gate_w': _L0_ffn_in['gate_w'], 'L0_ffn_w13': _L0_ffn_in['w13'], 'L0_ffn_w2': _L0_ffn_in['w2'], 'L0_ffn_norm_w': _L0_ffn_in['norm_w']}

def reference(x, txt, L0_tok_W, L0_tok_b, L0_tok_cls_tok, L0_tok_pos_emb, L0_attn_W_qkv, L0_attn_b_qkv, L0_attn_W_proj, L0_attn_b_proj, L0_ffn_gate_w, L0_ffn_w13, L0_ffn_w2, L0_ffn_norm_w):
    import jax
    import jax.numpy as jnp

    def _L0_tok_ref(x, W, b, cls_tok, pos_emb):
        import jax, jax.numpy as jnp
        import numpy as np
        P = 16

        def _patchify(x, p):
            B, C, H, W = x.shape
            gh, gw = (H // p, W // p)
            x = x.reshape(B, C, gh, p, gw, p)
            x = x.transpose(0, 2, 4, 1, 3, 5)
            return x.reshape(B, gh * gw, C * p * p)
        B = x.shape[0]
        patches = _patchify(x, P)
        emb = jnp.einsum('blk,ek->ble', patches, W) + b
        cls = jnp.broadcast_to(cls_tok, (B, 1, cls_tok.shape[-1]))
        emb = jnp.concatenate([cls, emb], axis=1)
        return emb + pos_emb

    def _L0_attn_ref(x, W_qkv, b_qkv, W_proj, b_proj):
        import jax, jax.numpy as jnp
        import numpy as np
        HIDDEN = 192
        HEADS = 8
        b, n, c = x.shape
        qkv = x @ W_qkv + b_qkv
        q, k, v = jnp.split(qkv, 3, axis=-1)
        q = q.reshape(b, HEADS, n, HIDDEN)
        k = k.reshape(b, HEADS, n, HIDDEN)
        v = v.reshape(b, HEADS, n, HIDDEN)
        energy = jnp.einsum('bhqd,bhkd->bhqk', q, k)
        scaling = jnp.float32(HIDDEN ** 0.5)
        attn = jax.nn.softmax(energy, axis=-1) / scaling
        out = jnp.einsum('bhal,bhlv->bhav', attn, v)
        out = out.reshape(b, n, HEADS * HIDDEN)
        return out @ W_proj + b_proj

    def _L0_ffn_ref(x, gate_w, w13, w2, norm_w):
        import jax, jax.numpy as jnp
        import numpy as np
        import math
        B, S, D = (4, 1024, 192)
        E = 8
        TOP_K = 2
        H = 512
        CAP_F = 1.25
        EPS = 1e-06
        ALPHA = 1.0
        Bx, Sx, Dx = x.shape
        N = Bx * Sx
        cap = int(math.ceil(CAP_F * TOP_K * N / E))
        xf = x.reshape(N, Dx)
        logits = xf.astype(jnp.float32) @ gate_w.T
        probs = jax.nn.softmax(logits, axis=-1)
        top_p, top_i = jax.lax.top_k(probs, TOP_K)
        w = top_p / jnp.sum(top_p, axis=-1, keepdims=True)
        flat_e = top_i.reshape(-1)
        onehot = jax.nn.one_hot(flat_e, E, dtype=jnp.int32)
        pos = jnp.take_along_axis(jnp.cumsum(onehot, axis=0) - 1, flat_e[:, None], axis=1)[:, 0]
        keep = pos < cap
        didx = flat_e * cap + jnp.minimum(pos, cap - 1)
        safe = jnp.where(keep, didx, E * cap)
        x_rep = jnp.repeat(xf, TOP_K, axis=0)
        buf = jnp.zeros((E * cap + 1, Dx), x.dtype).at[safe].set(x_rep)
        buf = buf[:-1].reshape(E, cap, Dx)
        z = 2.0 * buf
        z = z * jax.lax.rsqrt(jnp.mean(z * z, axis=-1, keepdims=True) + EPS)
        z = z * norm_w[:, None, :]
        gu = jnp.einsum('ecd,ehd->ech', z, w13)
        g, u = jnp.split(gu, 2, axis=-1)
        y = buf + ALPHA * jnp.einsum('ech,edh->ecd', jax.nn.silu(g) * u, w2)
        y_tok = y.reshape(E * cap, Dx)[didx]
        cw = (w.reshape(-1) * keep.astype(w.dtype)).astype(x.dtype)
        out = (cw[:, None] * y_tok).reshape(N, TOP_K, Dx).sum(axis=1)
        return out.reshape(Bx, Sx, Dx)
    h = _L0_tok_ref(x, L0_tok_W, L0_tok_b, L0_tok_cls_tok, L0_tok_pos_emb)
    h = jnp.concatenate([h, txt], axis=1)
    h = h + _L0_attn_ref(_layernorm(h, axis=-1), L0_attn_W_qkv, L0_attn_b_qkv, L0_attn_W_proj, L0_attn_b_proj)
    h = h + _L0_ffn_ref(_layernorm(h, axis=-1), L0_ffn_gate_w, L0_ffn_w13, L0_ffn_w2, L0_ffn_norm_w)
    return h

_drawn_inputs = setup_inputs


def setup_inputs(seed=0):
    import zlib

    import numpy as np

    out = dict(_drawn_inputs(seed))
    spreads = {'L0_attn_b_qkv': (0.0, 0.8), 'L0_attn_b_proj': (0.0, 0.1), 'L0_ffn_norm_w': (1.0, 0.6)}
    factors = {'L0_tok_b': 6.849,
     'L0_attn_W_qkv': 8.0,
     'L0_attn_W_proj': 8.0,
     'L0_ffn_gate_w': 8.0,
     'L0_ffn_w13': 8.0,
     'L0_ffn_w2': 8.0}
    for name, (base, spread) in spreads.items():
        noise = np.random.default_rng([zlib.crc32(name.encode()), seed]).standard_normal(out[name].shape)
        drawn = base * np.exp(spread * noise) if base else spread * noise
        out[name] = jnp.asarray(drawn.astype(out[name].dtype))
    for name, factor in factors.items():
        out[name] = (out[name] * factor).astype(out[name].dtype)
    return out
```

```python
from contextlib import ExitStack

import concourse.bass as bass
from concourse import mybir

F32 = mybir.dt.float32
F32R = mybir.dt.float32r
I32 = mybir.dt.int32
ALU = mybir.AluOpType
ACT = mybir.ActivationFunctionType
AXIS = mybir.AxisListType

HEADS = 8
PATCH = 16
HIDDEN = 512
TOP_K = 2
TICKS = 64
CHUNKS = 4
TILES = 4
LN_EPS = 1e-5
RMS_EPS = 1e-6


class Count:

    def __init__(self, before, first, each):
        self.before, self.first, self.each = before, first, each

    def start(self, turn):
        if isinstance(turn, int) and turn == 0:
            return self.before
        return (turn - 1) * self.each + (self.before + self.first)


class Uses:

    WHO = {"q": "ad", "k": "ad", "zt": "a", "xt": "ad", "log": "d", "cnt": "d", "pv": "ad", "y": "d"}

    def __init__(self, banks):
        qkv = [("q", n) for n in range(4)] + [("k", n) for n in range(4)]
        prior = [("zt", 0)]
        nxt = [("xt", 0)]
        v = [("v", n) for n in range(8)]
        att = [("pv", g) for g in range(HEADS)]
        att_mid = att[:2] + [("cnt", 0)] + att[2:]
        y = [("y", 0), ("y", 1)]
        self.lists = {
            "before": nxt + v,
            "first": qkv + nxt + v + att + y,
            "mid": qkv + prior + nxt + [("log", 0)] + v + att_mid + y,
            "last": qkv + prior + [("log", 0)] + att_mid + y,
            "after": [("zt", 0), ("log", 0), ("cnt", 0)],
        }
        self.banks = banks
        assert len(self.lists["mid"]) % banks == 0

    @staticmethod
    def who(name):
        if name[0] == "v":
            return "a" if name[1] % 2 == 0 else "d"
        return Uses.WHO[name[0]]

    def size(self, part, e=None):
        return sum(1 for n in self.lists[part] if e is None or e in self.who(n))

    def count(self, e):
        return Count(self.size("before", e), self.size("first", e), self.size("mid", e))


def split(x):
    return 128, x - 128


def build(nc, x, txt, tok_w, tok_b, cls_tok, pos_emb, w_qkv, b_qkv, w_proj, b_proj, gate_w, w13, w2, norm_w, out):
    B, C, IMG, _ = x.shape
    TXT, D = txt.shape[1:]
    GRID = IMG // PATCH
    IMG_T = GRID * GRID + 1
    S = IMG_T + TXT
    N = B * S
    E = gate_w.shape[0]
    CAP = -(-5 * TOP_K * N // (4 * E))
    D0, D1 = split(D)
    T0 = (S + 1) // 2
    T1 = S - T0
    SP = S + 1
    ROWS = S * HEADS
    W = HEADS * D
    ROW = D + 1 + E
    TM = -(-CAP // (CHUNKS * TILES))
    TM += TM % 2
    SLOTS = CHUNKS * TILES * TM
    CN = TILES * TM
    HT = HIDDEN // 128
    ADDED = 16 * TILES * CHUNKS // 2
    KP = C * PATCH * PATCH
    KT = KP // 128
    SEQS = min(B, 16)
    RT = B // SEQS
    IR = SEQS * GRID
    PY = PATCH * IMG
    LAST = B - 1
    GB = 5
    uses = Uses(GB)

    images_rows = nc.dram_tensor("images_rows", (B, IMG_T, D), F32, kind="Internal").ap()
    v_rows = nc.dram_tensor("v_rows", (ROWS, D), F32, kind="Internal").ap()
    slot_rows = nc.dram_tensor("slot_rows", (E * SLOTS + 4 * T0, ROW), F32, kind="Internal").ap()

    persistent = ExitStack()
    with persistent:
        def sb(name, shape, dt=F32, at=None):
            return (at or persistent).enter_context(nc.sbuf_tensor(name, shape, dt))

        def sem(name):
            return persistent.enter_context(nc.semaphore(name))

        bank = [persistent.enter_context(nc.psum_tensor(f"bank{n}", [128, 512], F32)) for n in range(8)]
        ring = bank[:GB]
        score_bank = bank[5:7]
        probs_t_bank = bank[7]

        ident = sb("ident", [128, 128])
        earlier = sb("earlier", [T0, T0])
        ones = sb("ones", [T0, T0])
        expert_no = sb("expert_no", [T0, 2, E])
        slot_base = sb("slot_base", [T0, 2, E])
        dump_row = sb("dump_row", [T0, 2, TOP_K])
        real = sb("real", [T0, 2, 1])
        minus_half = sb("minus_half", [128, 4])
        tick = sb("tick", [1, 3 * TICKS])
        norm_cols = sb("norm_cols", [128, 2, E])

        const_made = sem("const_made")
        const_ready = sem("const_ready")
        const_loaded = sem("const_loaded")
        slots_cleared = sem("slots_cleared")
        w_loaded = sem("w_loaded")
        w_high = sem("w_high")
        w_low = sem("w_low")
        bias_loaded = sem("bias_loaded")
        bias_high = sem("bias_high")
        images_loaded = sem("images_loaded")
        image_args_loaded = sem("image_args_loaded")
        regrouped = sem("regrouped")
        token_bias = sem("token_bias")
        pt_full = sem("pt_full")
        pt_high = sem("pt_high")
        pt_low = sem("pt_low")
        emb_full = sem("emb_full")
        emb_free = sem("emb_free")
        emb_stored = sem("emb_stored")
        stage1_done = sem("stage1_done")

        attention = ExitStack()

        def sa(name, shape, dt=F32):
            return sb(name, shape, dt, attention)

        wq_h = sa("wq_h", [128, 3 * W], F32R)
        wq_l = sa("wq_l", [128, 3 * W], F32R)
        wq_hl = sa("wq_hl", [128, 3 * W], F32R)
        wq_hb = sa("wq_hb", [128, 3 * W], F32R)
        wp_h = sa("wp_h", [128, HEADS, D], F32R)
        wp_l = sa("wp_l", [128, HEADS, D], F32R)
        wp_hl = sa("wp_hl", [128, HEADS, D], F32R)
        proj_bias = sa("proj_bias", [T0, D])
        gate_t = sa("gate_t", [128, 2, E])

        stage1 = ExitStack()

        def s1(name, shape, dt=F32):
            return sb(name, shape, dt, stage1)

        w_raw = s1("w_raw", [128, 2, W])
        img = s1("img", [IR, C, PY])
        img_grouped = s1("img_grouped", [IR, GRID, KP])
        tok_raw = s1("tok_raw", [128, 2, KP])
        tok_h = s1("tok_h", [128, KT, D], F32R)
        tok_l = s1("tok_l", [128, KT, D], F32R)
        pt_h = s1("pt_h", [128, KT, IR], F32R)
        pt_l = s1("pt_l", [128, KT, IR], F32R)
        pos = s1("pos", [IR, GRID * D])
        tok_bias = s1("tok_bias", [IR, D])
        emb = s1("emb", [IR, GRID, D])
        cls = s1("cls", [B, D])
        cls_pos = s1("cls_pos", [B, D])
        init_row = s1("init_row", [TM, CHUNKS * TILES, ROW])
        stage1.close()

        q_h = sa("q_h", [128, 2, ROWS + 1], F32R)
        q_l = sa("q_l", [128, ROWS + 1], F32R)
        q_l1 = sa("q_l1", [64, ROWS + 1], F32R)
        k_h = sa("k_h", [128, ROWS + 1], F32R)
        k_l = sa("k_l", [128, ROWS + 1], F32R)
        k_hl = sa("k_hl", [128, ROWS + 1], F32R)
        o_h = sa("o_h", [128, 2, ROWS], F32R)
        o_l = sa("o_l", [128, ROWS], F32R)
        o_l1 = sa("o_l1", [64, ROWS], F32R)
        v_h = sa("v_h", [T0, HEADS, 2, D], F32R)
        v_l = sa("v_l", [T0, HEADS, 2, D], F32R)
        v_out = sa("v_out", [T0, 4, 2 * D])
        probs = sa("probs", [T0, 3, 2, SP])
        pt2_h = sa("pt2_h", [T0, 2, 2, SP], F32R)
        pt2_l = sa("pt2_l", [T0, 2, 2, SP], F32R)
        xt_h = sa("xt_h", [128, 2, SP], F32R)
        xt_l = sa("xt_l", [128, SP], F32R)
        xt_l1 = sa("xt_l1", [128, SP], F32R)
        h_in = sa("h_in", [T0, 2, D])
        h_res = sa("h_res", [T0, 2, D])
        x_norm = sa("x_norm", [T0, 2, D + D1])
        h_mid = sa("h_mid", [T0, 2, D])
        z_row = sa("z_row", [T0, 2, ROW])
        z_t = sa("z_t", [128, 2, S])
        neg_max = sa("neg_max", [T0, HEADS, 2])
        row_sum = sa("row_sum", [T0, HEADS, 2])
        row_inv = sa("row_inv", [T0, HEADS, 2])
        stats = sa("stats", [T0, 2, 2, 6])
        mean_var = sa("mean_var", [T0, 2, 2, 2])
        rs = sa("rs", [T0, 2, 4, 2])
        logits = sa("logits", [T0, 2, E])
        rt = sa("rt", [T0, 12, 2, E])
        r1 = sa("r1", [T0, 8, 2, 1])
        counts = sa("counts", [T0, 3, E])
        base = sa("base", [T0, E])
        slot_of = sa("slot_of", [T0, 2, TOP_K, E])
        slot_f = sa("slot_f", [T0, 2, TOP_K, 1])
        slot_i = sa("slot_i", [T0, 2, TOP_K], I32)
        attention.close()

        experts = ExitStack()

        def se(name, shape, dt=F32):
            return sb(name, shape, dt, experts)

        up_raw = se("up_raw", [128, 2 * HT, D + D1])
        down_raw = se("down_raw", [128, 2, HIDDEN])
        up_h = se("up_h", [128, 2 * HT, 128], F32R)
        up_l = se("up_l", [128, 2 * HT, 128], F32R)
        up_hl = se("up_hl", [128, 2 * HT, 128], F32R)
        down_h = se("down_h", [128, HT, D], F32R)
        down_l = se("down_l", [128, HT, D], F32R)
        zs_in = se("zs_in", [TM, 2, TILES, ROW])
        zs = se("zs", [TM, 2, TILES, D + D1])
        zw = se("zw", [TM, CHUNKS, TILES, D])
        square = se("square", [TM, D])
        zr = se("zr", [TM, 2, 5, TILES])
        zst_h = se("zst_h", [128, 2, 2, CN], F32R)
        zst_l = se("zst_l", [128, 2, 2, CN], F32R)
        silu = se("silu", [128, HT, CN])
        act = se("act", [128, 2, HT, CN])
        act_h = se("act_h", [128, 2, HT, CN], F32R)
        act_l = se("act_l", [128, 2, HT, CN], F32R)
        y_out = se("y_out", [TM, 2, TILES, D])
        token_i = se("token_i", [TM, CHUNKS, TILES], I32)
        weight = se("weight", [TM, CHUNKS, TILES])
        experts.close()

        pads_ready = sem("pads_ready")
        h_loaded = sem("h_loaded")
        res_loaded = sem("res_loaded")
        res_biased = sem("res_biased")
        ln1_stats = sem("ln1_stats")
        ln1_rs = sem("ln1_rs")
        x_ready = sem("x_ready")
        ring_full = sem("ring_full")
        ring_act = sem("ring_act")
        ring_dve = sem("ring_dve")
        q_doubled = sem("q_doubled")
        v_stored = [sem(f"v_stored{n}") for n in range(4)]
        v_loaded = sem("v_loaded")
        v_high = sem("v_high")
        v_ready = sem("v_ready")
        scores_full = sem("scores_full")
        max_ready = sem("max_ready")
        exp_done = sem("exp_done")
        inv_ready = sem("inv_ready")
        probs_ready = sem("probs_ready")
        probs_t_full = sem("probs_t_full")
        probs_t_high = sem("probs_t_high")
        probs_t_low = sem("probs_t_low")
        h_mid_ready = sem("h_mid_ready")
        h_mid_stored = sem("h_mid_stored")
        ln2_stats = sem("ln2_stats")
        ln2_rs = sem("ln2_rs")
        z_ready = sem("z_ready")
        route_sub = sem("route_sub")
        route_exp = sem("route_exp")
        chosen = sem("chosen")
        counts_ready = sem("counts_ready")
        slots_ranked = sem("slots_ranked")
        slots_ready = sem("slots_ready")
        rows_scattered = sem("rows_scattered")
        dve_step = sem("dve_step")
        stats_step = [sem(f"stats_step{n}") for n in range(2)]
        pool_step = sem("pool_step")
        stage2_done = sem("stage2_done")

        ew_loaded = sem("ew_loaded")
        ew_full = sem("ew_full")
        ew_high = sem("ew_high")
        ew_low = sem("ew_low")
        z_loaded = [sem(f"z_loaded{n}") for n in range(2)]
        z_square = sem("z_square")
        z_scale = sem("z_scale")
        z_scaled = sem("z_scaled")
        z_weighted = sem("z_weighted")
        zt_full = sem("zt_full")
        zt_high = sem("zt_high")
        zt_low = sem("zt_low")
        gu_full = sem("gu_full")
        silu_ready = sem("silu_ready")
        act_ready = sem("act_ready")
        act_high = sem("act_high")
        act_low = sem("act_low")
        y_full = sem("y_full")
        y_ready = sem("y_ready")
        y_added = [sem(f"y_added{n}") for n in range(2)]

        block = persistent.enter_context(nc.Block())

        def load_tokens(eng, dst, b, signal):
            eng.dma_start(dst[0:IMG_T, 0, :], images_rows[b]).then_inc(signal, 16)
            eng.dma_start(dst[IMG_T:T0, 0, :], txt[b, 0:T0 - IMG_T, :]).then_inc(signal, 16)
            eng.dma_start(dst[0:T1, 1, :], txt[b, T0 - IMG_T:TXT, :]).then_inc(signal, 16)

        def position(part, turn, name, e=None):
            seq = [n for n in uses.lists[part] if e is None or e in uses.who(n)]
            c = uses.count(e)
            begin = {"before": 0, "after": None}.get(part, c.start(turn))
            if part == "after":
                begin = c.start(LAST) + uses.size("last", e)
            return begin + (seq.index(name) + 1)

        def part_of(turn):
            if not isinstance(turn, int):
                return "mid"
            return "first" if turn == 0 else "last" if turn == LAST else "mid"

        def ring_bank(part, name):
            begin = {"before": 0, "first": uses.size("before")}.get(part)
            if begin is None:
                begin = uses.size("before") + uses.size("first")
            if part == "after":
                begin += uses.size("last")
            return ring[(begin + uses.lists[part].index(name)) % GB]

        def carried(eng, row, carrier):
            cell = 1

            def wait(signal, value):
                nonlocal cell
                eng.wait_ge(signal, value)
                if not isinstance(value, int):
                    at = TICKS * row + cell
                    carrier(tick[0:1, at:at + 1])
                    cell += 1
            return wait

        def step_counter(eng, signal, wait=None):
            class Steps:
                start, n = 0, 0

                def turn(self, start):
                    self.start, self.n = start, 0

                def __call__(self, ins, carry=False):
                    self.n += 1
                    ins.then_inc(signal, 1)
                    (wait if wait and carry else eng.wait_ge)(signal, self.start + self.n)
            return Steps()

        @block.sync
        def _(sp):
            def load_w(dst, src, third, signal):
                if third == 2:
                    sp.dma_start(dst, src).then_inc(signal, 16)
                    return
                to = dst.rearrange("p (n c) -> p n c", c=2 * D)
                of = src.rearrange("p (n k d) -> p n k d", k=2, d=D)
                for k in range(2):
                    sp.dma_start(to[:, :, 128 * k:128 * k + 128], of[:, :, k, 0:128]).then_inc(signal, 16)
                    sp.dma_start(to[:, :, 256 + D1 * k:256 + D1 * k + D1], of[:, :, k, 128:D]).then_inc(signal, 16)

            sp.dma_start(proj_bias[:], b_proj.rearrange("(a d) -> a d", a=1).to_broadcast([T0, D])).then_inc(const_loaded, 16)
            with nc.allow_non_contiguous_dma(reason="few small columns"):
                gate_cols = gate_w.rearrange("e d -> d e")
                sp.dma_start(gate_t[:, 0, :], gate_cols[0:128, :]).then_inc(const_loaded, 16)
                sp.dma_start(gate_t[0:D1, 1, :], gate_cols[128:D, :]).then_inc(const_loaded, 16)
                norm_c = norm_w.rearrange("e d -> d e")
                sp.dma_start(norm_cols[:, 0, :], norm_c[0:128, :]).then_inc(const_loaded, 16)
                sp.dma_start(norm_cols[0:D1, 1, :], norm_c[128:D, :]).then_inc(const_loaded, 16)
                sp.dma_start(norm_cols[D1:2 * D1, 1, :], norm_c[128:D, :]).then_inc(const_loaded, 16)
            sp.dma_start(tok_raw[:, 0, :], tok_w[0:128, :]).then_inc(image_args_loaded, 16)
            sp.dma_start(tok_raw[0:D1, 1, :], tok_w[128:D, :]).then_inc(image_args_loaded, 16)
            sp.dma_start(tok_bias[:], tok_b.rearrange("(a d) -> a d", a=1).to_broadcast([IR, D])).then_inc(image_args_loaded, 16)
            pos_rows = pos_emb[0, 1:IMG_T, :].rearrange("(h w) d -> h (w d)", w=GRID)
            for s in range(SEQS):
                sp.dma_start(pos[s * GRID:(s + 1) * GRID, :], pos_rows).then_inc(image_args_loaded, 16)
            sp.dma_start(cls[:], cls_tok[0].to_broadcast([B, D])).then_inc(image_args_loaded, 16)
            sp.dma_start(cls_pos[:], pos_emb[0, 0:1, :].to_broadcast([B, D])).then_inc(image_args_loaded, 16)
            for r in range(RT):
                if r:
                    sp.wait_ge(regrouped, r)
                for s in range(SEQS):
                    src = x[r * SEQS + s].rearrange("c (g y) w -> g c (y w)", y=PATCH)
                    sp.dma_start(img[s * GRID:(s + 1) * GRID, :, :], src).then_inc(images_loaded, 16)
            for n in range(3):
                if n:
                    sp.wait_ge(w_low, n)
                cols = slice(n * W, (n + 1) * W)
                load_w(w_raw[:, 0, :], w_qkv[0:128, cols], n, w_loaded)
                for half in range(2):
                    load_w(w_raw[half * D1:(half + 1) * D1, 1, :], w_qkv[128:D, cols], n, w_loaded)
            sp.wait_ge(w_low, 3)
            wp = w_proj.rearrange("(h d) n -> d h n", d=D)
            as_heads = w_raw[:].rearrange("p a (h n) -> p a h n", h=HEADS)
            sp.dma_start(as_heads[:, 0], wp[0:128]).then_inc(w_loaded, 16)
            for half in range(2):
                sp.dma_start(as_heads[half * D1:(half + 1) * D1, 1], wp[128:D]).then_inc(w_loaded, 16)
            sp.wait_ge(w_low, 4)
            for row in (64, 96):
                for n in range(2):
                    load_w(w_raw[row:row + 1, n, :], b_qkv[n * W:(n + 1) * W].rearrange("(a d) -> a d", a=1), n, bias_loaded)
            sp.wait_ge(bias_high, 2)
            for row in (64, 96):
                sp.dma_start(w_raw[row:row + 1, 0, :], b_qkv[2 * W:3 * W].rearrange("(a d) -> a d", a=1)).then_inc(bias_loaded, 16)
            for r in range(RT):
                sp.wait_ge(emb_free, GRID * (r + 1))
                for s in range(SEQS):
                    dst = images_rows[r * SEQS + s, 1:IMG_T, :].rearrange("(h w) d -> h w d", w=GRID)
                    sp.dma_start(dst, emb[s * GRID:(s + 1) * GRID, :, :]).then_inc(emb_stored, 16)
            sp.wait_ge(token_bias, 2)
            sp.dma_start(images_rows[:, 0, :], cls[:]).then_inc(emb_stored, 16)
            sp.wait_ge(emb_stored, 16 * (B + 1))
            sp.wait_ge(slots_cleared, 16 * (E + 1))

            def v_chunk(n):
                t, c = n // 4, n % 4
                rows = v_rows.rearrange("(s h) d -> s (h d)", h=HEADS)
                return rows[t * T0:t * T0 + (T1 if t else T0), c * 2 * D:(c + 1) * 2 * D]

            def store_v(b, turn, part):
                for n in range(8):
                    e = "a" if n % 2 == 0 else "d"
                    sp.wait_ge(ring_act if e == "a" else ring_dve, position(part, turn, ("v", n), e))
                    m = T1 if n // 4 else T0
                    sp.dma_start(v_chunk(n), v_out[0:m, n % 4, :]).then_inc(v_stored[n % 4], 16)

            def load_v(b):
                for stored in v_stored:
                    sp.wait_ge(stored, b * 32 + 32)
                heads = v_rows.rearrange("(h s) d -> s h d", h=HEADS)
                sp.dma_start(v_l[:, :, 0, :].bitcast(F32), heads[0:T0]).then_inc(v_loaded, 16)
                sp.dma_start(v_l[0:T1, :, 1, :].bitcast(F32), heads[T0:S]).then_inc(v_loaded, 16)

            def turn(i, part):
                if part != "last":
                    sp.wait_ge(x_ready, i + 1)
                    load_tokens(sp, h_in, i + 1, h_loaded)
                if part != "first":
                    sp.wait_ge(h_mid_ready, i)
                load_tokens(sp, h_res, i, res_loaded)
                sp.wait_ge(ring_dve, position(part, i, ("q", 3), "d"))
                sp.dma_start(q_h[64:128, 1, 0:ROWS].bitcast(F32), q_h[0:64, 1, 0:ROWS].bitcast(F32)).then_inc(q_doubled, 16)
                if part != "last":
                    sp.wait_ge(v_loaded, i * 32 + 32)
                    store_v(i + 1, i, part)
                    sp.wait_ge(ring_full, position(part, i, ("pv", HEADS - 1)))
                    load_v(i + 1)
                sp.wait_ge(h_mid_ready, i + 1)
                sp.dma_start(out[bass.ds(i * S, T0), :], h_mid[:, 0, :]).then_inc(h_mid_stored, 16)
                sp.dma_start(out[bass.ds(i * S + T0, T1), :], h_mid[0:T1, 1, :]).then_inc(h_mid_stored, 16)

            sp.wait_ge(stage1_done, 4)
            sp.wait_ge(pads_ready, 1)
            load_tokens(sp, h_in, 0, h_loaded)
            store_v(0, 0, "before")
            load_v(0)
            turn(0, "first")
            with sp.Fori(1, LAST) as i:
                turn(i, "mid")
            turn(LAST, "last")
            sp.wait_ge(rows_scattered, 64 * B)
            sp.wait_ge(h_mid_stored, 32 * B)
            sp.wait_ge(stage2_done, 4)

            def expert(e, first):
                if not first:
                    sp.wait_ge(ew_full, e * (3 * HT))
                sp.dma_start(up_raw[:, :, 0:D], w13[e].rearrange("(t p) d -> p t d", p=128)).then_inc(ew_loaded, 16)
                sp.dma_start(up_raw[:, :, D:], w13[e].rearrange("(t p) d -> p t d", p=128)[:, :, 128:D]).then_inc(ew_loaded, 16)
                sp.dma_start(down_raw[:, 0, :], w2[e, 0:128, :]).then_inc(ew_loaded, 16)
                sp.dma_start(down_raw[0:D1, 1, :], w2[e, 128:D, :]).then_inc(ew_loaded, 16)
                for c in range(CHUNKS):
                    if not (first and c < 2):
                        sp.wait_ge(z_scaled, e * CHUNKS + (c - 1))
                        sp.wait_ge(z_weighted, e * CHUNKS + (c - 1))
                    src = slot_rows[bass.ds(e * SLOTS + c * CN, CN), :].rearrange("(t p) d -> p t d", p=TM)
                    sp.dma_start(zs_in_of(e, c), src).then_inc(z_loaded[c % 2], 16)

            def zs_in_of(e, c):
                return zs_in[:, c % 2, :, :]
            expert(0, True)
            with sp.Fori(1, E) as e:
                expert(e, False)
            for added in y_added:
                sp.wait_ge(added, ADDED * E)

        @block.gpsimd
        def _(pool):
            wait = carried(pool, 0, lambda to: nc.gpsimd.tensor_tensor(to, tick[0:1, 0:1], tick[0:1, 0:1], ALU.add))
            step = step_counter(pool, pool_step, wait)
            nc.gpsimd.memset(ident[:], 0.0).then_inc(const_made, 1)
            nc.gpsimd.memset(earlier[:], 1.0).then_inc(const_made, 1)
            nc.gpsimd.memset(real[:], 1.0).then_inc(const_made, 1)
            nc.gpsimd.memset(tick[:], 0.0).then_inc(const_made, 1)
            nc.gpsimd.memset(init_row[:], 0.0).then_inc(const_made, 1)
            pool.wait_ge(const_made, 5)
            nc.gpsimd.affine_select(out=ident[:], in_=ident[:], compare_op=ALU.not_equal, fill=1.0, base=0,
                                    pattern=[[-1, 128]], channel_multiplier=1).then_inc(const_ready, 1)
            nc.gpsimd.affine_select(out=earlier[:], in_=earlier[:], compare_op=ALU.is_gt, fill=0.0, base=0,
                                    pattern=[[1, T0]], channel_multiplier=-1).then_inc(const_ready, 1)
            nc.gpsimd.affine_select(out=real[:], in_=real[:], compare_op=ALU.is_gt, fill=0.0, base=S,
                                    pattern=[[-T0, 2], [0, 1]], channel_multiplier=-1).then_inc(const_ready, 1)
            nc.gpsimd.memset(ones[:], 1.0).then_inc(const_ready, 1)
            nc.gpsimd.memset(minus_half[:], -0.5).then_inc(const_ready, 1)
            nc.gpsimd.iota(expert_no[:], pattern=[[0, 2], [1, E]], base=0, channel_multiplier=0,
                           allow_small_or_imprecise_dtypes=True).then_inc(const_ready, 1)
            nc.gpsimd.iota(slot_base[:], pattern=[[0, 2], [SLOTS, E]], base=0, channel_multiplier=0,
                           allow_small_or_imprecise_dtypes=True).then_inc(const_ready, 1)
            nc.gpsimd.iota(dump_row[:], pattern=[[2 * T0, 2], [T0, TOP_K]], base=E * SLOTS, channel_multiplier=1,
                           allow_small_or_imprecise_dtypes=True).then_inc(const_ready, 1)
            nc.gpsimd.iota(init_row[:, :, D:D + 1], pattern=[[TM, CHUNKS * TILES], [0, 1]], base=N, channel_multiplier=1,
                           allow_small_or_imprecise_dtypes=True).then_inc(const_ready, 1)
            pool.wait_ge(const_ready, 9)
            for e in range(E):
                dst = slot_rows[e * SLOTS:(e + 1) * SLOTS, :].rearrange("(t p) d -> p t d", p=TM)
                pool.dma_start(dst, init_row[:]).then_inc(slots_cleared, 16)
            pool.dma_start(out[N:N + SLOTS, :].rearrange("(t p) d -> p t d", p=TM), init_row[:, :, 0:D]).then_inc(slots_cleared, 16)
            for r in range(RT):
                pool.wait_ge(images_loaded, 16 * SEQS * (r + 1))
                if r:
                    pool.wait_ge(pt_full, KT + 2 * GRID * r)
                for gw in range(GRID):
                    src = img[:].rearrange("p c (y g x) -> p (c y) g x", g=GRID, x=PATCH)[:, :, gw, :]
                    last = nc.gpsimd.tensor_copy(img_grouped[:, gw, :].rearrange("p (r x) -> p r x", x=PATCH), src)
                last.then_inc(regrouped, 1)
            pool.wait_ge(emb_stored, 16 * (B + 1))
            pool.wait_ge(slots_cleared, 16 * (E + 1))
            pool.engine_nop().then_inc(stage1_done, 1)
            pool.wait_ge(stage1_done, 4)

            def rs_steps(which, n):
                v, y, t, u = (rs[:, which, k, :] for k in range(4))
                step(nc.gpsimd.tensor_scalar(v, mean_var[:, which, :, 1], LN_EPS, None, ALU.add))
                step(nc.gpsimd.tensor_tensor(y, v, minus_half[0:T0, 0:2], ALU.pow))
                step(nc.gpsimd.tensor_tensor(t, y, y, ALU.mult))
                step(nc.gpsimd.tensor_tensor(t, t, v, ALU.mult), carry=True)
                step(nc.gpsimd.tensor_scalar(u, t, -0.5, 1.5, ALU.mult, ALU.add))
                return nc.gpsimd.tensor_tensor(y, y, u, ALU.mult)

            def split_v(b):
                wait(v_loaded, b * 32 + 32)
                for g in range(0, HEADS, 4):
                    step(nc.gpsimd.tensor_copy(v_h[:, g:g + 4], v_l[:, g:g + 4].bitcast(F32)))
                    nc.gpsimd.tensor_tensor(v_l[:, g:g + 4], v_l[:, g:g + 4].bitcast(F32), v_h[:, g:g + 4].bitcast(F32),
                                            ALU.subtract).then_inc(v_ready, 1)

            def ln1(b):
                wait(ln1_stats, b + 1)
                rs_steps(0, b).then_inc(ln1_rs, 1)

            def rank(b, first):
                pool.wait_ge(counts_ready, b + 1)
                pos_, keep, val = rt[:, 8], rt[:, 9], rt[:, 10]
                step(nc.gpsimd.tensor_tensor(pos_, counts[:, 0:2, :], base[:].unsqueeze(1).to_broadcast([T0, 2, E]), ALU.add))
                step(nc.gpsimd.tensor_tensor(base[:], base[:], counts[:, 2, :], ALU.add), carry=True)
                step(nc.gpsimd.tensor_scalar(keep, pos_, float(CAP), None, ALU.is_lt))
                step(nc.gpsimd.tensor_tensor(val, pos_, slot_base[:], ALU.add))
                for k in range(TOP_K):
                    dump = dump_row[:, :, k:k + 1].to_broadcast([T0, 2, E])
                    a = rt[:, 11]
                    step(nc.gpsimd.tensor_tensor(a, val, dump, ALU.subtract))
                    step(nc.gpsimd.tensor_tensor(a, a, keep, ALU.mult))
                    step(nc.gpsimd.tensor_tensor(a, a, dump, ALU.add))
                    last = nc.gpsimd.tensor_tensor(slot_of[:, :, k, :], a, rt[:, 4 + k], ALU.mult)
                    if k == 0:
                        step(last)
                last.then_inc(slots_ranked, 1)

            def scatter(b):
                wait(slots_ready, b + 1)
                for t in range(2):
                    m = T1 if t else T0
                    for k in range(TOP_K):
                        pool.indirect_dma_start(
                            out=slot_rows, out_offset=bass.IndirectOffsetOnAxis(ap=slot_i[0:m, t, k:k + 1], axis=0),
                            in_=z_row[0:m, t, :], in_offset=None).then_inc(rows_scattered, 16)

            def residual(b):
                pool.wait_ge(res_loaded, b * 48 + 48)
                nc.gpsimd.tensor_tensor(h_res[:], h_res[:], proj_bias[:].unsqueeze(1).to_broadcast([T0, 2, D]),
                                        ALU.add).then_inc(res_biased, 1)

            def normed(g, i):
                wait(inv_ready, i * HEADS + (g + 1))
                for t in range(2):
                    p = probs[:, g % 3, t, 0:S]
                    last = nc.gpsimd.tensor_scalar(p, p, row_inv[:, g, t:t + 1], float(D) ** -0.5, ALU.mult, ALU.mult)
                last.then_inc(probs_ready, 1)

            def turn(i, part, start):
                step.turn(start)
                split_v(i)
                if part != "last":
                    ln1(i + 1)
                residual(i)
                for s in range(HEADS):
                    normed(s, i)
                    if part != "first" and s == 5:
                        rank(i - 1, False)
                if part != "first":
                    scatter(i - 1)
                wait(ln2_stats, i + 1)
                rs_steps(1, i).then_inc(ln2_rs, 1)
                return step.n

            pads = [q_h[:, :, ROWS:], q_l[:, ROWS:], q_l1[:, ROWS:], k_h[:, ROWS:], k_l[:, ROWS:], k_hl[:, ROWS:],
                    v_l[:], probs[:], xt_h[:], xt_l[:], xt_l1[0:64, :], h_in[:], h_res[:], base[:], z_row[:]]
            for p in pads:
                step(nc.gpsimd.memset(p.bitcast(F32) if p.dtype == F32R else p, 0.0))
            step(nc.gpsimd.memset(xt_l1[64:128, :].bitcast(F32), 1.0))
            nc.gpsimd.iota(z_row[:, :, D:D + 1], pattern=[[T0, 2], [0, 1]], base=-S, channel_multiplier=1,
                           allow_small_or_imprecise_dtypes=True).then_inc(pads_ready, 1)
            wait(pads_ready, 1)
            at = step.n
            step.turn(at)
            ln1(0)
            at += step.n
            n0 = turn(0, "first", at)
            n_mid = n0 + 11
            with pool.Fori(1, LAST) as i:
                assert turn(i, "mid", (i - 1) * n_mid + (at + n0)) == n_mid, step.n - n0
            at = at + n0 + (LAST - 1) * n_mid
            at += turn(LAST, "last", at)
            step.turn(at)
            rank(LAST, False)
            scatter(LAST)
            at += step.n
            wait(rows_scattered, 64 * B)
            pool.engine_nop().then_inc(stage2_done, 1)
            wait(stage2_done, 4)

            def scale_chunk(e, c, first):
                b = c % 2
                wait(z_square, e * CHUNKS + (c + 1))
                ss, v, y, t, u = (zr[:, b, k, :] for k in range(5))
                step(nc.gpsimd.tensor_scalar(v, ss, 4.0 / D, RMS_EPS, ALU.mult, ALU.add))
                step(nc.gpsimd.tensor_tensor(y, v, minus_half[0:TM, 0:TILES], ALU.pow))
                step(nc.gpsimd.tensor_tensor(t, y, y, ALU.mult))
                step(nc.gpsimd.tensor_tensor(t, t, v, ALU.mult), carry=True)
                step(nc.gpsimd.tensor_scalar(u, t, -1.0, 3.0, ALU.mult, ALU.add))
                nc.gpsimd.tensor_tensor(y, y, u, ALU.mult).then_inc(z_scale, 1)
                if not first:
                    wait(y_added[b], e * ADDED)
                nc.gpsimd.tensor_copy(token_i[:, c, :], zs_in[:, b, :, D])
                step(nc.gpsimd.tensor_copy(weight[:, c, :], zs_in[:, b, :, bass.ds(e + (D + 1), 1)].rearrange("p t o -> p (t o)")), carry=True)
                for t in range(TILES):
                    last = nc.gpsimd.tensor_scalar(zw[:, c, t, :], zs_in[:, b, t, 0:D], weight[:, c, t:t + 1], None, ALU.mult)
                last.then_inc(z_weighted, 1)

            def act_lows(e, c, h):
                pool.wait_ge(act_high, e * CHUNKS * HT + (c * HT + h + 1))
                nc.gpsimd.tensor_tensor(act_l[:, c % 2, h, :], act[:, c % 2, h, :], act_h[:, c % 2, h, :].bitcast(F32),
                                        ALU.subtract).then_inc(act_low, 1)

            def add_rows(e, c, first):
                if c == 0 and not first:
                    for added in y_added:
                        wait(added, e * ADDED)
                wait(y_ready, e * CHUNKS + (c + 1))
                for t in range(TILES):
                    pool.indirect_dma_start(
                        out=out, out_offset=bass.IndirectOffsetOnAxis(ap=token_i[:, c, t:t + 1], axis=0),
                        in_=y_out[:, c % 2, t, :], in_offset=None, compute_op=ALU.add).then_inc(y_added[c % 2], 16)

            def expert(e, first, start):
                step.turn(start)
                scale_chunk(e, 0, first)
                for c in range(CHUNKS):
                    if c + 1 < CHUNKS:
                        scale_chunk(e, c + 1, first)
                    for h in range(HT):
                        act_lows(e, c, h)
                    if c:
                        add_rows(e, c - 1, first)
                add_rows(e, CHUNKS - 1, first)
                return step.n

            n = expert(0, True, at)
            with pool.Fori(1, E) as e:
                expert(e, False, (e - 1) * n + (at + n))

        @block.scalar
        def _(a):
            wait = carried(a, 1, lambda to: nc.scalar.copy(to, tick[0:1, 0:1]))
            for n in range(3):
                a.wait_ge(w_loaded, 16 * (12, 24, 27)[n])
                cols = slice(n * W, (n + 1) * W)
                nc.scalar.copy(wq_h[:, cols], w_raw[:, 0, :]).then_inc(w_high, 1)
                nc.scalar.copy(wq_hl[:, cols], w_raw[:, 1, :]).then_inc(w_high, 1)
            a.wait_ge(w_loaded, 16 * 30)
            as_heads = w_raw[:].rearrange("p a (h n) -> p a h n", h=HEADS)
            nc.scalar.copy(wp_h[:], as_heads[:, 0]).then_inc(w_high, 1)
            nc.scalar.copy(wp_hl[:], as_heads[:, 1]).then_inc(w_high, 1)
            for k in range(KT):
                a.wait_ge(pt_full, k + 1)
                nc.scalar.copy(tok_h[:, k, :], bank[k % 2][:, 0:D]).then_inc(pt_high, 1)
            for g in range(RT * GRID):
                for half in range(2):
                    n = 2 * g + half
                    a.wait_ge(pt_full, KT + n + 1)
                    src = bank[2 + n % 2][:, 0:3 * IR].rearrange("p (k r) -> p k r", k=3)
                    nc.scalar.copy(pt_h[:, 3 * half:3 * half + 3, :], src).then_inc(pt_high, 1)
            a.wait_ge(emb_stored, 16 * (B + 1))
            a.wait_ge(bias_high, 3)
            nc.scalar.copy(minus_half[0:1, 3:4], minus_half[0:1, 3:4]).then_inc(stage1_done, 1)
            a.wait_ge(stage1_done, 4)

            def use(part, i, name):
                a.wait_ge(ring_full, position(part, i, name))
                return ring_bank(part, name)

            def tokens_of(t_, rows, j, sub=None):
                return t_

            def qk_high(i, part, kind, n):
                src = use(part, i, (kind, n))
                src = src[:, 0:3 * SP].rearrange("p (k s) -> p k s", k=3)
                main, pair = (q_h[:, 0, :], q_h[:, 1, :]) if kind == "q" else (k_h, k_hl)
                m = main[:, 0:ROWS].rearrange("p (s j) -> p j s", j=HEADS)
                r = pair[:, 0:ROWS].rearrange("p (s j) -> p j s", j=HEADS)
                nc.scalar.copy(m[:, 2 * n:2 * n + 2, :], src[:, 0:2, 0:S])
                nc.scalar.copy(r[0:64, 2 * n, :], src[0:64, 2, 0:S])
                nc.scalar.copy(r[0:64, 2 * n + 1, :], src[64:128, 2, 0:S]).then_inc(ring_act, 1)

            def xt_high(i, part, b):
                src = use(part, i, ("xt", 0))[:, 0:2 * S].rearrange("p (k s) -> p k s", k=2)
                nc.scalar.copy(xt_h[:, :, 0:S], src).then_inc(ring_act, 1)

            def v_evac(i, part, b, n):
                src = use(part, i, ("v", n))
                m = T1 if n // 4 else T0
                if not (part == "before" and n < 4):
                    a.wait_ge(v_stored[n % 4], b * 32 + 16 * (n // 4))
                nc.scalar.copy(v_out[0:m, n % 4, :], src[0:m, 0:2 * D]).then_inc(ring_act, 1)

            def zt_evac(part, i, b):
                src = use(part, i, ("zt", 0))[:, 0:2 * S].rearrange("p (k s) -> p k s", k=2)
                nc.scalar.copy(z_t[:, 0, :], src[:, 0])
                nc.scalar.copy(z_t[0:D1, 1, :], src[0:D1, 1]).then_inc(ring_act, 1)

            def route_exps(b):
                a.wait_ge(route_sub, b + 1)
                nc.scalar.activation(rt[:, 1], rt[:, 0], ACT.Exp).then_inc(route_exp, 1)

            def exps(i, g):
                a.wait_ge(max_ready, i * HEADS + (g + 1))
                src = score_bank[g % 2][0:T0, 0:2 * SP].rearrange("p (t s) -> p t s", t=2)
                for t in range(2):
                    last = nc.scalar.activation(probs[:, g % 3, t, 0:S], src[:, t, 0:S], ACT.Exp,
                                                bias=neg_max[:, g, t:t + 1], accum_out=row_sum[:, g, t:t + 1])
                last.then_inc(exp_done, 1)

            def probs_t_h(i, g):
                a.wait_ge(probs_t_full, i * HEADS + (g + 1))
                src = probs_t_bank[0:T0, 0:2 * SP].rearrange("p (t s) -> p t s", t=2)
                nc.scalar.copy(pt2_h[:, g % 2], src).then_inc(probs_t_high, 1)

            def o_high(i, part, g):
                src = use(part, i, ("pv", g))
                cols = slice(S * g, S * (g + 1))
                nc.scalar.copy(o_h[:, 0, cols], src[:, 0:S])
                nc.scalar.copy(o_h[0:64, 1, cols], src[0:64, SP:SP + S]).then_inc(ring_act, 1)

            def turn(i, part):
                for kind in "qk":
                    for n in range(4):
                        qk_high(i, part, kind, n)
                if part != "first":
                    zt_evac(part, i, i - 1)
                if part != "last":
                    xt_high(i, part, i + 1)
                    for n in range(0, 8, 2):
                        v_evac(i, part, i + 1, n)
                for s in range(HEADS + 3):
                    if s < HEADS:
                        exps(i, s)
                    if 0 <= s - 2 < HEADS:
                        probs_t_h(i, s - 2)
                    if 0 <= s - 3:
                        o_high(i, part, s - 3)
                    if part != "first" and s == 2:
                        route_exps(i - 1)

            a.wait_ge(pads_ready, 1)
            xt_high(0, "before", 0)
            for n in range(0, 8, 2):
                v_evac(0, "before", 0, n)
            turn(0, "first")
            with a.Fori(1, LAST) as i:
                turn(i, "mid")
            turn(LAST, "last")
            zt_evac("after", 0, LAST)
            route_exps(LAST)
            a.wait_ge(rows_scattered, 64 * B)
            nc.scalar.copy(minus_half[0:1, 3:4], minus_half[0:1, 3:4]).then_inc(stage2_done, 1)
            a.wait_ge(stage2_done, 4)

            def expert(e, first):
                for r in range(2 * HT):
                    a.wait_ge(ew_full, e * (3 * HT) + (r + 1))
                    nc.scalar.copy(up_h[:, r, :], bank[r % 4][:, 0:128])
                    nc.scalar.copy(up_hl[:, r, :], bank[r % 4][:, 128:256]).then_inc(ew_high, 1)
                for h in range(HT):
                    a.wait_ge(ew_full, e * (3 * HT) + (2 * HT + h + 1))
                    nc.scalar.copy(down_h[:, h, :], bank[h][:, 0:D]).then_inc(ew_high, 1)
                zt_h(e, 0)
                for c in range(CHUNKS):
                    if c + 1 < CHUNKS:
                        zt_h(e, c + 1)
                    for h in range(HT):
                        n = c * 2 * HT + 2 * h
                        a.wait_ge(gu_full, e * (2 * HT * CHUNKS) + (n + 1))
                        nc.scalar.activation(silu[:, h, :], bank[n % 4][:, 0:CN], ACT.Silu).then_inc(silu_ready, 1)
                        a.wait_ge(act_ready, e * (HT * CHUNKS) + (c * HT + h + 1))
                        nc.scalar.copy(act_h[:, c % 2, h, :], act[:, c % 2, h, :]).then_inc(act_high, 1)

            def zt_h(e, c):
                wait(zt_full, e * CHUNKS + (c + 1))
                for k in range(2):
                    last = nc.scalar.activation(zst_h[:, c % 2, k, :], bank[4 + k][:, 0:CN], ACT.Copy,
                                                scale=norm_cols[:, k, bass.ds(e, 1)])
                last.then_inc(zt_high, 1)

            expert(0, True)
            with a.Fori(1, E) as e:
                expert(e, False)

        @block.vector
        def _(v):
            wait = carried(v, 2, lambda to: nc.vector.tensor_copy(to, tick[0:1, 0:1]))
            step = step_counter(v, dve_step)
            alone = [step_counter(v, signal, wait) for signal in stats_step]
            for n in range(3):
                v.wait_ge(w_high, 2 * (n + 1))
                cols = slice(n * W, (n + 1) * W)
                nc.vector.tensor_copy(wq_hb[0:D1, cols], wq_hl[0:D1, cols].bitcast(F32))
                nc.vector.memset(wq_hb[64:128, cols].bitcast(F32), 0.0)
                nc.vector.tensor_tensor(wq_l[:, cols], w_raw[:, 0, :], wq_h[:, cols].bitcast(F32), ALU.subtract)
                step(nc.vector.tensor_tensor(wq_hl[64:128, cols], w_raw[64:128, 1, :],
                                             wq_hl[64:128, cols].bitcast(F32), ALU.subtract))
                nc.vector.memset(tok_l[:, 0, 0:1].bitcast(F32), 0.0).then_inc(w_low, 1)
            v.wait_ge(w_high, 8)
            as_heads = w_raw[:].rearrange("p a (h n) -> p a h n", h=HEADS)
            nc.vector.tensor_tensor(wp_l[:], as_heads[:, 0], wp_h[:].bitcast(F32), ALU.subtract)
            step(nc.vector.tensor_tensor(wp_hl[64:128], as_heads[64:128, 1], wp_hl[64:128].bitcast(F32), ALU.subtract))
            nc.vector.memset(tok_l[:, 0, 0:1].bitcast(F32), 0.0).then_inc(w_low, 1)
            for n in range(3):
                v.wait_ge(bias_loaded, 16 * (16 if n < 2 else 18))
                cols = slice(n * W, (n + 1) * W)
                src = w_raw[:, n % 2, :]
                nc.vector.tensor_copy(wq_hb[64:65, cols], src[64:65, :])
                step(nc.vector.tensor_copy(wq_hb[96:97, cols], src[96:97, :]))
                nc.vector.tensor_tensor(wq_hb[96:97, cols], src[96:97, :], wq_hb[96:97, cols].bitcast(F32),
                                        ALU.subtract).then_inc(bias_high, 1)
            v.wait_ge(bias_high, 3)
            v.wait_ge(image_args_loaded, 16 * (5 + SEQS))
            pos_g = pos[:].rearrange("p (w d) -> p w d", w=GRID)
            nc.vector.tensor_tensor(pos_g, pos_g, tok_bias[:].unsqueeze(1).to_broadcast([IR, GRID, D]), ALU.add).then_inc(token_bias, 1)
            nc.vector.tensor_tensor(cls[:], cls[:], cls_pos[:], ALU.add).then_inc(token_bias, 1)
            for k in range(KT):
                v.wait_ge(pt_high, k + 1)
                nc.vector.tensor_tensor(tok_l[:, k, :], bank[k % 2][:, 0:D], tok_h[:, k, :].bitcast(F32), ALU.subtract).then_inc(pt_low, 1)
            v.wait_ge(token_bias, 2)
            for g in range(RT * GRID):
                r, gw = g // GRID, g % GRID
                for half in range(2):
                    n = 2 * g + half
                    v.wait_ge(pt_high, KT + n + 1)
                    src = bank[2 + n % 2][:, 0:3 * IR].rearrange("p (k r) -> p k r", k=3)
                    ks = slice(3 * half, 3 * half + 3)
                    nc.vector.tensor_tensor(pt_l[:, ks, :], src, pt_h[:, ks, :].bitcast(F32), ALU.subtract).then_inc(pt_low, 1)
                if gw == 0 and r:
                    v.wait_ge(emb_stored, 16 * SEQS * r)
                v.wait_ge(emb_full, g + 1)
                nc.vector.tensor_tensor(emb[:, gw, :], bank[4][0:IR, 0:D], pos_g[:, gw, :], ALU.add).then_inc(emb_free, 1)
            v.wait_ge(emb_stored, 16 * (B + 1))
            nc.vector.memset(minus_half[0:1, 2:3], -0.5).then_inc(stage1_done, 1)
            v.wait_ge(stage1_done, 4)

            def use(part, i, name):
                e = uses.who(name)
                if "a" in e:
                    v.wait_ge(ring_act, position(part, i, name, "a"))
                else:
                    v.wait_ge(ring_full, position(part, i, name))
                return ring_bank(part, name)

            def qk_low(i, part, kind, n):
                src = use(part, i, (kind, n))
                src = src[:, 0:3 * SP].rearrange("p (k s) -> p k s", k=3)
                hm, lm, pair = (q_h[:, 0, :], q_l, q_h[:, 1, :]) if kind == "q" else (k_h, k_l, k_hl)
                by_chunk = lambda t: t[:, 0:ROWS].rearrange("p (s j) -> p j s", j=HEADS)
                js = slice(2 * n, 2 * n + 2)
                nc.vector.tensor_tensor(by_chunk(lm)[:, js, :], src[:, 0:2, 0:S], by_chunk(hm)[:, js, :].bitcast(F32), ALU.subtract)
                r = by_chunk(pair)
                for k in range(2):
                    j = 2 * n + k
                    dst = by_chunk(q_l1)[:, j, :] if kind == "q" else r[64:128, j, :]
                    last = nc.vector.tensor_tensor(dst, src[64 * k:64 * k + 64, 2, 0:S], r[0:64, j, :].bitcast(F32), ALU.subtract)
                last.then_inc(ring_dve, 1)

            def stat(which, src, b, signal):
                alone[which].turn(b)
                for t in range(2):
                    ins = nc.vector.bn_stats(stats[:, which, t, :], src[:, t, :])
                    if t:
                        alone[which](ins, carry=True)
                for t in range(2):
                    last = nc.vector.bn_aggr(mean_var[:, which, t, :], stats[:, which, t, :])
                last.then_inc(signal, 1)

            def apply(dst, src, which, t):
                return nc.vector.tensor_scalar(dst, src, mean_var[:, which, t, 0:1], rs[:, which, 1, t:t + 1],
                                               ALU.subtract, ALU.mult)

            def ln1_stat(b):
                v.wait_ge(h_loaded, b * 48 + 48)
                stat(0, h_in, b, ln1_stats)

            def ln1_apply(b):
                v.wait_ge(ln1_rs, b + 1)
                for t in range(2):
                    apply(x_norm[:, t, 0:D], h_in[:, t, :], 0, t)
                    last = apply(x_norm[:, t, D:], h_in[:, t, 128:D], 0, t)
                last.then_inc(x_ready, 1)

            def xt_low(i, part):
                src = use(part, i, ("xt", 0))[:, 0:2 * S].rearrange("p (k s) -> p k s", k=2)
                nc.vector.tensor_tensor(xt_l[:, 0:S], src[:, 0], xt_h[:, 0, 0:S].bitcast(F32), ALU.subtract)
                nc.vector.tensor_tensor(xt_l1[0:64, 0:S], src[0:64, 1], xt_h[0:64, 1, 0:S].bitcast(F32),
                                        ALU.subtract).then_inc(ring_dve, 1)

            def v_evac(i, part, b, n):
                src = use(part, i, ("v", n))
                m = T1 if n // 4 else T0
                if not (part == "before" and n < 4):
                    v.wait_ge(v_stored[n % 4], b * 32 + 16 * (n // 4))
                nc.vector.tensor_copy(v_out[0:m, n % 4, :], src[0:m, 0:2 * D]).then_inc(ring_dve, 1)

            def bc(t):
                return t.to_broadcast([T0, 2, E])

            def route_logits(part, i, b):
                src = use(part, i, ("log", 0))[0:T0, 0:2 * E].rearrange("p (t e) -> p t e", t=2)
                nc.vector.tensor_copy(logits[0:T0, 0, :], src[0:T0, 0, :])
                step(nc.vector.tensor_copy(logits[0:T1, 1, :], src[0:T1, 1, :]))
                nc.vector.tensor_copy(rt[:, 7], logits[:]).then_inc(ring_dve, 1)
                step(nc.vector.tensor_reduce(r1[:, 0], logits[:], AXIS.X, ALU.max))
                nc.vector.tensor_tensor(rt[:, 0], logits[:], bc(r1[:, 0]), ALU.subtract).then_inc(route_sub, 1)

            def route_choose(b):
                v.wait_ge(route_exp, b + 1)
                p, m, w = rt[:, 2], rt[:, 3], r1
                step(nc.vector.tensor_reduce(w[:, 1], rt[:, 1], AXIS.X, ALU.add))
                step(nc.vector.reciprocal(w[:, 2], w[:, 1]))
                step(nc.vector.tensor_tensor(p, rt[:, 1], bc(w[:, 2]), ALU.mult))
                rest = p
                for k in range(TOP_K):
                    eq, pick = rt[:, 6], rt[:, 4 + k]
                    step(nc.vector.tensor_reduce(w[:, 3 + k], rest, AXIS.X, ALU.max))
                    step(nc.vector.tensor_tensor(eq, rest, bc(w[:, 3 + k]), ALU.is_equal))
                    step(nc.vector.scalar_tensor_tensor(eq, eq, -float(E), expert_no[:], ALU.mult, ALU.add))
                    step(nc.vector.tensor_reduce(w[:, 5], eq, AXIS.X, ALU.min))
                    step(nc.vector.tensor_scalar(w[:, 5], w[:, 5], float(E), None, ALU.add))
                    step(nc.vector.tensor_tensor(pick, expert_no[:], bc(w[:, 5]), ALU.is_equal))
                    if k == 0:
                        step(nc.vector.scalar_tensor_tensor(m, pick, -2.0, p, ALU.mult, ALU.add))
                        rest = m
                for k in range(TOP_K):
                    ins = nc.vector.tensor_tensor(rt[:, 4 + k], rt[:, 4 + k], bc(real[:]), ALU.mult)
                step(ins)
                nc.vector.tensor_tensor(w[:, 6], w[:, 3], w[:, 4], ALU.add)
                step(nc.vector.tensor_tensor(rt[:, 7], rt[:, 4], rt[:, 5], ALU.add))
                nc.vector.tensor_tensor(rt[:, 6], rt[:, 7], p, ALU.mult)
                step(nc.vector.reciprocal(w[:, 7], w[:, 6]))
                nc.vector.tensor_tensor(z_row[:, :, D + 1:], rt[:, 6], bc(w[:, 7]), ALU.mult)
                nc.vector.tensor_scalar(z_row[:, :, D:D + 1], z_row[:, :, D:D + 1], float(S), None, ALU.add).then_inc(chosen, 1)

            def route_counts(part, i, b):
                src = use(part, i, ("cnt", 0))[0:T0, 0:3 * E].rearrange("p (t e) -> p t e", t=3)
                nc.vector.tensor_copy(counts[:], src).then_inc(ring_dve, 1)
                v.wait_ge(ring_dve, position(part, i, ("cnt", 0), "d"))
                nc.vector.memset(r1[:, 5], 0.0).then_inc(counts_ready, 1)

            def route_slots(b):
                v.wait_ge(slots_ranked, b + 1)
                step(nc.vector.tensor_reduce(slot_f[:].rearrange("p t k o -> p (t k) o"), slot_of[:].rearrange("p t k e -> p (t k) e"),
                                             AXIS.X, ALU.add))
                nc.vector.tensor_copy(slot_i[:], slot_f[:].rearrange("p t k o -> p t (k o)")).then_inc(slots_ready, 1)

            def maxes(i, g):
                v.wait_ge(scores_full, i * HEADS + (g + 1))
                src = score_bank[g % 2][0:T0, 0:2 * SP].rearrange("p (t s) -> p t s", t=2)
                nc.vector.tensor_reduce(neg_max[:, g, :].unsqueeze(2), src[:, :, 0:S], AXIS.X, ALU.max, negate=True).then_inc(max_ready, 1)

            def invs(i, g):
                v.wait_ge(exp_done, i * HEADS + (g + 1))
                nc.vector.reciprocal(row_inv[:, g, :], row_sum[:, g, :]).then_inc(inv_ready, 1)

            def probs_t_l(i, g):
                v.wait_ge(probs_t_high, i * HEADS + (g + 1))
                src = probs_t_bank[0:T0, 0:2 * SP].rearrange("p (t s) -> p t s", t=2)
                nc.vector.tensor_tensor(pt2_l[:, g % 2], src, pt2_h[:, g % 2].bitcast(F32), ALU.subtract).then_inc(probs_t_low, 1)

            def o_low(i, part, g):
                src = use(part, i, ("pv", g))
                cols = slice(S * g, S * (g + 1))
                nc.vector.tensor_tensor(o_l[:, cols], src[:, 0:S], o_h[:, 0, cols].bitcast(F32), ALU.subtract)
                nc.vector.tensor_tensor(o_l1[:, cols], src[0:64, SP:SP + S], o_h[0:64, 1, cols].bitcast(F32), ALU.subtract)
                nc.vector.tensor_copy(o_h[64:128, 1, cols], src[0:64, SP:SP + S]).then_inc(ring_dve, 1)

            def y_evac(i, part):
                v.wait_ge(res_biased, i + 1)
                if part != "first":
                    v.wait_ge(h_mid_stored, i * 32)
                for t in range(2):
                    src = use(part, i, ("y", t))
                    m = T1 if t else T0
                    nc.vector.tensor_tensor(h_mid[0:m, t, :], src[0:m, 0:D], h_res[0:m, t, :], ALU.add).then_inc(ring_dve, 1)
                v.wait_ge(ring_dve, position(part, i, ("y", 1), "d"))
                nc.vector.memset(r1[:, 5], 0.0).then_inc(h_mid_ready, 1)

            def ln2(i, part):
                stat(1, h_mid, i, ln2_stats)
                v.wait_ge(ln2_rs, i + 1)
                if part != "first":
                    v.wait_ge(rows_scattered, i * 64)
                for t in range(2):
                    last = apply(z_row[:, t, 0:D], h_mid[:, t, :], 1, t)
                last.then_inc(z_ready, 1)

            def turn(i, part, start):
                step.turn(start)
                for n in range(4):
                    qk_low(i, part, "q", n)
                if part != "last":
                    ln1_stat(i + 1)
                for n in range(2):
                    qk_low(i, part, "k", n)
                if part != "last":
                    ln1_apply(i + 1)
                for n in range(2, 4):
                    qk_low(i, part, "k", n)
                if part != "last":
                    xt_low(i, part)
                if part != "first":
                    route_logits(part, i, i - 1)
                if part != "last":
                    for n in range(1, 8, 2):
                        v_evac(i, part, i + 1, n)
                for s in range(HEADS + 3):
                    if s < HEADS:
                        maxes(i, s)
                        invs(i, s)
                    if 0 <= s - 2 < HEADS:
                        probs_t_l(i, s - 2)
                    if 0 <= s - 3:
                        o_low(i, part, s - 3)
                    if part != "first":
                        if s == 3:
                            route_choose(i - 1)
                        if s == 4:
                            route_counts(part, i, i - 1)
                        if s == 7:
                            route_slots(i - 1)
                y_evac(i, part)
                ln2(i, part)
                return step.n

            v.wait_ge(pads_ready, 1)
            nc.vector.memset(logits[:], 0.0)
            step(nc.vector.memset(h_mid[:], 0.0))
            at = step.n
            step.turn(at)
            ln1_stat(0)
            at += step.n
            ln1_apply(0)
            xt_low(0, "before")
            for n in range(1, 8, 2):
                v_evac(0, "before", 0, n)
            n0 = turn(0, "first", at)
            n_mid = n0 + 22
            with v.Fori(1, LAST) as i:
                got = turn(i, "mid", (i - 1) * n_mid + (at + n0))
                assert got == n_mid, got - n0
            at = at + n0 + (LAST - 1) * n_mid
            at += turn(LAST, "last", at)
            step.turn(at)
            route_logits("after", 0, LAST)
            route_choose(LAST)
            route_counts("after", 0, LAST)
            route_slots(LAST)
            at += step.n
            v.wait_ge(rows_scattered, 64 * B)
            nc.vector.memset(minus_half[0:1, 2:3], -0.5).then_inc(stage2_done, 1)
            v.wait_ge(stage2_done, 4)

            def z_chunk(e, c):
                b = c % 2
                v.wait_ge(z_loaded[b], e * (8 * CHUNKS) + 16 * (c // 2 + 1))
                for t in range(TILES):
                    ins = nc.vector.tensor_tensor_reduce(square[:], zs_in[:, b, t, 0:D], zs_in[:, b, t, 0:D], 1.0, 0.0,
                                                         ALU.mult, ALU.add, zr[:, b, 0, t:t + 1])
                    if t < TILES - 1:
                        step(ins)
                ins.then_inc(z_square, 1)
                v.wait_ge(z_scale, e * CHUNKS + (c + 1))
                for t in range(TILES):
                    s_ = zr[:, b, 2, t:t + 1]
                    nc.vector.tensor_scalar(zs[:, b, t, 0:D], zs_in[:, b, t, 0:D], s_, None, ALU.mult)
                    last = nc.vector.tensor_scalar(zs[:, b, t, D:], zs_in[:, b, t, 128:D], s_, None, ALU.mult)
                last.then_inc(z_scaled, 1)

            def zt_l(e, c):
                v.wait_ge(zt_high, e * CHUNKS + (c + 1))
                for k in range(2):
                    last = nc.vector.scalar_tensor_tensor(zst_l[:, c % 2, k, :], bank[4 + k][:, 0:CN],
                                                          norm_cols[:, k, bass.ds(e, 1)], zst_h[:, c % 2, k, :].bitcast(F32),
                                                          ALU.mult, ALU.subtract)
                last.then_inc(zt_low, 1)

            def y_evac3(e, c, first):
                v.wait_ge(z_weighted, e * CHUNKS + (c + 1))
                if not (first and c < 2):
                    v.wait_ge(y_added[c % 2], e * ADDED + 16 * TILES * (c // 2))
                for u in range(2):
                    v.wait_ge(y_full, e * (2 * CHUNKS) + (2 * c + u + 1))
                    for t in (2 * u, 2 * u + 1):
                        last = nc.vector.scalar_tensor_tensor(y_out[:, c % 2, t, :], bank[6 + u][0:TM, (t % 2) * D:(t % 2) * D + D],
                                                              weight[:, c, t:t + 1], zw[:, c, t, :], ALU.mult, ALU.add)
                last.then_inc(y_ready, 1)

            def expert(e, first, start):
                step.turn(start)
                z_chunk(e, 0)
                for r in range(2 * HT):
                    v.wait_ge(ew_high, e * (3 * HT) + (r + 1))
                    nc.vector.tensor_tensor(up_l[:, r, :], bank[r % 4][:, 0:128], up_h[:, r, :].bitcast(F32), ALU.subtract)
                    nc.vector.tensor_tensor(up_hl[64:128, r, :], bank[r % 4][64:128, 128:256], up_hl[64:128, r, :].bitcast(F32),
                                            ALU.subtract).then_inc(ew_low, 1)
                for h in range(HT):
                    v.wait_ge(ew_high, e * (3 * HT) + (2 * HT + h + 1))
                    nc.vector.tensor_tensor(down_l[:, h, :], bank[h][:, 0:D], down_h[:, h, :].bitcast(F32), ALU.subtract).then_inc(ew_low, 1)
                zt_l(e, 0)
                for c in range(CHUNKS):
                    if c + 1 < CHUNKS:
                        z_chunk(e, c + 1)
                        zt_l(e, c + 1)
                    for h in range(HT):
                        n = c * 2 * HT + 2 * h + 1
                        v.wait_ge(gu_full, e * (2 * HT * CHUNKS) + (n + 1))
                        v.wait_ge(silu_ready, e * (HT * CHUNKS) + (c * HT + h + 1))
                        nc.vector.tensor_tensor(act[:, c % 2, h, :], silu[:, h, :], bank[n % 4][:, 0:CN], ALU.mult).then_inc(act_ready, 1)
                    if c:
                        y_evac3(e, c - 1, first)
                y_evac3(e, CHUNKS - 1, first)
                return step.n

            n = expert(0, True, at)
            with v.Fori(1, E) as e:
                expert(e, False, (e - 1) * n + (at + n))

        @block.tensor
        def _(pe):
            def passes(dst, pairs):
                for n, (lhs, rhs) in enumerate(pairs):
                    last = nc.tensor.matmul(dst, lhs, rhs, start=(n == 0), stop=(n == len(pairs) - 1))
                return last

            pe.wait_ge(const_ready, 9)
            pe.wait_ge(image_args_loaded, 16 * (5 + SEQS))
            for k in range(KT):
                if k >= 2:
                    pe.wait_ge(pt_low, k - 1)
                nc.tensor.transpose(bank[k % 2][:, 0:128], tok_raw[:, 0, 128 * k:128 * k + 128], ident[:])
                nc.tensor.transpose(bank[k % 2][:, 128:D], tok_raw[0:D1, 1, 128 * k:128 * k + 128], ident[0:D1, 0:D1]).then_inc(pt_full, 1)
            for g in range(RT * GRID):
                r, gw = g // GRID, g % GRID
                if gw == 0:
                    pe.wait_ge(regrouped, r + 1)
                for half in range(2):
                    n = 2 * g + half
                    if n >= 2:
                        pe.wait_ge(pt_low, KT + n - 1)
                    for k in range(3):
                        kk = 3 * half + k
                        last = nc.tensor.transpose(bank[2 + n % 2][:, k * IR:(k + 1) * IR],
                                                   img_grouped[:, gw, 128 * kk:128 * kk + 128], ident[0:IR, 0:IR])
                    last.then_inc(pt_full, 1)
                if g:
                    pe.wait_ge(emb_free, g)
                pe.wait_ge(pt_low, KT + 2 * g + 2)
                pairs = []
                for k in range(KT):
                    pairs += [(pt_h[:, k, :], tok_h[:, k, :]), (pt_h[:, k, :], tok_l[:, k, :]), (pt_l[:, k, :], tok_h[:, k, :])]
                passes(bank[4][0:IR, 0:D], pairs).then_inc(emb_full, 1)
            pe.wait_ge(emb_stored, 16 * (B + 1))
            nc.tensor.transpose(bank[0][0:1, 0:1], ident[0:1, 0:1], ident[0:1, 0:1]).then_inc(stage1_done, 1)
            pe.wait_ge(stage1_done, 4)
            pe.wait_ge(const_loaded, 16 * 6)

            def use(part, i, name):
                order = {"before": [("before", n) for n in uses.lists["before"]]}
                here = uses.lists[part].index(name)
                back = here - GB
                if back >= 0:
                    old_part, old = part, uses.lists[part][back]
                    old_turn = i
                elif part == "before":
                    return ring_bank(part, name)
                else:
                    old_part = {"first": "before", "mid": "mid", "last": "mid", "after": "last"}[part]
                    old = uses.lists[old_part][back]
                    old_turn = {"before": 0, "mid": i - 1 if part != "last" else LAST - 1, "last": LAST}[old_part]
                e = "d" if "d" in uses.who(old) else "a"
                c = uses.count(e)
                seq = [n for n in uses.lists[old_part] if e in uses.who(n)]
                if part == "mid" and back < 0:
                    value = c.start(i) - (len(seq) - seq.index(old) - 1)
                elif old_part == "before":
                    value = seq.index(old) + 1
                else:
                    value = position(old_part, old_turn, old, e)
                pe.wait_ge(ring_dve if e == "d" else ring_act, value)
                return ring_bank(part, name)

            def x_side(t=None):
                cols = slice(0, SP) if t is None else slice(t * T0, t * T0 + (T1 if t else T0))
                return xt_h[:, 0, cols], xt_l[:, cols], xt_h[:, 1, cols], xt_l1[:, cols]

            def w_side(cols):
                return wq_h[:, cols], wq_l[:, cols], wq_hl[:, cols], wq_hb[:, cols]

            def products(x_, w_):
                (xh, xl, xhh, xl1), (wh, wl, whl, whb) = x_, w_
                return [(xh, wh), (xh, wl), (xl, wh), (xhh, whl), (xl1, whb)]

            def turned(pairs):
                return [(b_, a_) for a_, b_ in pairs]

            def qk(i, part, kind, n):
                dst = use(part, i, (kind, n))
                first = (0 if kind == "q" else W) + 2 * n * D
                for k in range(3):
                    cols = slice(first + 128 * k, first + 128 * k + 128)
                    last = passes(dst[:, k * SP:(k + 1) * SP], turned(products(x_side(), w_side(cols))))
                last.then_inc(ring_full, 1)

            def xt(i, part, b):
                dst = use(part, i, ("xt", 0))
                pe.wait_ge(x_ready, b + 1)
                for t in range(2):
                    m = T1 if t else T0
                    for k in range(2):
                        last = nc.tensor.transpose(dst[:, k * S + t * T0:k * S + t * T0 + m],
                                                   x_norm[0:m, t, 128 * k:128 * k + 128], ident[0:m, 0:m])
                last.then_inc(ring_full, 1)

            def v_product(i, part, n):
                dst = use(part, i, ("v", n))
                if n == 0:
                    pe.wait_ge(ring_dve, position(part, i, ("xt", 0), "d"))
                t, c = n // 4, n % 4
                m = T1 if t else T0
                cols = slice(2 * W + c * 2 * D, 2 * W + (c + 1) * 2 * D)
                passes(dst[0:m, 0:2 * D], products(x_side(t), w_side(cols))).then_inc(ring_full, 1)

            def zt(part, i, b):
                dst = use(part, i, ("zt", 0))
                pe.wait_ge(z_ready, b + 1)
                for t in range(2):
                    m = T1 if t else T0
                    nc.tensor.transpose(dst[:, t * T0:t * T0 + m], z_row[0:m, t, 0:128], ident[0:m, 0:m])
                    last = nc.tensor.transpose(dst[0:D1, S + t * T0:S + t * T0 + m], z_row[0:m, t, 128:D], ident[0:m, 0:m])
                last.then_inc(ring_full, 1)

            def gate(part, i, b):
                dst = use(part, i, ("log", 0))
                pe.wait_ge(ring_act, position(part, i, ("zt", 0), "a"))
                for t in range(2):
                    m = T1 if t else T0
                    cols = slice(t * T0, t * T0 + m)
                    last = passes(dst[0:m, t * E:(t + 1) * E], [(z_t[:, 0, cols], gate_t[:, 0, :]), (z_t[0:D1, 1, cols], gate_t[0:D1, 1, :])])
                last.then_inc(ring_full, 1)

            def counting(part, i, b):
                dst = use(part, i, ("cnt", 0))
                pe.wait_ge(chosen, b + 1)
                m0, m1 = rt[:, 7, 0, :], rt[:, 7, 1, :]
                passes(dst[0:T0, 0:E], [(earlier[:], m0)])
                passes(dst[0:T0, E:2 * E], [(ones[:], m0), (earlier[:], m1)])
                passes(dst[0:T0, 2 * E:3 * E], [(ones[:], m0), (ones[:], m1)]).then_inc(ring_full, 1)

            def scores(i, g):
                if g < 2:
                    if not (isinstance(i, int) and i == 0):
                        pe.wait_ge(exp_done, i * HEADS + (g - 1))
                else:
                    pe.wait_ge(exp_done, i * HEADS + (g - 1))
                dst = score_bank[g % 2]
                keys = slice(S * g, S * g + SP)
                for t in range(2):
                    rows = slice(S * g + T0 * t, S * g + T0 * (t + 1))
                    last = passes(dst[0:T0, t * SP:(t + 1) * SP], [
                        (q_h[:, 0, rows], k_h[:, keys]), (q_h[:, 0, rows], k_l[:, keys]), (q_l[:, rows], k_h[:, keys]),
                        (q_h[:, 1, rows], k_hl[:, keys]), (q_l1[:, rows], k_hl[0:64, keys])])
                last.then_inc(scores_full, 1)

            def probs_turn(i, g):
                if not (isinstance(i, int) and i == 0 and g == 0):
                    pe.wait_ge(probs_t_low, i * HEADS + g)
                pe.wait_ge(probs_ready, i * HEADS + (g + 1))
                for kt in range(2):
                    for t in range(2):
                        last = nc.tensor.transpose(probs_t_bank[0:T0, kt * SP + t * T0:kt * SP + (t + 1) * T0],
                                                   probs[:, g % 3, t, kt * T0:(kt + 1) * T0], ident[0:T0, 0:T0])
                last.then_inc(probs_t_full, 1)

            def pv(i, part, g):
                dst = use(part, i, ("pv", g))
                pe.wait_ge(probs_t_low, i * HEADS + (g + 1))
                if g % 4 == 0:
                    pe.wait_ge(v_ready, i * 2 + (g // 4 + 1))
                for d0, d1, col in ((0, 128, 0), (128, D, SP)):
                    pairs = []
                    for kt in range(2):
                        ph, pl = pt2_h[:, g % 2, kt, :], pt2_l[:, g % 2, kt, :]
                        vh, vl = v_h[:, g, kt, d0:d1], v_l[:, g, kt, d0:d1]
                        pairs += [(vh, ph), (vh, pl), (vl, ph)]
                    last = passes(dst[0:d1 - d0, col:col + SP], pairs)
                last.then_inc(ring_full, 1)

            def project(i, part):
                pe.wait_ge(ring_dve, position(part, i, ("pv", HEADS - 1), "d"))
                for t in range(2):
                    dst = use(part, i, ("y", t))
                    m = T1 if t else T0
                    pairs = []
                    for j in range(HEADS):
                        first = HEADS * T0 * t + j
                        rows = slice(first, first + HEADS * (m - 1) + 1, HEADS)
                        oh, ol, ohh, ol1 = o_h[:, 0, rows], o_l[:, rows], o_h[:, 1, rows], o_l1[:, rows]
                        pairs += [(oh, wp_h[:, j, :]), (oh, wp_l[:, j, :]), (ol, wp_h[:, j, :]),
                                  (ohh, wp_hl[:, j, :]), (ol1, wp_hl[0:64, j, :])]
                    passes(dst[0:m, 0:D], pairs).then_inc(ring_full, 1)

            def turn(i, part):
                for kind in "qk":
                    for n in range(4):
                        qk(i, part, kind, n)
                if part != "first":
                    zt(part, i, i - 1)
                if part != "last":
                    xt(i, part, i + 1)
                if part != "first":
                    gate(part, i, i - 1)
                if part != "last":
                    for n in range(8):
                        v_product(i, part, n)
                pe.wait_ge(q_doubled, i * 16 + 16)
                pe.wait_ge(ring_dve, position(part, i, ("k", 3), "d"))
                for s in range(HEADS + 3):
                    if s < HEADS:
                        scores(i, s)
                    if 0 <= s - 2 < HEADS:
                        probs_turn(i, s - 2)
                    if s == 5 and part != "first":
                        counting(part, i, i - 1)
                    if 0 <= s - 3:
                        pv(i, part, s - 3)
                project(i, part)

            xt(0, "before", 0)
            for n in range(8):
                v_product(0, "before", n)
            turn(0, "first")
            with pe.Fori(1, LAST) as i:
                turn(i, "mid")
            turn(LAST, "last")
            zt("after", LAST, LAST)
            gate("after", LAST, LAST)
            counting("after", LAST, LAST)
            pe.wait_ge(rows_scattered, 64 * B)
            nc.tensor.transpose(bank[0][0:1, 0:1], ident[0:1, 0:1], ident[0:1, 0:1]).then_inc(stage2_done, 1)
            pe.wait_ge(stage2_done, 4)

            def zs_turn(e, c, first):
                pe.wait_ge(z_scaled, e * CHUNKS + (c + 1))
                if not (first and c == 0):
                    pe.wait_ge(zt_low, e * CHUNKS + c)
                for k in range(2):
                    for t in range(TILES):
                        last = nc.tensor.transpose(bank[4 + k][:, t * TM:(t + 1) * TM], zs[:, c % 2, t, 128 * k:128 * k + 128],
                                                   ident[0:TM, 0:TM])
                last.then_inc(zt_full, 1)

            def gate_up(e, c, first):
                pe.wait_ge(zt_low, e * CHUNKS + (c + 1))
                b = c % 2
                for n in range(2 * HT):
                    r = n // 2 + HT * (n % 2)
                    if c or n >= 4:
                        pe.wait_ge(act_ready, e * (HT * CHUNKS) + (c * HT + n // 2 - 1))
                    last = passes(bank[(c * 2 * HT + n) % 4][:, 0:CN], [
                        (up_h[:, r, :], zst_h[:, b, 0, :]), (up_l[:, r, :], zst_h[:, b, 0, :]), (up_h[:, r, :], zst_l[:, b, 0, :]),
                        (up_hl[:, r, :], zst_h[:, b, 1, :]), (up_hl[0:64, r, :], zst_l[0:64, b, 1, :])])
                    last.then_inc(gu_full, 1)

            def down(e, c, first):
                pe.wait_ge(act_low, e * (HT * CHUNKS) + HT * (c + 1))
                if not (first and c == 0):
                    pe.wait_ge(y_ready, e * CHUNKS + c)
                for t in range(TILES):
                    rows = slice(t * TM, (t + 1) * TM)
                    pairs = []
                    for h in range(HT):
                        ah, al = act_h[:, c % 2, h, rows], act_l[:, c % 2, h, rows]
                        pairs += [(ah, down_h[:, h, :]), (ah, down_l[:, h, :]), (al, down_h[:, h, :])]
                    last = passes(bank[6 + t // 2][0:TM, (t % 2) * D:(t % 2) * D + D], pairs)
                    if t % 2:
                        last.then_inc(y_full, 1)

            def expert(e, first):
                pe.wait_ge(ew_loaded, e * 64 + 64)
                if not first:
                    pe.wait_ge(act_ready, e * (HT * CHUNKS))
                for r in range(2 * HT):
                    if r >= 4:
                        pe.wait_ge(ew_low, e * (3 * HT) + (r - 3))
                    nc.tensor.transpose(bank[r % 4][:, 0:128], up_raw[:, r, 0:128], ident[:])
                    nc.tensor.transpose(bank[r % 4][:, 128:256], up_raw[:, r, 128:256], ident[:]).then_inc(ew_full, 1)
                for h in range(HT):
                    pe.wait_ge(ew_low, e * (3 * HT) + (2 * HT + h - 3))
                    cols = slice(128 * h, 128 * h + 128)
                    nc.tensor.transpose(bank[h][:, 0:128], down_raw[:, 0, cols], ident[:])
                    nc.tensor.transpose(bank[h][:, 128:D], down_raw[0:D1, 1, cols], ident[0:D1, 0:D1]).then_inc(ew_full, 1)
                zs_turn(e, 0, first)
                pe.wait_ge(ew_low, e * (3 * HT) + 3 * HT)
                for c in range(CHUNKS):
                    if c + 1 < CHUNKS:
                        zs_turn(e, c + 1, False)
                    gate_up(e, c, first)
                    if c:
                        down(e, c - 1, first)
                down(e, CHUNKS - 1, first)

            expert(0, True)
            with pe.Fori(1, E) as e:
                expert(e, False)
    return SLOTS


_INS = ["x", "txt", "L0_tok_W", "L0_tok_b", "L0_tok_cls_tok", "L0_tok_pos_emb", "L0_attn_W_qkv", "L0_attn_b_qkv",
        "L0_attn_W_proj", "L0_attn_b_proj", "L0_ffn_gate_w", "L0_ffn_w13", "L0_ffn_w2", "L0_ffn_norm_w"]


def slots_of(tokens, experts):
    capacity = -(-5 * TOP_K * tokens // (4 * experts))
    tile = -(-capacity // (CHUNKS * TILES))
    return CHUNKS * TILES * (tile + tile % 2)


def kernel(**inputs):
    import numpy as np
    import concourse.bacc as bacc
    from concourse.bass_utils import run_bass_kernel_spmd

    nc = bacc.Bacc("TRN2", target_bir_lowering=False, num_devices=1)
    arrays, args = {}, []
    for name in _INS:
        a = np.ascontiguousarray(inputs[name])
        arrays[f"in_{name}"] = a
        args.append(nc.dram_tensor(f"in_{name}", a.shape, mybir.dt.from_np(a.dtype), kind="ExternalInput").ap())
    batch, text, width = arrays["in_txt"].shape
    grid = arrays["in_x"].shape[2] // PATCH
    tokens = batch * (grid * grid + 1 + text)
    rows = tokens + slots_of(tokens, arrays["in_L0_ffn_gate_w"].shape[0])
    out = nc.dram_tensor("out_rows", (rows, width), F32, kind="ExternalOutput").ap()
    build(nc, *args, out)
    r = run_bass_kernel_spmd(nc, [arrays], core_ids=[0])
    return r.results[0]["out_rows"][:tokens].reshape(batch, -1, width)
```

```python
from contextlib import ExitStack

import concourse.bass as bass
from concourse import mybir

F32 = mybir.dt.float32
F32R = mybir.dt.float32r
I32 = mybir.dt.int32
ALU = mybir.AluOpType
ACT = mybir.ActivationFunctionType
AXIS = mybir.AxisListType

HEADS = 8
PATCH = 16
HIDDEN = 512
TOP_K = 2
TICKS = 64
CHUNKS = 4
TILES = 4
COUNT_STEP = 8
XT_STEP = 8
V_CHUNKS = ((0,), (1,), (2, 3))
LN_EPS = 1e-5
RMS_EPS = 1e-6


class Count:

    def __init__(self, before, first, each):
        self.before, self.first, self.each = before, first, each

    def start(self, turn):
        if isinstance(turn, int) and turn == 0:
            return self.before
        return (turn - 1) * self.each + (self.before + self.first)


class Uses:

    WHO = {"q": "ad", "k": "ad", "zt": "a", "xt": "ad", "log": "d", "cnt": "d", "pv": "ad", "y": "d", "v": "a"}

    def __init__(self, banks):
        pv = [("pv", g) for g in range(HEADS)]
        q = [("q", n) for n in range(4)]
        k = [("k", n) for n in range(4)]
        v = [("v", n) for n in range(8)]
        xt, y = [("xt", 0)], [("y", 0), ("y", 1)]
        turn = xt + [pv[5], v[0], pv[6], v[1], pv[7]] + v[2:4] + y + q + k + [("zt", 0), v[4], ("log", 0)] + v[5:]
        self.lists = {
            "before": xt + v + q + k,
            "first": pv[:5] + turn,
            "mid": pv[:5] + [("cnt", 0)] + turn,
            "last": pv[:5] + [("cnt", 0)] + pv[5:] + y + [("zt", 0), ("log", 0)],
            "after": [("cnt", 0)],
        }
        self.banks = banks
        assert len(self.lists["mid"]) % banks == 0

    @staticmethod
    def who(name):
        return Uses.WHO[name[0]]

    def size(self, part, e=None):
        return sum(1 for n in self.lists[part] if e is None or e in self.who(n))

    def count(self, e):
        return Count(self.size("before", e), self.size("first", e), self.size("mid", e))


def split(x):
    return 128, x - 128


def build(nc, x, txt, tok_w, tok_b, cls_tok, pos_emb, w_qkv, b_qkv, w_proj, b_proj, gate_w, w13, w2, norm_w, out):
    B, C, IMG, _ = x.shape
    TXT, D = txt.shape[1:]
    GRID = IMG // PATCH
    IMG_T = GRID * GRID + 1
    S = IMG_T + TXT
    N = B * S
    E = gate_w.shape[0]
    CAP = -(-5 * TOP_K * N // (4 * E))
    D0, D1 = split(D)
    T0 = (S + 1) // 2
    T1 = S - T0
    HALF = HEADS // 2
    assert HALF * S <= HEADS * T0
    SP = S + 1
    ROWS = S * HEADS
    W = HEADS * D
    ROW = D + 1 + E
    TM = -(-CAP // (CHUNKS * TILES))
    TM += TM % 2
    SLOTS = CHUNKS * TILES * TM
    CN = TILES * TM
    HT = HIDDEN // 128
    ADDED = 16 * TILES * CHUNKS // 2
    KP = C * PATCH * PATCH
    KT = KP // 128
    SEQS = min(B, 16)
    RT = B // SEQS
    IR = SEQS * GRID
    PY = PATCH * IMG
    LAST = B - 1
    GB = 5
    uses = Uses(GB)

    images_rows = nc.dram_tensor("images_rows", (B, IMG_T, D), F32, kind="Internal").ap()
    v_rows = nc.dram_tensor("v_rows", (ROWS, D), F32, kind="Internal").ap()
    slot_rows = nc.dram_tensor("slot_rows", (E * SLOTS + 4 * T0, ROW), F32, kind="Internal").ap()

    persistent = ExitStack()
    with persistent:
        def sb(name, shape, dt=F32, at=None):
            return (at or persistent).enter_context(nc.sbuf_tensor(name, shape, dt))

        def sem(name):
            return persistent.enter_context(nc.semaphore(name))

        bank = [persistent.enter_context(nc.psum_tensor(f"bank{n}", [128, 512], F32)) for n in range(8)]
        ring = bank[:GB]
        score_bank = bank[5:7]
        probs_t_bank = bank[7]

        ident = sb("ident", [128, 128])
        earlier = sb("earlier", [T0, T0])
        ones = sb("ones", [T0, T0])
        expert_no = sb("expert_no", [T0, 2, E])
        slot_base = sb("slot_base", [T0, 2, E])
        dump_row = sb("dump_row", [T0, 2, TOP_K])
        real = sb("real", [T0, 2, 1])
        minus_half = sb("minus_half", [128, 4])
        tick = sb("tick", [1, 3 * TICKS])
        norm_cols = sb("norm_cols", [128, 2, E])

        const_made = sem("const_made")
        const_ready = sem("const_ready")
        const_loaded = sem("const_loaded")
        slots_cleared = sem("slots_cleared")
        w_loaded = sem("w_loaded")
        w_high = sem("w_high")
        w_low = sem("w_low")
        bias_loaded = sem("bias_loaded")
        bias_high = sem("bias_high")
        images_loaded = sem("images_loaded")
        image_args_loaded = sem("image_args_loaded")
        regrouped = sem("regrouped")
        token_bias = sem("token_bias")
        pt_full = sem("pt_full")
        pt_high = sem("pt_high")
        pt_low = sem("pt_low")
        emb_full = sem("emb_full")
        emb_free = sem("emb_free")
        emb_stored = sem("emb_stored")
        stage1_done = sem("stage1_done")

        attention = ExitStack()

        def sa(name, shape, dt=F32):
            return sb(name, shape, dt, attention)

        wq_h = sa("wq_h", [128, 3 * W], F32R)
        wq_l = sa("wq_l", [128, 3 * W], F32R)
        wq_hl = sa("wq_hl", [128, 3 * W], F32R)
        wq_hb = sa("wq_hb", [128, 3 * W], F32R)
        wp_h = sa("wp_h", [128, HEADS, D], F32R)
        wp_l = sa("wp_l", [128, HEADS, D], F32R)
        wp_hl = sa("wp_hl", [128, HEADS, D], F32R)
        proj_bias = sa("proj_bias", [T0, D])
        gate_t = sa("gate_t", [128, 2, E])

        stage1 = ExitStack()

        def s1(name, shape, dt=F32):
            return sb(name, shape, dt, stage1)

        w_raw = s1("w_raw", [128, 2, W])
        img = s1("img", [IR, C, PY])
        img_grouped = s1("img_grouped", [IR, GRID, KP])
        tok_raw = s1("tok_raw", [128, 2, KP])
        tok_h = s1("tok_h", [128, KT, D], F32R)
        tok_l = s1("tok_l", [128, KT, D], F32R)
        pt_h = s1("pt_h", [128, KT, IR], F32R)
        pt_l = s1("pt_l", [128, KT, IR], F32R)
        pos = s1("pos", [IR, GRID * D])
        tok_bias = s1("tok_bias", [IR, D])
        emb = s1("emb", [IR, GRID, D])
        cls = s1("cls", [B, D])
        cls_pos = s1("cls_pos", [B, D])
        init_row = s1("init_row", [TM, CHUNKS * TILES, ROW])
        stage1.close()

        q_h = sa("q_h", [128, 2, ROWS + 1], F32R)
        q_l = sa("q_l", [128, ROWS + 1], F32R)
        q_l1 = sa("q_l1", [64, ROWS + 1], F32R)
        k_h = sa("k_h", [128, ROWS + 1], F32R)
        k_l = sa("k_l", [128, ROWS + 1], F32R)
        k_hl = sa("k_hl", [128, ROWS + 1], F32R)
        o_h = sa("o_h", [128, 2, ROWS], F32R)
        o_l = sa("o_l", [128, ROWS], F32R)
        o_l1 = sa("o_l1", [64, ROWS], F32R)
        v_h = sa("v_h", [T0, HEADS, 2, D], F32R)
        v_l = sa("v_l", [T0, HEADS, 2, D], F32R)
        v_out = sa("v_out", [T0, 4, 2 * D])
        probs = sa("probs", [T0, 3, 2, SP])
        pt2_h = sa("pt2_h", [T0, 2, 2, SP], F32R)
        pt2_l = sa("pt2_l", [T0, 2, 2, SP], F32R)
        xt_h = sa("xt_h", [128, 2, SP], F32R)
        xt_l = sa("xt_l", [128, SP], F32R)
        xt_l1 = sa("xt_l1", [128, SP], F32R)
        h_in = sa("h_in", [T0, 2, D])
        h_res = sa("h_res", [T0, 2, D])
        x_norm = sa("x_norm", [T0, 2, D + D1])
        h_mid = sa("h_mid", [T0, 2, D])
        z_row = sa("z_row", [T0, 2, ROW])
        z_t = sa("z_t", [128, 2, S])
        neg_max = sa("neg_max", [T0, HEADS, 2])
        row_sum = sa("row_sum", [T0, HEADS, 2])
        row_inv = sa("row_inv", [T0, HEADS, 2])
        stats = sa("stats", [T0, 2, 2, 6])
        neg_mean = sa("neg_mean", [T0, 2])
        mean_var = sa("mean_var", [T0, 2, 2, 2])
        rs = sa("rs", [T0, 2, 4, 2])
        logits = sa("logits", [T0, 2, E])
        rt = sa("rt", [T0, 12, 2, E])
        r1 = sa("r1", [T0, 8, 2, 1])
        counts = sa("counts", [T0, 3, E])
        base = sa("base", [T0, E])
        slot_of = sa("slot_of", [T0, 2, TOP_K, E])
        slot_f = sa("slot_f", [T0, 2, TOP_K, 1])
        slot_i = sa("slot_i", [T0, 2, TOP_K], I32)
        attention.close()

        experts = ExitStack()

        def se(name, shape, dt=F32):
            return sb(name, shape, dt, experts)

        up_raw = se("up_raw", [128, 2 * HT, D + D1])
        down_raw = se("down_raw", [128, 2, HIDDEN])
        up_h = se("up_h", [128, 2 * HT, 128], F32R)
        up_l = se("up_l", [128, 2 * HT, 128], F32R)
        up_hl = se("up_hl", [128, 2 * HT, 128], F32R)
        down_h = se("down_h", [128, HT, D], F32R)
        down_l = se("down_l", [128, HT, D], F32R)
        zs_in = se("zs_in", [TM, 2, TILES, ROW])
        zs = se("zs", [TM, 2, TILES, D + D1])
        zw = se("zw", [TM, CHUNKS, TILES, D])
        square = se("square", [TM, D])
        zr = se("zr", [TM, 2, 5, TILES])
        zst_h = se("zst_h", [128, 2, 2, CN], F32R)
        zst_l = se("zst_l", [128, 2, 2, CN], F32R)
        silu = se("silu", [128, HT, CN])
        act = se("act", [128, 2, HT, CN])
        act_h = se("act_h", [128, 2, HT, CN], F32R)
        act_l = se("act_l", [128, 2, HT, CN], F32R)
        y_out = se("y_out", [TM, 2, TILES, D])
        token_i = se("token_i", [TM, CHUNKS, TILES], I32)
        weight = se("weight", [TM, CHUNKS, TILES])
        experts.close()

        pads_ready = sem("pads_ready")
        h_loaded = sem("h_loaded")
        res_loaded = sem("res_loaded")
        res_biased = sem("res_biased")
        ln1_stats = sem("ln1_stats")
        x_ready = sem("x_ready")
        ring_full = sem("ring_full")
        ring_act = sem("ring_act")
        ring_dve = sem("ring_dve")
        q_doubled = sem("q_doubled")
        v_stored = [sem(f"v_stored{n}") for n in range(4)]
        v_loaded = [sem(f"v_loaded{n}") for n in range(2)]
        v_high = sem("v_high")
        v_ready = sem("v_ready")
        scores_full = sem("scores_full")
        max_ready = sem("max_ready")
        exp_done = sem("exp_done")
        inv_ready = sem("inv_ready")
        probs_ready = sem("probs_ready")
        probs_t_full = sem("probs_t_full")
        probs_t_high = sem("probs_t_high")
        probs_t_low = sem("probs_t_low")
        h_mid_ready = sem("h_mid_ready")
        h_mid_stored = sem("h_mid_stored")
        ln2_stats = sem("ln2_stats")
        ln2_rs = sem("ln2_rs")
        z_ready = sem("z_ready")
        route_sub = sem("route_sub")
        route_exp = sem("route_exp")
        chosen = sem("chosen")
        counts_ready = sem("counts_ready")
        slots_ranked = sem("slots_ranked")
        slots_ready = sem("slots_ready")
        rows_scattered = sem("rows_scattered")
        dve_step = sem("dve_step")
        stats_step = [sem(f"stats_step{n}") for n in range(2)]
        pool_step = sem("pool_step")
        stage2_done = sem("stage2_done")

        ew_loaded = sem("ew_loaded")
        ew_full = sem("ew_full")
        ew_high = sem("ew_high")
        ew_low = sem("ew_low")
        z_loaded = [sem(f"z_loaded{n}") for n in range(2)]
        z_square = sem("z_square")
        z_scale = sem("z_scale")
        z_scaled = sem("z_scaled")
        z_weighted = sem("z_weighted")
        zt_full = sem("zt_full")
        zt_high = sem("zt_high")
        zt_low = sem("zt_low")
        gu_full = sem("gu_full")
        silu_ready = sem("silu_ready")
        act_ready = sem("act_ready")
        act_high = sem("act_high")
        act_low = sem("act_low")
        y_full = sem("y_full")
        y_ready = sem("y_ready")
        y_added = [sem(f"y_added{n}") for n in range(2)]

        block = persistent.enter_context(nc.Block())

        def load_tokens(eng, dst, b, signal):
            eng.dma_start(dst[0:IMG_T, 0, :], images_rows[b]).then_inc(signal, 16)
            eng.dma_start(dst[IMG_T:T0, 0, :], txt[b, 0:T0 - IMG_T, :]).then_inc(signal, 16)
            eng.dma_start(dst[0:T1, 1, :], txt[b, T0 - IMG_T:TXT, :]).then_inc(signal, 16)

        def position(part, turn, name, e=None):
            seq = [n for n in uses.lists[part] if e is None or e in uses.who(n)]
            c = uses.count(e)
            begin = {"before": 0, "after": None}.get(part, c.start(turn))
            if part == "after":
                begin = c.start(LAST) + uses.size("last", e)
            return begin + (seq.index(name) + 1)

        def part_of(turn):
            if not isinstance(turn, int):
                return "mid"
            return "first" if turn == 0 else "last" if turn == LAST else "mid"

        def ring_bank(part, name):
            begin = {"before": 0, "first": uses.size("before")}.get(part)
            if begin is None:
                begin = uses.size("before") + uses.size("first")
            if part == "after":
                begin += uses.size("last")
            return ring[(begin + uses.lists[part].index(name)) % GB]

        def carried(eng, row, carrier):
            cell = 1

            def wait(signal, value):
                nonlocal cell
                eng.wait_ge(signal, value)
                if not isinstance(value, int):
                    at = TICKS * row + cell
                    carrier(tick[0:1, at:at + 1])
                    cell += 1
            return wait

        def step_counter(eng, signal, wait=None):
            class Steps:
                start, n = 0, 0

                def turn(self, start):
                    self.start, self.n = start, 0

                def __call__(self, ins, carry=False):
                    self.n += 1
                    ins.then_inc(signal, 1)
                    (wait if wait and carry else eng.wait_ge)(signal, self.start + self.n)
            return Steps()

        @block.sync
        def _(sp):
            def load_w(dst, src, third, signal):
                if third == 2:
                    sp.dma_start(dst, src).then_inc(signal, 16)
                    return
                to = dst.rearrange("p (n c) -> p n c", c=2 * D)
                of = src.rearrange("p (n k d) -> p n k d", k=2, d=D)
                for k in range(2):
                    sp.dma_start(to[:, :, 128 * k:128 * k + 128], of[:, :, k, 0:128]).then_inc(signal, 16)
                    sp.dma_start(to[:, :, 256 + D1 * k:256 + D1 * k + D1], of[:, :, k, 128:D]).then_inc(signal, 16)

            sp.dma_start(proj_bias[:], b_proj.rearrange("(a d) -> a d", a=1).to_broadcast([T0, D])).then_inc(const_loaded, 16)
            with nc.allow_non_contiguous_dma(reason="few small columns"):
                gate_cols = gate_w.rearrange("e d -> d e")
                sp.dma_start(gate_t[:, 0, :], gate_cols[0:128, :]).then_inc(const_loaded, 16)
                sp.dma_start(gate_t[0:D1, 1, :], gate_cols[128:D, :]).then_inc(const_loaded, 16)
                norm_c = norm_w.rearrange("e d -> d e")
                sp.dma_start(norm_cols[:, 0, :], norm_c[0:128, :]).then_inc(const_loaded, 16)
                sp.dma_start(norm_cols[0:D1, 1, :], norm_c[128:D, :]).then_inc(const_loaded, 16)
                sp.dma_start(norm_cols[D1:2 * D1, 1, :], norm_c[128:D, :]).then_inc(const_loaded, 16)
            sp.dma_start(tok_raw[:, 0, :], tok_w[0:128, :]).then_inc(image_args_loaded, 16)
            sp.dma_start(tok_raw[0:D1, 1, :], tok_w[128:D, :]).then_inc(image_args_loaded, 16)
            sp.dma_start(tok_bias[:], tok_b.rearrange("(a d) -> a d", a=1).to_broadcast([IR, D])).then_inc(image_args_loaded, 16)
            pos_rows = pos_emb[0, 1:IMG_T, :].rearrange("(h w) d -> h (w d)", w=GRID)
            for s in range(SEQS):
                sp.dma_start(pos[s * GRID:(s + 1) * GRID, :], pos_rows).then_inc(image_args_loaded, 16)
            sp.dma_start(cls[:], cls_tok[0].to_broadcast([B, D])).then_inc(image_args_loaded, 16)
            sp.dma_start(cls_pos[:], pos_emb[0, 0:1, :].to_broadcast([B, D])).then_inc(image_args_loaded, 16)
            for r in range(RT):
                if r:
                    sp.wait_ge(regrouped, r)
                for s in range(SEQS):
                    src = x[r * SEQS + s].rearrange("c (g y) w -> g c (y w)", y=PATCH)
                    sp.dma_start(img[s * GRID:(s + 1) * GRID, :, :], src).then_inc(images_loaded, 16)
            for n in range(3):
                if n:
                    sp.wait_ge(w_low, n)
                cols = slice(n * W, (n + 1) * W)
                load_w(w_raw[:, 0, :], w_qkv[0:128, cols], n, w_loaded)
                for half in range(2):
                    load_w(w_raw[half * D1:(half + 1) * D1, 1, :], w_qkv[128:D, cols], n, w_loaded)
            sp.wait_ge(w_low, 3)
            wp = w_proj.rearrange("(h d) n -> d h n", d=D)
            as_heads = w_raw[:].rearrange("p a (h n) -> p a h n", h=HEADS)
            sp.dma_start(as_heads[:, 0], wp[0:128]).then_inc(w_loaded, 16)
            for half in range(2):
                sp.dma_start(as_heads[half * D1:(half + 1) * D1, 1], wp[128:D]).then_inc(w_loaded, 16)
            sp.wait_ge(w_low, 4)
            for row in (64, 96):
                for n in range(2):
                    load_w(w_raw[row:row + 1, n, :], b_qkv[n * W:(n + 1) * W].rearrange("(a d) -> a d", a=1), n, bias_loaded)
            sp.wait_ge(bias_high, 2)
            for row in (64, 96):
                sp.dma_start(w_raw[row:row + 1, 0, :], b_qkv[2 * W:3 * W].rearrange("(a d) -> a d", a=1)).then_inc(bias_loaded, 16)
            for r in range(RT):
                sp.wait_ge(emb_free, GRID * (r + 1))
                for s in range(SEQS):
                    dst = images_rows[r * SEQS + s, 1:IMG_T, :].rearrange("(h w) d -> h w d", w=GRID)
                    sp.dma_start(dst, emb[s * GRID:(s + 1) * GRID, :, :]).then_inc(emb_stored, 16)
            sp.wait_ge(token_bias, 2)
            sp.dma_start(images_rows[:, 0, :], cls[:]).then_inc(emb_stored, 16)
            sp.wait_ge(emb_stored, 16 * (B + 1))
            sp.wait_ge(slots_cleared, 16 * (E + 1))

            def v_chunk(n):
                t, c = n // 4, n % 4
                rows = v_rows.rearrange("(s h) d -> s (h d)", h=HEADS)
                return rows[t * T0:t * T0 + (T1 if t else T0), c * 2 * D:(c + 1) * 2 * D]

            def store_v(b, turn, part, t):
                for n in range(4 * t, 4 * t + 4):
                    sp.wait_ge(ring_act, position(part, turn, ("v", n), "a"))
                    m = T1 if t else T0
                    sp.dma_start(v_chunk(n), v_out[0:m, n % 4, :]).then_inc(v_stored[n % 4], 16)

            def load_v(b, t):
                for stored in v_stored:
                    sp.wait_ge(stored, b * 32 + 16 * (t + 1))
                heads = v_rows.rearrange("(h s) d -> s h d", h=HEADS)[:, HALF * t:HALF * t + HALF, :]
                dst = v_l[:, HALF * t:HALF * t + HALF].bitcast(F32)
                sp.dma_start(dst[:, :, 0, :], heads[0:T0]).then_inc(v_loaded[t], 16)
                sp.dma_start(dst[0:T1, :, 1, :], heads[T0:S]).then_inc(v_loaded[t], 16)

            def double_q(turn, part):
                sp.wait_ge(ring_dve, position(part, turn, ("q", 3), "d"))
                sp.dma_start(q_h[64:128, 1, 0:ROWS].bitcast(F32), q_h[0:64, 1, 0:ROWS].bitcast(F32)).then_inc(q_doubled, 16)

            def turn(i, part):
                if part != "last":
                    sp.wait_ge(x_ready, 2 * i + 2)
                    load_tokens(sp, h_in, i + 1, h_loaded)
                if part != "first":
                    sp.wait_ge(h_mid_ready, i)
                load_v(i, 1)
                load_tokens(sp, h_res, i, res_loaded)
                if part != "last":
                    for loaded in v_loaded:
                        sp.wait_ge(loaded, i * 32 + 32)
                    store_v(i + 1, i, part, 0)
                    sp.wait_ge(ring_full, position(part, i, ("pv", HALF - 1)))
                    load_v(i + 1, 0)
                sp.wait_ge(h_mid_ready, i + 1)
                sp.dma_start(out[bass.ds(i * S, T0), :], h_mid[:, 0, :]).then_inc(h_mid_stored, 16)
                sp.dma_start(out[bass.ds(i * S + T0, T1), :], h_mid[0:T1, 1, :]).then_inc(h_mid_stored, 16)
                if part != "last":
                    double_q(i, part)
                    store_v(i + 1, i, part, 1)

            sp.wait_ge(stage1_done, 4)
            sp.wait_ge(pads_ready, 1)
            load_tokens(sp, h_in, 0, h_loaded)
            store_v(0, 0, "before", 0)
            load_v(0, 0)
            store_v(0, 0, "before", 1)
            double_q(0, "before")
            turn(0, "first")
            with sp.Fori(1, LAST) as i:
                turn(i, "mid")
            turn(LAST, "last")
            sp.wait_ge(rows_scattered, 64 * B)
            sp.wait_ge(h_mid_stored, 32 * B)
            sp.wait_ge(stage2_done, 4)

            def expert(e, first):
                if not first:
                    sp.wait_ge(ew_full, e * (3 * HT))
                sp.dma_start(up_raw[:, :, 0:D], w13[e].rearrange("(t p) d -> p t d", p=128)).then_inc(ew_loaded, 16)
                sp.dma_start(up_raw[:, :, D:], w13[e].rearrange("(t p) d -> p t d", p=128)[:, :, 128:D]).then_inc(ew_loaded, 16)
                sp.dma_start(down_raw[:, 0, :], w2[e, 0:128, :]).then_inc(ew_loaded, 16)
                sp.dma_start(down_raw[0:D1, 1, :], w2[e, 128:D, :]).then_inc(ew_loaded, 16)
                for c in range(CHUNKS):
                    if not (first and c < 2):
                        sp.wait_ge(z_scaled, e * CHUNKS + (c - 1))
                        sp.wait_ge(z_weighted, e * CHUNKS + (c - 1))
                    src = slot_rows[bass.ds(e * SLOTS + c * CN, CN), :].rearrange("(t p) d -> p t d", p=TM)
                    sp.dma_start(zs_in_of(e, c), src).then_inc(z_loaded[c % 2], 16)

            def zs_in_of(e, c):
                return zs_in[:, c % 2, :, :]
            expert(0, True)
            with sp.Fori(1, E) as e:
                expert(e, False)
            for added in y_added:
                sp.wait_ge(added, ADDED * E)

        @block.gpsimd
        def _(pool):
            wait = carried(pool, 0, lambda to: nc.gpsimd.tensor_tensor(to, tick[0:1, 0:1], tick[0:1, 0:1], ALU.add))
            step = step_counter(pool, pool_step, wait)
            nc.gpsimd.memset(ident[:], 0.0).then_inc(const_made, 1)
            nc.gpsimd.memset(earlier[:], 1.0).then_inc(const_made, 1)
            nc.gpsimd.memset(real[:], 1.0).then_inc(const_made, 1)
            nc.gpsimd.memset(tick[:], 0.0).then_inc(const_made, 1)
            nc.gpsimd.memset(init_row[:], 0.0).then_inc(const_made, 1)
            pool.wait_ge(const_made, 5)
            nc.gpsimd.affine_select(out=ident[:], in_=ident[:], compare_op=ALU.not_equal, fill=1.0, base=0,
                                    pattern=[[-1, 128]], channel_multiplier=1).then_inc(const_ready, 1)
            nc.gpsimd.affine_select(out=earlier[:], in_=earlier[:], compare_op=ALU.is_gt, fill=0.0, base=0,
                                    pattern=[[1, T0]], channel_multiplier=-1).then_inc(const_ready, 1)
            nc.gpsimd.affine_select(out=real[:], in_=real[:], compare_op=ALU.is_gt, fill=0.0, base=S,
                                    pattern=[[-T0, 2], [0, 1]], channel_multiplier=-1).then_inc(const_ready, 1)
            nc.gpsimd.memset(ones[:], 1.0).then_inc(const_ready, 1)
            nc.gpsimd.memset(minus_half[:], -0.5).then_inc(const_ready, 1)
            nc.gpsimd.iota(expert_no[:], pattern=[[0, 2], [1, E]], base=-E, channel_multiplier=0,
                           allow_small_or_imprecise_dtypes=True).then_inc(const_ready, 1)
            nc.gpsimd.iota(slot_base[:], pattern=[[0, 2], [SLOTS, E]], base=0, channel_multiplier=0,
                           allow_small_or_imprecise_dtypes=True).then_inc(const_ready, 1)
            nc.gpsimd.iota(dump_row[:], pattern=[[2 * T0, 2], [T0, TOP_K]], base=E * SLOTS, channel_multiplier=1,
                           allow_small_or_imprecise_dtypes=True).then_inc(const_ready, 1)
            nc.gpsimd.iota(init_row[:, :, D:D + 1], pattern=[[TM, CHUNKS * TILES], [0, 1]], base=N, channel_multiplier=1,
                           allow_small_or_imprecise_dtypes=True).then_inc(const_ready, 1)
            pool.wait_ge(const_ready, 9)
            for e in range(E):
                dst = slot_rows[e * SLOTS:(e + 1) * SLOTS, :].rearrange("(t p) d -> p t d", p=TM)
                pool.dma_start(dst, init_row[:]).then_inc(slots_cleared, 16)
            pool.dma_start(out[N:N + SLOTS, :].rearrange("(t p) d -> p t d", p=TM), init_row[:, :, 0:D]).then_inc(slots_cleared, 16)
            for r in range(RT):
                pool.wait_ge(images_loaded, 16 * SEQS * (r + 1))
                if r:
                    pool.wait_ge(pt_full, KT + 2 * GRID * r)
                for gw in range(GRID):
                    src = img[:].rearrange("p c (y g x) -> p (c y) g x", g=GRID, x=PATCH)[:, :, gw, :]
                    last = nc.gpsimd.tensor_copy(img_grouped[:, gw, :].rearrange("p (r x) -> p r x", x=PATCH), src)
                last.then_inc(regrouped, 1)
            pool.wait_ge(emb_stored, 16 * (B + 1))
            pool.wait_ge(slots_cleared, 16 * (E + 1))
            pool.engine_nop().then_inc(stage1_done, 1)
            pool.wait_ge(stage1_done, 4)

            def rs_start(which):
                v, y, t, u = (rs[:, which, k, :] for k in range(4))
                step(nc.gpsimd.tensor_scalar(v, mean_var[:, which, :, 1], LN_EPS, None, ALU.add))
                step(nc.gpsimd.tensor_tensor(y, v, minus_half[0:T0, 0:2], ALU.pow))

            def rs_polish(which):
                v, y, t, u = (rs[:, which, k, :] for k in range(4))
                step(nc.gpsimd.tensor_tensor(t, y, y, ALU.mult))
                step(nc.gpsimd.tensor_tensor(t, t, v, ALU.mult), carry=True)
                step(nc.gpsimd.tensor_scalar(u, t, -0.5, 1.5, ALU.mult, ALU.add))
                return nc.gpsimd.tensor_tensor(y, y, u, ALU.mult)

            def v_low(b, n):
                wait(v_high, b * HALF + (n + 1))
                g = slice(2 * n, 2 * n + 2)
                nc.gpsimd.tensor_tensor(v_l[:, g], v_l[:, g].bitcast(F32), v_h[:, g].bitcast(F32), ALU.subtract).then_inc(v_ready, 1)

            def ln1_start(b):
                wait(ln1_stats, b + 1)
                nc.gpsimd.tensor_scalar(neg_mean[:], mean_var[:, 0, :, 0], -1.0, 0.0, ALU.mult, ALU.add)
                rs_start(0)

            def ln1_apply(t):
                m, r = neg_mean[:, t:t + 1], rs[:, 0, 1, t:t + 1]
                nc.gpsimd.tensor_scalar(x_norm[:, t, 0:D], h_in[:, t, :], m, r, ALU.add, ALU.mult)
                nc.gpsimd.tensor_scalar(x_norm[:, t, D:], h_in[:, t, 128:D], m, r, ALU.add, ALU.mult).then_inc(x_ready, 1)

            def rank(b, first):
                pool.wait_ge(counts_ready, b + 1)
                pos_, keep, val = rt[:, 8], rt[:, 9], rt[:, 10]
                step(nc.gpsimd.tensor_tensor(pos_, counts[:, 0:2, :], base[:].unsqueeze(1).to_broadcast([T0, 2, E]), ALU.add))
                step(nc.gpsimd.tensor_tensor(base[:], base[:], counts[:, 2, :], ALU.add), carry=True)
                step(nc.gpsimd.tensor_scalar(keep, pos_, float(CAP), None, ALU.is_lt))
                step(nc.gpsimd.tensor_tensor(val, pos_, slot_base[:], ALU.add))
                for k in range(TOP_K):
                    dump = dump_row[:, :, k:k + 1].to_broadcast([T0, 2, E])
                    a = rt[:, 11]
                    step(nc.gpsimd.tensor_tensor(a, val, dump, ALU.subtract))
                    step(nc.gpsimd.tensor_tensor(a, a, keep, ALU.mult))
                    step(nc.gpsimd.tensor_tensor(a, a, dump, ALU.add))
                    last = nc.gpsimd.tensor_tensor(slot_of[:, :, k, :], a, rt[:, 4 + k], ALU.mult)
                    if k == 0:
                        step(last)
                last.then_inc(slots_ranked, 1)

            def scatter(b):
                wait(slots_ready, b + 1)
                for t in range(2):
                    m = T1 if t else T0
                    for k in range(TOP_K):
                        pool.indirect_dma_start(
                            out=slot_rows, out_offset=bass.IndirectOffsetOnAxis(ap=slot_i[0:m, t, k:k + 1], axis=0),
                            in_=z_row[0:m, t, :], in_offset=None).then_inc(rows_scattered, 16)

            def residual(b):
                pool.wait_ge(res_loaded, b * 48 + 48)
                nc.gpsimd.tensor_tensor(h_res[:], h_res[:], proj_bias[:].unsqueeze(1).to_broadcast([T0, 2, D]),
                                        ALU.add).then_inc(res_biased, 1)

            def normed(g, i):
                wait(inv_ready, i * HEADS + (g + 1))
                for t in range(2):
                    p = probs[:, g % 3, t, 0:S]
                    last = nc.gpsimd.tensor_scalar(p, p, row_inv[:, g, t:t + 1], float(D) ** -0.5, ALU.mult, ALU.mult)
                last.then_inc(probs_ready, 1)

            def turn(i, part, start):
                step.turn(start)
                for g in range(HEADS):
                    normed(g, i)
                    if part != "last":
                        if g == 2:
                            ln1_start(i + 1)
                        if g == 3:
                            step(rs_polish(0))
                        if g in (5, 6):
                            ln1_apply(g - 5)
                    if g in (4, 7):
                        v_low(i, g // 3 + 1)
                if part != "first":
                    rank(i - 1, False)
                residual(i)
                if part != "first":
                    scatter(i - 1)
                wait(ln2_stats, i + 1)
                rs_start(1)
                rs_polish(1).then_inc(ln2_rs, 1)
                if part != "last":
                    for n in range(2):
                        v_low(i + 1, n)
                return step.n

            pads = [q_h[:, :, ROWS:], q_l[:, ROWS:], q_l1[:, ROWS:], k_h[:, ROWS:], k_l[:, ROWS:], k_hl[:, ROWS:],
                    v_l[:], probs[:], xt_h[:], xt_l[:], xt_l1[0:64, :], h_in[:], h_res[:], base[:], z_row[:]]
            for p in pads:
                step(nc.gpsimd.memset(p.bitcast(F32) if p.dtype == F32R else p, 0.0))
            step(nc.gpsimd.memset(xt_l1[64:128, :].bitcast(F32), 1.0))
            nc.gpsimd.iota(z_row[:, :, D:D + 1], pattern=[[T0, 2], [0, 1]], base=-S, channel_multiplier=1,
                           allow_small_or_imprecise_dtypes=True).then_inc(pads_ready, 1)
            wait(pads_ready, 1)
            at = step.n
            step.turn(at)
            ln1_start(0)
            step(rs_polish(0))
            for t in range(2):
                ln1_apply(t)
            for n in range(2):
                v_low(0, n)
            at += step.n
            n0 = turn(0, "first", at)
            n_mid = n0 + 11
            with pool.Fori(1, LAST) as i:
                assert turn(i, "mid", (i - 1) * n_mid + (at + n0)) == n_mid, step.n - n0
            at = at + n0 + (LAST - 1) * n_mid
            at += turn(LAST, "last", at)
            step.turn(at)
            rank(LAST, False)
            scatter(LAST)
            at += step.n
            wait(rows_scattered, 64 * B)
            pool.engine_nop().then_inc(stage2_done, 1)
            wait(stage2_done, 4)

            def scale_chunk(e, c, first):
                b = c % 2
                wait(z_square, e * CHUNKS + (c + 1))
                ss, v, y, t, u = (zr[:, b, k, :] for k in range(5))
                step(nc.gpsimd.tensor_scalar(v, ss, 4.0 / D, RMS_EPS, ALU.mult, ALU.add))
                step(nc.gpsimd.tensor_tensor(y, v, minus_half[0:TM, 0:TILES], ALU.pow))
                step(nc.gpsimd.tensor_tensor(t, y, y, ALU.mult))
                step(nc.gpsimd.tensor_tensor(t, t, v, ALU.mult), carry=True)
                step(nc.gpsimd.tensor_scalar(u, t, -1.0, 3.0, ALU.mult, ALU.add))
                nc.gpsimd.tensor_tensor(y, y, u, ALU.mult).then_inc(z_scale, 1)
                if not first:
                    wait(y_added[b], e * ADDED)
                nc.gpsimd.tensor_copy(token_i[:, c, :], zs_in[:, b, :, D])
                step(nc.gpsimd.tensor_copy(weight[:, c, :], zs_in[:, b, :, bass.ds(e + (D + 1), 1)].rearrange("p t o -> p (t o)")), carry=True)
                for t in range(TILES):
                    last = nc.gpsimd.tensor_scalar(zw[:, c, t, :], zs_in[:, b, t, 0:D], weight[:, c, t:t + 1], None, ALU.mult)
                last.then_inc(z_weighted, 1)

            def act_lows(e, c, h):
                pool.wait_ge(act_high, e * CHUNKS * HT + (c * HT + h + 1))
                nc.gpsimd.tensor_tensor(act_l[:, c % 2, h, :], act[:, c % 2, h, :], act_h[:, c % 2, h, :].bitcast(F32),
                                        ALU.subtract).then_inc(act_low, 1)

            def add_rows(e, c, first):
                if c == 0 and not first:
                    for added in y_added:
                        wait(added, e * ADDED)
                wait(y_ready, e * CHUNKS + (c + 1))
                for t in range(TILES):
                    pool.indirect_dma_start(
                        out=out, out_offset=bass.IndirectOffsetOnAxis(ap=token_i[:, c, t:t + 1], axis=0),
                        in_=y_out[:, c % 2, t, :], in_offset=None, compute_op=ALU.add).then_inc(y_added[c % 2], 16)

            def expert(e, first, start):
                step.turn(start)
                scale_chunk(e, 0, first)
                for c in range(CHUNKS):
                    if c + 1 < CHUNKS:
                        scale_chunk(e, c + 1, first)
                    for h in range(HT):
                        act_lows(e, c, h)
                    if c:
                        add_rows(e, c - 1, first)
                add_rows(e, CHUNKS - 1, first)
                return step.n

            n = expert(0, True, at)
            with pool.Fori(1, E) as e:
                expert(e, False, (e - 1) * n + (at + n))

        @block.scalar
        def _(a):
            wait = carried(a, 1, lambda to: nc.scalar.copy(to, tick[0:1, 0:1]))
            for n in range(3):
                a.wait_ge(w_loaded, 16 * (12, 24, 27)[n])
                cols = slice(n * W, (n + 1) * W)
                nc.scalar.copy(wq_h[:, cols], w_raw[:, 0, :]).then_inc(w_high, 1)
                nc.scalar.copy(wq_hl[:, cols], w_raw[:, 1, :]).then_inc(w_high, 1)
            a.wait_ge(w_loaded, 16 * 30)
            as_heads = w_raw[:].rearrange("p a (h n) -> p a h n", h=HEADS)
            nc.scalar.copy(wp_h[:], as_heads[:, 0]).then_inc(w_high, 1)
            nc.scalar.copy(wp_hl[:], as_heads[:, 1]).then_inc(w_high, 1)
            for k in range(KT):
                a.wait_ge(pt_full, k + 1)
                nc.scalar.copy(tok_h[:, k, :], bank[k % 2][:, 0:D]).then_inc(pt_high, 1)
            for g in range(RT * GRID):
                for half in range(2):
                    n = 2 * g + half
                    a.wait_ge(pt_full, KT + n + 1)
                    src = bank[2 + n % 2][:, 0:3 * IR].rearrange("p (k r) -> p k r", k=3)
                    nc.scalar.copy(pt_h[:, 3 * half:3 * half + 3, :], src).then_inc(pt_high, 1)
            a.wait_ge(emb_stored, 16 * (B + 1))
            a.wait_ge(bias_high, 3)
            nc.scalar.copy(minus_half[0:1, 3:4], minus_half[0:1, 3:4]).then_inc(stage1_done, 1)
            a.wait_ge(stage1_done, 4)

            def use(part, i, name):
                a.wait_ge(ring_full, position(part, i, name))
                return ring_bank(part, name)

            def qk_high(i, part, kind, n):
                src = use(part, i, (kind, n))
                src = src[:, 0:3 * SP].rearrange("p (k s) -> p k s", k=3)
                main, pair = (q_h[:, 0, :], q_h[:, 1, :]) if kind == "q" else (k_h, k_hl)
                m = main[:, 0:ROWS].rearrange("p (s j) -> p j s", j=HEADS)
                r = pair[:, 0:ROWS].rearrange("p (s j) -> p j s", j=HEADS)
                nc.scalar.copy(m[:, 2 * n:2 * n + 2, :], src[:, 0:2, 0:S])
                nc.scalar.copy(r[0:64, 2 * n, :], src[0:64, 2, 0:S])
                nc.scalar.copy(r[0:64, 2 * n + 1, :], src[64:128, 2, 0:S]).then_inc(ring_act, 1)

            def xt_high(i, part, b):
                src = use(part, i, ("xt", 0))[:, 0:2 * S].rearrange("p (k s) -> p k s", k=2)
                nc.scalar.copy(xt_h[:, :, 0:S], src).then_inc(ring_act, 1)

            def v_evac(i, part, b, n):
                src = use(part, i, ("v", n))
                m = T1 if n // 4 else T0
                if not (part == "before" and n < 4):
                    a.wait_ge(v_stored[n % 4], b * 32 + 16 * (n // 4))
                nc.scalar.copy(v_out[0:m, n % 4, :], src[0:m, 0:2 * D]).then_inc(ring_act, 1)

            def zt_evac(part, i, b):
                src = use(part, i, ("zt", 0))[:, 0:2 * S].rearrange("p (k s) -> p k s", k=2)
                nc.scalar.copy(z_t[:, 0, :], src[:, 0])
                nc.scalar.copy(z_t[0:D1, 1, :], src[0:D1, 1]).then_inc(ring_act, 1)

            def route_exps(b):
                a.wait_ge(route_sub, b + 1)
                nc.scalar.activation(rt[:, 1], rt[:, 0], ACT.Exp).then_inc(route_exp, 1)

            def exps(i, g):
                a.wait_ge(max_ready, i * HEADS + (g + 1))
                src = score_bank[g % 2][0:T0, 0:2 * SP].rearrange("p (t s) -> p t s", t=2)
                for t in range(2):
                    last = nc.scalar.activation(probs[:, g % 3, t, 0:S], src[:, t, 0:S], ACT.Exp,
                                                bias=neg_max[:, g, t:t + 1], accum_out=row_sum[:, g, t:t + 1])
                last.then_inc(exp_done, 1)

            def probs_t_h(i, g):
                a.wait_ge(probs_t_full, i * HEADS + (g + 1))
                src = probs_t_bank[0:T0, 0:2 * SP].rearrange("p (t s) -> p t s", t=2)
                nc.scalar.copy(pt2_h[:, g % 2], src).then_inc(probs_t_high, 1)

            def o_high(i, part, g):
                src = use(part, i, ("pv", g))
                cols = slice(S * g, S * (g + 1))
                nc.scalar.copy(o_h[:, 0, cols], src[:, 0:S])
                nc.scalar.copy(o_h[0:64, 1, cols], src[0:64, SP:SP + S])
                nc.scalar.copy(o_h[64:128, 1, cols], src[0:64, SP:SP + S]).then_inc(ring_act, 1)

            def v_highs(b, n):
                if n % 2 == 0:
                    wait(v_loaded[n // 2], b * 32 + 32)
                g = slice(2 * n, 2 * n + 2)
                nc.scalar.copy(v_h[:, g], v_l[:, g].bitcast(F32)).then_inc(v_high, 1)

            def turn(i, part):
                nxt = part != "last"
                for s in range(HEADS + 3):
                    if 4 <= s <= HEADS:
                        o_high(i, part, s - 4)
                    if 0 <= s - 2 < HEADS:
                        probs_t_h(i, s - 2)
                    if s < HEADS:
                        exps(i, s)
                    if s in (4, 5):
                        v_highs(i, s - 2)
                    if s == XT_STEP and nxt:
                        xt_high(i, part, i + 1)
                    if s >= HEADS:
                        o_high(i, part, s - 3)
                        for n in V_CHUNKS[s - HEADS] if nxt else []:
                            v_evac(i, part, i + 1, n)
                if nxt:
                    for n in range(4):
                        qk_high(i, part, "q", n)
                        if n >= 2:
                            v_highs(i + 1, n - 2)
                    for n in range(4):
                        qk_high(i, part, "k", n)
                zt_evac(part, i, i)
                if nxt:
                    v_evac(i, part, i + 1, 4)
                route_exps(i)
                for n in range(5, 8) if nxt else []:
                    v_evac(i, part, i + 1, n)

            a.wait_ge(pads_ready, 1)
            xt_high(0, "before", 0)
            for n in range(8):
                v_evac(0, "before", 0, n)
            for kind in "qk":
                for n in range(4):
                    qk_high(0, "before", kind, n)
            for n in range(2):
                v_highs(0, n)
            turn(0, "first")
            with a.Fori(1, LAST) as i:
                turn(i, "mid")
            turn(LAST, "last")
            a.wait_ge(rows_scattered, 64 * B)
            nc.scalar.copy(minus_half[0:1, 3:4], minus_half[0:1, 3:4]).then_inc(stage2_done, 1)
            a.wait_ge(stage2_done, 4)

            def expert(e, first):
                for r in range(2 * HT):
                    a.wait_ge(ew_full, e * (3 * HT) + (r + 1))
                    nc.scalar.copy(up_h[:, r, :], bank[r % 4][:, 0:128])
                    nc.scalar.copy(up_hl[:, r, :], bank[r % 4][:, 128:256]).then_inc(ew_high, 1)
                for h in range(HT):
                    a.wait_ge(ew_full, e * (3 * HT) + (2 * HT + h + 1))
                    nc.scalar.copy(down_h[:, h, :], bank[h][:, 0:D]).then_inc(ew_high, 1)
                zt_h(e, 0)
                for c in range(CHUNKS):
                    if c + 1 < CHUNKS:
                        zt_h(e, c + 1)
                    for h in range(HT):
                        n = c * 2 * HT + 2 * h
                        a.wait_ge(gu_full, e * (2 * HT * CHUNKS) + (n + 1))
                        nc.scalar.activation(silu[:, h, :], bank[n % 4][:, 0:CN], ACT.Silu).then_inc(silu_ready, 1)
                        a.wait_ge(act_ready, e * (HT * CHUNKS) + (c * HT + h + 1))
                        nc.scalar.copy(act_h[:, c % 2, h, :], act[:, c % 2, h, :]).then_inc(act_high, 1)

            def zt_h(e, c):
                wait(zt_full, e * CHUNKS + (c + 1))
                for k in range(2):
                    last = nc.scalar.activation(zst_h[:, c % 2, k, :], bank[4 + k][:, 0:CN], ACT.Copy,
                                                scale=norm_cols[:, k, bass.ds(e, 1)])
                last.then_inc(zt_high, 1)

            expert(0, True)
            with a.Fori(1, E) as e:
                expert(e, False)

        @block.vector
        def _(v):
            wait = carried(v, 2, lambda to: nc.vector.tensor_copy(to, tick[0:1, 0:1]))
            step = step_counter(v, dve_step)
            alone = [step_counter(v, signal, wait) for signal in stats_step]
            for n in range(3):
                v.wait_ge(w_high, 2 * (n + 1))
                cols = slice(n * W, (n + 1) * W)
                nc.vector.tensor_copy(wq_hb[0:D1, cols], wq_hl[0:D1, cols].bitcast(F32))
                nc.vector.memset(wq_hb[64:128, cols].bitcast(F32), 0.0)
                nc.vector.tensor_tensor(wq_l[:, cols], w_raw[:, 0, :], wq_h[:, cols].bitcast(F32), ALU.subtract)
                step(nc.vector.tensor_tensor(wq_hl[64:128, cols], w_raw[64:128, 1, :],
                                             wq_hl[64:128, cols].bitcast(F32), ALU.subtract))
                nc.vector.memset(tok_l[:, 0, 0:1].bitcast(F32), 0.0).then_inc(w_low, 1)
            v.wait_ge(w_high, 8)
            as_heads = w_raw[:].rearrange("p a (h n) -> p a h n", h=HEADS)
            nc.vector.tensor_tensor(wp_l[:], as_heads[:, 0], wp_h[:].bitcast(F32), ALU.subtract)
            step(nc.vector.tensor_tensor(wp_hl[64:128], as_heads[64:128, 1], wp_hl[64:128].bitcast(F32), ALU.subtract))
            nc.vector.memset(tok_l[:, 0, 0:1].bitcast(F32), 0.0).then_inc(w_low, 1)
            for n in range(3):
                v.wait_ge(bias_loaded, 16 * (16 if n < 2 else 18))
                cols = slice(n * W, (n + 1) * W)
                src = w_raw[:, n % 2, :]
                nc.vector.tensor_copy(wq_hb[64:65, cols], src[64:65, :])
                step(nc.vector.tensor_copy(wq_hb[96:97, cols], src[96:97, :]))
                nc.vector.tensor_tensor(wq_hb[96:97, cols], src[96:97, :], wq_hb[96:97, cols].bitcast(F32),
                                        ALU.subtract).then_inc(bias_high, 1)
            v.wait_ge(bias_high, 3)
            v.wait_ge(image_args_loaded, 16 * (5 + SEQS))
            pos_g = pos[:].rearrange("p (w d) -> p w d", w=GRID)
            nc.vector.tensor_tensor(pos_g, pos_g, tok_bias[:].unsqueeze(1).to_broadcast([IR, GRID, D]), ALU.add).then_inc(token_bias, 1)
            nc.vector.tensor_tensor(cls[:], cls[:], cls_pos[:], ALU.add).then_inc(token_bias, 1)
            for k in range(KT):
                v.wait_ge(pt_high, k + 1)
                nc.vector.tensor_tensor(tok_l[:, k, :], bank[k % 2][:, 0:D], tok_h[:, k, :].bitcast(F32), ALU.subtract).then_inc(pt_low, 1)
            v.wait_ge(token_bias, 2)
            for g in range(RT * GRID):
                r, gw = g // GRID, g % GRID
                for half in range(2):
                    n = 2 * g + half
                    v.wait_ge(pt_high, KT + n + 1)
                    src = bank[2 + n % 2][:, 0:3 * IR].rearrange("p (k r) -> p k r", k=3)
                    ks = slice(3 * half, 3 * half + 3)
                    nc.vector.tensor_tensor(pt_l[:, ks, :], src, pt_h[:, ks, :].bitcast(F32), ALU.subtract).then_inc(pt_low, 1)
                if gw == 0 and r:
                    v.wait_ge(emb_stored, 16 * SEQS * r)
                v.wait_ge(emb_full, g + 1)
                nc.vector.tensor_tensor(emb[:, gw, :], bank[4][0:IR, 0:D], pos_g[:, gw, :], ALU.add).then_inc(emb_free, 1)
            v.wait_ge(emb_stored, 16 * (B + 1))
            nc.vector.memset(minus_half[0:1, 2:3], -0.5).then_inc(stage1_done, 1)
            v.wait_ge(stage1_done, 4)

            def use(part, i, name):
                e = uses.who(name)
                if "a" in e:
                    v.wait_ge(ring_act, position(part, i, name, "a"))
                else:
                    v.wait_ge(ring_full, position(part, i, name))
                return ring_bank(part, name)

            def qk_low(i, part, kind, n):
                src = use(part, i, (kind, n))
                src = src[:, 0:3 * SP].rearrange("p (k s) -> p k s", k=3)
                hm, lm, pair = (q_h[:, 0, :], q_l, q_h[:, 1, :]) if kind == "q" else (k_h, k_l, k_hl)
                by_chunk = lambda t: t[:, 0:ROWS].rearrange("p (s j) -> p j s", j=HEADS)
                js = slice(2 * n, 2 * n + 2)
                nc.vector.tensor_tensor(by_chunk(lm)[:, js, :], src[:, 0:2, 0:S], by_chunk(hm)[:, js, :].bitcast(F32), ALU.subtract)
                r = by_chunk(pair)
                for k in range(2):
                    j = 2 * n + k
                    dst = by_chunk(q_l1)[:, j, :] if kind == "q" else r[64:128, j, :]
                    last = nc.vector.tensor_tensor(dst, src[64 * k:64 * k + 64, 2, 0:S], r[0:64, j, :].bitcast(F32), ALU.subtract)
                last.then_inc(ring_dve, 1)

            def stat(which, src, b, signal):
                alone[which].turn(b)
                for t in range(2):
                    ins = nc.vector.bn_stats(stats[:, which, t, :], src[:, t, :])
                    if t:
                        alone[which](ins, carry=True)
                for t in range(2):
                    last = nc.vector.bn_aggr(mean_var[:, which, t, :], stats[:, which, t, :])
                last.then_inc(signal, 1)

            def apply(dst, src, which, t):
                return nc.vector.tensor_scalar(dst, src, mean_var[:, which, t, 0:1], rs[:, which, 1, t:t + 1],
                                               ALU.subtract, ALU.mult)

            def ln1_stat(b):
                v.wait_ge(h_loaded, b * 48 + 48)
                stat(0, h_in, b, ln1_stats)

            def xt_low(i, part):
                src = use(part, i, ("xt", 0))[:, 0:2 * S].rearrange("p (k s) -> p k s", k=2)
                nc.vector.tensor_tensor(xt_l[:, 0:S], src[:, 0], xt_h[:, 0, 0:S].bitcast(F32), ALU.subtract)
                nc.vector.tensor_tensor(xt_l1[0:64, 0:S], src[0:64, 1], xt_h[0:64, 1, 0:S].bitcast(F32),
                                        ALU.subtract).then_inc(ring_dve, 1)

            def bc(t):
                return t.to_broadcast([T0, 2, E])

            def route_logits(part, i, b):
                src = use(part, i, ("log", 0))[0:T0, 0:2 * E].rearrange("p (t e) -> p t e", t=2)
                nc.vector.tensor_copy(logits[0:T0, 0, :], src[0:T0, 0, :])
                step(nc.vector.tensor_copy(logits[0:T1, 1, :], src[0:T1, 1, :]))
                nc.vector.tensor_copy(rt[:, 7], logits[:]).then_inc(ring_dve, 1)
                step(nc.vector.tensor_reduce(r1[:, 0], logits[:], AXIS.X, ALU.max))
                nc.vector.tensor_tensor(rt[:, 0], logits[:], bc(r1[:, 0]), ALU.subtract).then_inc(route_sub, 1)

            def choose_likelihood(b):
                v.wait_ge(route_exp, b + 1)
                step(nc.vector.tensor_reduce(r1[:, 1], rt[:, 1], AXIS.X, ALU.add))
                step(nc.vector.reciprocal(r1[:, 2], r1[:, 1]))
                step(nc.vector.tensor_tensor(rt[:, 2], rt[:, 1], bc(r1[:, 2]), ALU.mult))

            def choose_expert(k):
                p, m, eq, pick = rt[:, 2], rt[:, 3], rt[:, 6], rt[:, 4 + k]
                rest = m if k else p
                step(nc.vector.tensor_reduce(r1[:, 3 + k], rest, AXIS.X, ALU.max))
                step(nc.vector.tensor_tensor(eq, rest, bc(r1[:, 3 + k]), ALU.is_equal))
                step(nc.vector.tensor_tensor(eq, eq, expert_no[:], ALU.mult))
                step(nc.vector.tensor_reduce(r1[:, 5], eq, AXIS.X, ALU.min))
                step(nc.vector.tensor_tensor(pick, expert_no[:], bc(r1[:, 5]), ALU.is_equal))
                if k == 0:
                    step(nc.vector.scalar_tensor_tensor(m, pick, -2.0, p, ALU.mult, ALU.add))

            def choose_weights():
                w = r1
                for k in range(TOP_K):
                    ins = nc.vector.tensor_tensor(rt[:, 4 + k], rt[:, 4 + k], bc(real[:]), ALU.mult)
                step(ins)
                nc.vector.tensor_tensor(w[:, 6], w[:, 3], w[:, 4], ALU.add)
                step(nc.vector.tensor_tensor(rt[:, 7], rt[:, 4], rt[:, 5], ALU.add))
                nc.vector.tensor_tensor(rt[:, 6], rt[:, 7], rt[:, 2], ALU.mult)
                step(nc.vector.reciprocal(w[:, 7], w[:, 6]))
                nc.vector.tensor_tensor(z_row[:, :, D + 1:], rt[:, 6], bc(w[:, 7]), ALU.mult)
                nc.vector.tensor_scalar(z_row[:, :, D:D + 1], z_row[:, :, D:D + 1], float(S), None, ALU.add).then_inc(chosen, 1)

            def route_counts(part, i, b):
                src = use(part, i, ("cnt", 0))[0:T0, 0:3 * E].rearrange("p (t e) -> p t e", t=3)
                nc.vector.tensor_copy(counts[:], src).then_inc(ring_dve, 1)
                v.wait_ge(ring_dve, position(part, i, ("cnt", 0), "d"))
                nc.vector.memset(r1[:, 5], 0.0).then_inc(counts_ready, 1)

            def route_slots(b):
                v.wait_ge(slots_ranked, b + 1)
                step(nc.vector.tensor_reduce(slot_f[:].rearrange("p t k o -> p (t k) o"), slot_of[:].rearrange("p t k e -> p (t k) e"),
                                             AXIS.X, ALU.add))
                nc.vector.tensor_copy(slot_i[:], slot_f[:].rearrange("p t k o -> p t (k o)")).then_inc(slots_ready, 1)

            def maxes(i, g):
                v.wait_ge(scores_full, i * HEADS + (g + 1))
                src = score_bank[g % 2][0:T0, 0:2 * SP].rearrange("p (t s) -> p t s", t=2)
                nc.vector.tensor_reduce(neg_max[:, g, :].unsqueeze(2), src[:, :, 0:S], AXIS.X, ALU.max, negate=True).then_inc(max_ready, 1)

            def invs(i, g):
                v.wait_ge(exp_done, i * HEADS + (g + 1))
                nc.vector.reciprocal(row_inv[:, g, :], row_sum[:, g, :]).then_inc(inv_ready, 1)

            def probs_t_l(i, g):
                v.wait_ge(probs_t_high, i * HEADS + (g + 1))
                src = probs_t_bank[0:T0, 0:2 * SP].rearrange("p (t s) -> p t s", t=2)
                nc.vector.tensor_tensor(pt2_l[:, g % 2], src, pt2_h[:, g % 2].bitcast(F32), ALU.subtract).then_inc(probs_t_low, 1)

            def o_low(i, part, g):
                src = use(part, i, ("pv", g))
                cols = slice(S * g, S * (g + 1))
                nc.vector.tensor_tensor(o_l[:, cols], src[:, 0:S], o_h[:, 0, cols].bitcast(F32), ALU.subtract)
                nc.vector.tensor_tensor(o_l1[:, cols], src[0:64, SP:SP + S], o_h[0:64, 1, cols].bitcast(F32),
                                        ALU.subtract).then_inc(ring_dve, 1)

            def y_evac(i, part):
                v.wait_ge(res_biased, i + 1)
                if part != "first":
                    v.wait_ge(h_mid_stored, i * 32)
                for t in range(2):
                    src = use(part, i, ("y", t))
                    m = T1 if t else T0
                    nc.vector.tensor_tensor(h_mid[0:m, t, :], src[0:m, 0:D], h_res[0:m, t, :], ALU.add).then_inc(ring_dve, 1)
                v.wait_ge(ring_dve, position(part, i, ("y", 1), "d"))
                nc.vector.memset(r1[:, 5], 0.0).then_inc(h_mid_ready, 1)

            def ln2_apply(i, part):
                v.wait_ge(ln2_rs, i + 1)
                if part != "first":
                    v.wait_ge(rows_scattered, i * 64)
                for t in range(2):
                    last = apply(z_row[:, t, 0:D], h_mid[:, t, :], 1, t)
                last.then_inc(z_ready, 1)

            def turn(i, part, start):
                step.turn(start)
                nxt = part != "last"
                for s in range(HEADS + 3):
                    if s < HEADS:
                        maxes(i, s)
                    if 1 <= s <= HEADS:
                        invs(i, s - 1)
                    if 4 <= s <= HEADS:
                        o_low(i, part, s - 4)
                    if 0 <= s - 2 < HEADS:
                        probs_t_l(i, s - 2)
                    if s == 2 and nxt:
                        ln1_stat(i + 1)
                    if part != "first":
                        if s == 1:
                            choose_expert(1)
                        if s == 4:
                            choose_weights()
                        if s == COUNT_STEP:
                            route_counts(part, i, i - 1)
                    if s == XT_STEP and nxt:
                        xt_low(i, part)
                    if s >= HEADS:
                        o_low(i, part, s - 3)
                if part != "first":
                    route_slots(i - 1)
                y_evac(i, part)
                stat(1, h_mid, i, ln2_stats)
                if nxt:
                    for n in range(2):
                        qk_low(i, part, "q", n)
                ln2_apply(i, part)
                if nxt:
                    for n in range(2, 4):
                        qk_low(i, part, "q", n)
                    for n in range(4):
                        qk_low(i, part, "k", n)
                route_logits(part, i, i)
                choose_likelihood(i)
                choose_expert(0)
                return step.n

            v.wait_ge(pads_ready, 1)
            nc.vector.memset(logits[:], 0.0)
            step(nc.vector.memset(h_mid[:], 0.0))
            at = step.n
            step.turn(at)
            ln1_stat(0)
            at += step.n
            xt_low(0, "before")
            for kind in "qk":
                for n in range(4):
                    qk_low(0, "before", kind, n)
            n0 = turn(0, "first", at)
            n_mid = n0 + 9
            with v.Fori(1, LAST) as i:
                got = turn(i, "mid", (i - 1) * n_mid + (at + n0))
                assert got == n_mid, got - n0
            at = at + n0 + (LAST - 1) * n_mid
            at += turn(LAST, "last", at)
            step.turn(at)
            choose_expert(1)
            choose_weights()
            route_counts("after", 0, LAST)
            route_slots(LAST)
            at += step.n
            v.wait_ge(rows_scattered, 64 * B)
            nc.vector.memset(minus_half[0:1, 2:3], -0.5).then_inc(stage2_done, 1)
            v.wait_ge(stage2_done, 4)

            def z_chunk(e, c):
                b = c % 2
                v.wait_ge(z_loaded[b], e * (8 * CHUNKS) + 16 * (c // 2 + 1))
                for t in range(TILES):
                    ins = nc.vector.tensor_tensor_reduce(square[:], zs_in[:, b, t, 0:D], zs_in[:, b, t, 0:D], 1.0, 0.0,
                                                         ALU.mult, ALU.add, zr[:, b, 0, t:t + 1])
                    if t < TILES - 1:
                        step(ins)
                ins.then_inc(z_square, 1)
                v.wait_ge(z_scale, e * CHUNKS + (c + 1))
                for t in range(TILES):
                    s_ = zr[:, b, 2, t:t + 1]
                    nc.vector.tensor_scalar(zs[:, b, t, 0:D], zs_in[:, b, t, 0:D], s_, None, ALU.mult)
                    last = nc.vector.tensor_scalar(zs[:, b, t, D:], zs_in[:, b, t, 128:D], s_, None, ALU.mult)
                last.then_inc(z_scaled, 1)

            def zt_l(e, c):
                v.wait_ge(zt_high, e * CHUNKS + (c + 1))
                for k in range(2):
                    last = nc.vector.scalar_tensor_tensor(zst_l[:, c % 2, k, :], bank[4 + k][:, 0:CN],
                                                          norm_cols[:, k, bass.ds(e, 1)], zst_h[:, c % 2, k, :].bitcast(F32),
                                                          ALU.mult, ALU.subtract)
                last.then_inc(zt_low, 1)

            def y_evac3(e, c, first):
                v.wait_ge(z_weighted, e * CHUNKS + (c + 1))
                if not (first and c < 2):
                    v.wait_ge(y_added[c % 2], e * ADDED + 16 * TILES * (c // 2))
                for u in range(2):
                    v.wait_ge(y_full, e * (2 * CHUNKS) + (2 * c + u + 1))
                    for t in (2 * u, 2 * u + 1):
                        last = nc.vector.scalar_tensor_tensor(y_out[:, c % 2, t, :], bank[6 + u][0:TM, (t % 2) * D:(t % 2) * D + D],
                                                              weight[:, c, t:t + 1], zw[:, c, t, :], ALU.mult, ALU.add)
                last.then_inc(y_ready, 1)

            def expert(e, first, start):
                step.turn(start)
                z_chunk(e, 0)
                for r in range(2 * HT):
                    v.wait_ge(ew_high, e * (3 * HT) + (r + 1))
                    nc.vector.tensor_tensor(up_l[:, r, :], bank[r % 4][:, 0:128], up_h[:, r, :].bitcast(F32), ALU.subtract)
                    nc.vector.tensor_tensor(up_hl[64:128, r, :], bank[r % 4][64:128, 128:256], up_hl[64:128, r, :].bitcast(F32),
                                            ALU.subtract).then_inc(ew_low, 1)
                for h in range(HT):
                    v.wait_ge(ew_high, e * (3 * HT) + (2 * HT + h + 1))
                    nc.vector.tensor_tensor(down_l[:, h, :], bank[h][:, 0:D], down_h[:, h, :].bitcast(F32), ALU.subtract).then_inc(ew_low, 1)
                zt_l(e, 0)
                for c in range(CHUNKS):
                    if c + 1 < CHUNKS:
                        z_chunk(e, c + 1)
                        zt_l(e, c + 1)
                    for h in range(HT):
                        n = c * 2 * HT + 2 * h + 1
                        v.wait_ge(gu_full, e * (2 * HT * CHUNKS) + (n + 1))
                        v.wait_ge(silu_ready, e * (HT * CHUNKS) + (c * HT + h + 1))
                        nc.vector.tensor_tensor(act[:, c % 2, h, :], silu[:, h, :], bank[n % 4][:, 0:CN], ALU.mult).then_inc(act_ready, 1)
                    if c:
                        y_evac3(e, c - 1, first)
                y_evac3(e, CHUNKS - 1, first)
                return step.n

            n = expert(0, True, at)
            with v.Fori(1, E) as e:
                expert(e, False, (e - 1) * n + (at + n))

        @block.tensor
        def _(pe):
            def passes(dst, pairs):
                for n, (lhs, rhs) in enumerate(pairs):
                    last = nc.tensor.matmul(dst, lhs, rhs, start=(n == 0), stop=(n == len(pairs) - 1))
                return last

            pe.wait_ge(const_ready, 9)
            pe.wait_ge(image_args_loaded, 16 * (5 + SEQS))
            for k in range(KT):
                if k >= 2:
                    pe.wait_ge(pt_low, k - 1)
                nc.tensor.transpose(bank[k % 2][:, 0:128], tok_raw[:, 0, 128 * k:128 * k + 128], ident[:])
                nc.tensor.transpose(bank[k % 2][:, 128:D], tok_raw[0:D1, 1, 128 * k:128 * k + 128], ident[0:D1, 0:D1]).then_inc(pt_full, 1)
            for g in range(RT * GRID):
                r, gw = g // GRID, g % GRID
                if gw == 0:
                    pe.wait_ge(regrouped, r + 1)
                for half in range(2):
                    n = 2 * g + half
                    if n >= 2:
                        pe.wait_ge(pt_low, KT + n - 1)
                    for k in range(3):
                        kk = 3 * half + k
                        last = nc.tensor.transpose(bank[2 + n % 2][:, k * IR:(k + 1) * IR],
                                                   img_grouped[:, gw, 128 * kk:128 * kk + 128], ident[0:IR, 0:IR])
                    last.then_inc(pt_full, 1)
                if g:
                    pe.wait_ge(emb_free, g)
                pe.wait_ge(pt_low, KT + 2 * g + 2)
                pairs = []
                for k in range(KT):
                    pairs += [(pt_h[:, k, :], tok_h[:, k, :]), (pt_h[:, k, :], tok_l[:, k, :]), (pt_l[:, k, :], tok_h[:, k, :])]
                passes(bank[4][0:IR, 0:D], pairs).then_inc(emb_full, 1)
            pe.wait_ge(emb_stored, 16 * (B + 1))
            nc.tensor.transpose(bank[0][0:1, 0:1], ident[0:1, 0:1], ident[0:1, 0:1]).then_inc(stage1_done, 1)
            pe.wait_ge(stage1_done, 4)
            pe.wait_ge(const_loaded, 16 * 6)

            def use(part, i, name):
                here = uses.lists[part].index(name)
                back = here - GB
                if back >= 0:
                    old_part, old = part, uses.lists[part][back]
                    old_turn = i
                elif part == "before":
                    return ring_bank(part, name)
                else:
                    old_part = {"first": "before", "mid": "mid", "last": "mid", "after": "last"}[part]
                    old = uses.lists[old_part][back]
                    old_turn = {"before": 0, "mid": i - 1 if part != "last" else LAST - 1, "last": LAST}[old_part]
                e = "d" if "d" in uses.who(old) else "a"
                c = uses.count(e)
                seq = [n for n in uses.lists[old_part] if e in uses.who(n)]
                if part == "mid" and back < 0:
                    value = c.start(i) - (len(seq) - seq.index(old) - 1)
                elif old_part == "before":
                    value = seq.index(old) + 1
                else:
                    value = position(old_part, old_turn, old, e)
                pe.wait_ge(ring_dve if e == "d" else ring_act, value)
                return ring_bank(part, name)

            def x_side(t=None):
                cols = slice(0, SP) if t is None else slice(t * T0, t * T0 + (T1 if t else T0))
                return xt_h[:, 0, cols], xt_l[:, cols], xt_h[:, 1, cols], xt_l1[:, cols]

            def w_side(cols):
                return wq_h[:, cols], wq_l[:, cols], wq_hl[:, cols], wq_hb[:, cols]

            def products(x_, w_):
                (xh, xl, xhh, xl1), (wh, wl, whl, whb) = x_, w_
                return [(xh, wh), (xh, wl), (xl, wh), (xhh, whl), (xl1, whb)]

            def turned(pairs):
                return [(b_, a_) for a_, b_ in pairs]

            def qk(i, part, kind, n):
                dst = use(part, i, (kind, n))
                first = (0 if kind == "q" else W) + 2 * n * D
                for k in range(3):
                    cols = slice(first + 128 * k, first + 128 * k + 128)
                    last = passes(dst[:, k * SP:(k + 1) * SP], turned(products(x_side(), w_side(cols))))
                last.then_inc(ring_full, 1)

            def xt(i, part, b):
                dst = use(part, i, ("xt", 0))
                pe.wait_ge(x_ready, 2 * b + 2)
                for t in range(2):
                    m = T1 if t else T0
                    for k in range(2):
                        last = nc.tensor.transpose(dst[:, k * S + t * T0:k * S + t * T0 + m],
                                                   x_norm[0:m, t, 128 * k:128 * k + 128], ident[0:m, 0:m])
                last.then_inc(ring_full, 1)

            def v_product(i, part, n):
                dst = use(part, i, ("v", n))
                if n == 0:
                    pe.wait_ge(ring_dve, position(part, i, ("xt", 0), "d"))
                t, c = n // 4, n % 4
                m = T1 if t else T0
                cols = slice(2 * W + c * 2 * D, 2 * W + (c + 1) * 2 * D)
                passes(dst[0:m, 0:2 * D], products(x_side(t), w_side(cols))).then_inc(ring_full, 1)

            def zt(part, i, b):
                dst = use(part, i, ("zt", 0))
                pe.wait_ge(z_ready, b + 1)
                for t in range(2):
                    m = T1 if t else T0
                    nc.tensor.transpose(dst[:, t * T0:t * T0 + m], z_row[0:m, t, 0:128], ident[0:m, 0:m])
                    last = nc.tensor.transpose(dst[0:D1, S + t * T0:S + t * T0 + m], z_row[0:m, t, 128:D], ident[0:m, 0:m])
                last.then_inc(ring_full, 1)

            def gate(part, i, b):
                dst = use(part, i, ("log", 0))
                pe.wait_ge(ring_act, position(part, i, ("zt", 0), "a"))
                for t in range(2):
                    m = T1 if t else T0
                    cols = slice(t * T0, t * T0 + m)
                    last = passes(dst[0:m, t * E:(t + 1) * E], [(z_t[:, 0, cols], gate_t[:, 0, :]), (z_t[0:D1, 1, cols], gate_t[0:D1, 1, :])])
                last.then_inc(ring_full, 1)

            def counting(part, i, b):
                dst = use(part, i, ("cnt", 0))
                pe.wait_ge(chosen, b + 1)
                m0, m1 = rt[:, 7, 0, :], rt[:, 7, 1, :]
                passes(dst[0:T0, 0:E], [(earlier[:], m0)])
                passes(dst[0:T0, E:2 * E], [(ones[:], m0), (earlier[:], m1)])
                passes(dst[0:T0, 2 * E:3 * E], [(ones[:], m0), (ones[:], m1)]).then_inc(ring_full, 1)

            def scores(i, g):
                if g < 2:
                    if not (isinstance(i, int) and i == 0):
                        pe.wait_ge(exp_done, i * HEADS + (g - 1))
                else:
                    pe.wait_ge(exp_done, i * HEADS + (g - 1))
                dst = score_bank[g % 2]
                keys = slice(S * g, S * g + SP)
                for t in range(2):
                    rows = slice(S * g + T0 * t, S * g + T0 * (t + 1))
                    last = passes(dst[0:T0, t * SP:(t + 1) * SP], [
                        (q_h[:, 0, rows], k_h[:, keys]), (q_h[:, 0, rows], k_l[:, keys]), (q_l[:, rows], k_h[:, keys]),
                        (q_h[:, 1, rows], k_hl[:, keys]), (q_l1[:, rows], k_hl[0:64, keys])])
                last.then_inc(scores_full, 1)

            def probs_turn(i, g):
                if not (isinstance(i, int) and i == 0 and g == 0):
                    pe.wait_ge(probs_t_low, i * HEADS + g)
                pe.wait_ge(probs_ready, i * HEADS + (g + 1))
                for kt in range(2):
                    for t in range(2):
                        last = nc.tensor.transpose(probs_t_bank[0:T0, kt * SP + t * T0:kt * SP + (t + 1) * T0],
                                                   probs[:, g % 3, t, kt * T0:(kt + 1) * T0], ident[0:T0, 0:T0])
                last.then_inc(probs_t_full, 1)

            def pv(i, part, g):
                dst = use(part, i, ("pv", g))
                pe.wait_ge(probs_t_low, i * HEADS + (g + 1))
                if g % 2 == 0:
                    pe.wait_ge(v_ready, i * HALF + (g // 2 + 1))
                for d0, d1, col in ((0, 128, 0), (128, D, SP)):
                    pairs = []
                    for kt in range(2):
                        ph, pl = pt2_h[:, g % 2, kt, :], pt2_l[:, g % 2, kt, :]
                        vh, vl = v_h[:, g, kt, d0:d1], v_l[:, g, kt, d0:d1]
                        pairs += [(vh, ph), (vh, pl), (vl, ph)]
                    last = passes(dst[0:d1 - d0, col:col + SP], pairs)
                last.then_inc(ring_full, 1)

            def project(i, part):
                pe.wait_ge(ring_dve, position(part, i, ("pv", HEADS - 1), "d"))
                for t in range(2):
                    dst = use(part, i, ("y", t))
                    m = T1 if t else T0
                    pairs = []
                    for j in range(HEADS):
                        first = HEADS * T0 * t + j
                        rows = slice(first, first + HEADS * (m - 1) + 1, HEADS)
                        oh, ol, ohh, ol1 = o_h[:, 0, rows], o_l[:, rows], o_h[:, 1, rows], o_l1[:, rows]
                        pairs += [(oh, wp_h[:, j, :]), (oh, wp_l[:, j, :]), (ol, wp_h[:, j, :]),
                                  (ohh, wp_hl[:, j, :]), (ol1, wp_hl[0:64, j, :])]
                    passes(dst[0:m, 0:D], pairs).then_inc(ring_full, 1)

            def turn(i, part):
                nxt = part != "last"
                pe.wait_ge(q_doubled, i * 16 + 16)
                if part == "first":
                    pe.wait_ge(ring_dve, position("before", 0, ("k", 3), "d"))
                else:
                    pe.wait_ge(ring_dve, uses.count("d").start(i) - 1)
                for s in range(HEADS + 3):
                    if s < HEADS:
                        scores(i, s)
                    if 0 <= s - 2 < HEADS:
                        probs_turn(i, s - 2)
                    if s == COUNT_STEP and part != "first":
                        counting(part, i, i - 1)
                    if s == XT_STEP and nxt:
                        xt(i, part, i + 1)
                    if 0 <= s - 3:
                        pv(i, part, s - 3)
                    for n in V_CHUNKS[s - HEADS] if nxt and s >= HEADS else []:
                        v_product(i, part, n)
                project(i, part)
                if nxt:
                    for n in range(4):
                        qk(i, part, "q", n)
                    for n in range(4):
                        qk(i, part, "k", n)
                zt(part, i, i)
                if nxt:
                    v_product(i, part, 4)
                gate(part, i, i)
                for n in range(5, 8) if nxt else []:
                    v_product(i, part, n)

            xt(0, "before", 0)
            for n in range(8):
                v_product(0, "before", n)
            for kind in "qk":
                for n in range(4):
                    qk(0, "before", kind, n)
            turn(0, "first")
            with pe.Fori(1, LAST) as i:
                turn(i, "mid")
            turn(LAST, "last")
            counting("after", LAST, LAST)
            pe.wait_ge(rows_scattered, 64 * B)
            nc.tensor.transpose(bank[0][0:1, 0:1], ident[0:1, 0:1], ident[0:1, 0:1]).then_inc(stage2_done, 1)
            pe.wait_ge(stage2_done, 4)

            def zs_turn(e, c, first):
                pe.wait_ge(z_scaled, e * CHUNKS + (c + 1))
                if not (first and c == 0):
                    pe.wait_ge(zt_low, e * CHUNKS + c)
                for k in range(2):
                    for t in range(TILES):
                        last = nc.tensor.transpose(bank[4 + k][:, t * TM:(t + 1) * TM], zs[:, c % 2, t, 128 * k:128 * k + 128],
                                                   ident[0:TM, 0:TM])
                last.then_inc(zt_full, 1)

            def gate_up(e, c, first):
                pe.wait_ge(zt_low, e * CHUNKS + (c + 1))
                b = c % 2
                for n in range(2 * HT):
                    r = n // 2 + HT * (n % 2)
                    if c or n >= 4:
                        pe.wait_ge(act_ready, e * (HT * CHUNKS) + (c * HT + n // 2 - 1))
                    last = passes(bank[(c * 2 * HT + n) % 4][:, 0:CN], [
                        (up_h[:, r, :], zst_h[:, b, 0, :]), (up_l[:, r, :], zst_h[:, b, 0, :]), (up_h[:, r, :], zst_l[:, b, 0, :]),
                        (up_hl[:, r, :], zst_h[:, b, 1, :]), (up_hl[0:64, r, :], zst_l[0:64, b, 1, :])])
                    last.then_inc(gu_full, 1)

            def down(e, c, first):
                pe.wait_ge(act_low, e * (HT * CHUNKS) + HT * (c + 1))
                if not (first and c == 0):
                    pe.wait_ge(y_ready, e * CHUNKS + c)
                for t in range(TILES):
                    rows = slice(t * TM, (t + 1) * TM)
                    pairs = []
                    for h in range(HT):
                        ah, al = act_h[:, c % 2, h, rows], act_l[:, c % 2, h, rows]
                        pairs += [(ah, down_h[:, h, :]), (ah, down_l[:, h, :]), (al, down_h[:, h, :])]
                    last = passes(bank[6 + t // 2][0:TM, (t % 2) * D:(t % 2) * D + D], pairs)
                    if t % 2:
                        last.then_inc(y_full, 1)

            def expert(e, first):
                pe.wait_ge(ew_loaded, e * 64 + 64)
                if not first:
                    pe.wait_ge(act_ready, e * (HT * CHUNKS))
                for r in range(2 * HT):
                    if r >= 4:
                        pe.wait_ge(ew_low, e * (3 * HT) + (r - 3))
                    nc.tensor.transpose(bank[r % 4][:, 0:128], up_raw[:, r, 0:128], ident[:])
                    nc.tensor.transpose(bank[r % 4][:, 128:256], up_raw[:, r, 128:256], ident[:]).then_inc(ew_full, 1)
                for h in range(HT):
                    pe.wait_ge(ew_low, e * (3 * HT) + (2 * HT + h - 3))
                    cols = slice(128 * h, 128 * h + 128)
                    nc.tensor.transpose(bank[h][:, 0:128], down_raw[:, 0, cols], ident[:])
                    nc.tensor.transpose(bank[h][:, 128:D], down_raw[0:D1, 1, cols], ident[0:D1, 0:D1]).then_inc(ew_full, 1)
                zs_turn(e, 0, first)
                pe.wait_ge(ew_low, e * (3 * HT) + 3 * HT)
                for c in range(CHUNKS):
                    if c + 1 < CHUNKS:
                        zs_turn(e, c + 1, False)
                    gate_up(e, c, first)
                    if c:
                        down(e, c - 1, first)
                down(e, CHUNKS - 1, first)

            expert(0, True)
            with pe.Fori(1, E) as e:
                expert(e, False)
    return SLOTS


_INS = ["x", "txt", "L0_tok_W", "L0_tok_b", "L0_tok_cls_tok", "L0_tok_pos_emb", "L0_attn_W_qkv", "L0_attn_b_qkv",
        "L0_attn_W_proj", "L0_attn_b_proj", "L0_ffn_gate_w", "L0_ffn_w13", "L0_ffn_w2", "L0_ffn_norm_w"]


def slots_of(tokens, experts):
    capacity = -(-5 * TOP_K * tokens // (4 * experts))
    tile = -(-capacity // (CHUNKS * TILES))
    return CHUNKS * TILES * (tile + tile % 2)


def kernel(**inputs):
    import numpy as np
    import concourse.bacc as bacc
    from concourse.bass_utils import run_bass_kernel_spmd

    nc = bacc.Bacc("TRN2", target_bir_lowering=False, num_devices=1)
    arrays, args = {}, []
    for name in _INS:
        a = np.ascontiguousarray(inputs[name])
        arrays[f"in_{name}"] = a
        args.append(nc.dram_tensor(f"in_{name}", a.shape, mybir.dt.from_np(a.dtype), kind="ExternalInput").ap())
    batch, text, width = arrays["in_txt"].shape
    grid = arrays["in_x"].shape[2] // PATCH
    tokens = batch * (grid * grid + 1 + text)
    rows = tokens + slots_of(tokens, arrays["in_L0_ffn_gate_w"].shape[0])
    out = nc.dram_tensor("out_rows", (rows, width), F32, kind="ExternalOutput").ap()
    build(nc, *args, out)
    r = run_bass_kernel_spmd(nc, [arrays], core_ids=[0])
    return r.results[0]["out_rows"][:tokens].reshape(batch, -1, width)
```

```python
from contextlib import ExitStack

import concourse.bass as bass
from concourse import mybir

F32 = mybir.dt.float32
F32R = mybir.dt.float32r
I32 = mybir.dt.int32
ALU = mybir.AluOpType
ACT = mybir.ActivationFunctionType
AXIS = mybir.AxisListType

HEADS = 8
PATCH = 16
HIDDEN = 512
TOP_K = 2
TICKS = 64
CHUNKS = 4
TILES = 4
COUNT_STEP = 8
XT_STEP = 8
V_CHUNKS = ((0,), (1,), (2, 3))
LN_EPS = 1e-5
RMS_EPS = 1e-6


class Count:

    def __init__(self, before, first, each):
        self.before, self.first, self.each = before, first, each

    def start(self, turn):
        if isinstance(turn, int) and turn == 0:
            return self.before
        return (turn - 1) * self.each + (self.before + self.first)


class Uses:

    WHO = {"q": "ad", "k": "ad", "zt": "a", "xt": "ad", "log": "d", "cnt": "d", "pv": "ad", "y": "d", "v": "a"}

    def __init__(self, banks):
        pv = [("pv", g) for g in range(HEADS)]
        q = [("q", n) for n in range(4)]
        k = [("k", n) for n in range(4)]
        v = [("v", n) for n in range(8)]
        xt, y = [("xt", 0)], [("y", 0), ("y", 1)]
        turn = xt + [pv[5], v[0], pv[6], v[1], pv[7]] + v[2:4] + y + q + k + [("zt", 0), v[4], v[5], ("log", 0)] + v[6:]
        self.lists = {
            "before": xt + v + q + k,
            "first": pv[:5] + turn,
            "mid": pv[:5] + [("cnt", 0)] + turn,
            "last": pv[:5] + [("cnt", 0)] + pv[5:] + y + [("zt", 0), ("log", 0)],
            "after": [("cnt", 0)],
        }
        self.banks = banks
        assert len(self.lists["mid"]) % banks == 0

    @staticmethod
    def who(name):
        return Uses.WHO[name[0]]

    def size(self, part, e=None):
        return sum(1 for n in self.lists[part] if e is None or e in self.who(n))

    def count(self, e):
        return Count(self.size("before", e), self.size("first", e), self.size("mid", e))


def split(x):
    return 128, x - 128


def build(nc, x, txt, tok_w, tok_b, cls_tok, pos_emb, w_qkv, b_qkv, w_proj, b_proj, gate_w, w13, w2, norm_w, out):
    B, C, IMG, _ = x.shape
    TXT, D = txt.shape[1:]
    GRID = IMG // PATCH
    IMG_T = GRID * GRID + 1
    S = IMG_T + TXT
    N = B * S
    E = gate_w.shape[0]
    CAP = -(-5 * TOP_K * N // (4 * E))
    D0, D1 = split(D)
    T0 = (S + 1) // 2
    T1 = S - T0
    HALF = HEADS // 2
    assert HALF * S <= HEADS * T0
    SP = S + 1
    ROWS = S * HEADS
    W = HEADS * D
    ROW = D + 1 + E + 1
    TM = -(-CAP // (CHUNKS * TILES))
    TM += TM % 2
    SLOTS = CHUNKS * TILES * TM
    CN = TILES * TM
    HT = HIDDEN // 128
    ADDED = 16 * TILES * CHUNKS // 2
    KP = C * PATCH * PATCH
    KT = KP // 128
    SEQS = min(B, 16)
    RT = B // SEQS
    IR = SEQS * GRID
    PY = PATCH * IMG
    LAST = B - 1
    GB = 5
    uses = Uses(GB)

    images_rows = nc.dram_tensor("images_rows", (B, IMG_T, D), F32, kind="Internal").ap()
    v_rows = nc.dram_tensor("v_rows", (ROWS, D), F32, kind="Internal").ap()
    slot_rows = nc.dram_tensor("slot_rows", (E * SLOTS + 4 * T0, ROW), F32, kind="Internal").ap()

    persistent = ExitStack()
    with persistent:
        def sb(name, shape, dt=F32, at=None):
            return (at or persistent).enter_context(nc.sbuf_tensor(name, shape, dt))

        def sem(name):
            return persistent.enter_context(nc.semaphore(name))

        bank = [persistent.enter_context(nc.psum_tensor(f"bank{n}", [128, 512], F32)) for n in range(8)]
        ring = bank[:GB]
        score_bank = bank[5:7]
        probs_t_bank = bank[7]

        ident = sb("ident", [128, 128])
        earlier = sb("earlier", [T0, T0])
        earlier_r = sb("earlier_r", [T0, T0], F32R)
        ones_r = sb("ones_r", [T0, T0], F32R)
        expert_no = sb("expert_no", [T0, 2, E])
        slot_base = sb("slot_base", [T0, 2, E])
        dump_row = sb("dump_row", [T0, 2, TOP_K])
        expert_of_real = sb("expert_of_real", [T0, 2, E])
        minus_half = sb("minus_half", [128, 4])
        tick = sb("tick", [1, 3 * TICKS])
        norm_cols = sb("norm_cols", [128, 2, E])
        tile_first = sb("tile_first", [TM, CHUNKS, TILES])
        empty_row = sb("empty_row", [TM, ROW])

        const_made = sem("const_made")
        const_ready = sem("const_ready")
        const_loaded = sem("const_loaded")
        slots_cleared = sem("slots_cleared")
        w_loaded = [sem(f"w_loaded{n}") for n in range(4)]
        w_high = sem("w_high")
        w_low = sem("w_low")
        w_rows_cleared = sem("w_rows_cleared")
        bias_loaded = sem("bias_loaded")
        bias_high = sem("bias_high")
        bias_low = sem("bias_low")
        bias_placed = sem("bias_placed")
        tok_loaded = sem("tok_loaded")
        images_loaded = sem("images_loaded")
        image_args_loaded = sem("image_args_loaded")
        regrouped = sem("regrouped")
        token_bias = sem("token_bias")
        tok_full = sem("tok_full")
        tok_high = sem("tok_high")
        tok_low = sem("tok_low")
        pt_full = sem("pt_full")
        pt_high = sem("pt_high")
        pt_low = sem("pt_low")
        emb_full = sem("emb_full")
        emb_ready = sem("emb_ready")
        emb_stored = sem("emb_stored")
        stage1_done = sem("stage1_done")

        attention = ExitStack()

        def sa(name, shape, dt=F32):
            return sb(name, shape, dt, attention)

        wq_h = sa("wq_h", [128, 3 * W], F32R)
        wq_l = sa("wq_l", [128, 3 * W], F32R)
        wq_hl = sa("wq_hl", [128, 3 * W], F32R)
        wq_hb = sa("wq_hb", [128, 3 * W], F32R)
        wp_h = sa("wp_h", [128, HEADS, D], F32R)
        wp_l = sa("wp_l", [128, HEADS, D], F32R)
        wp_hl = sa("wp_hl", [128, HEADS, D], F32R)
        proj_bias = sa("proj_bias", [T0, D])
        gate_t = sa("gate_t", [128, 2, E])

        stage1 = ExitStack()

        def s1(name, shape, dt=F32):
            return sb(name, shape, dt, stage1)

        w_raw = [s1(f"w_raw{n}", [128, 2, W]) for n in range(2)]
        img = s1("img", [IR, C, PY])
        img_grouped = s1("img_grouped", [IR, GRID, KP])
        tok_raw = s1("tok_raw", [128, 2, KP])
        tok_h = s1("tok_h", [128, KT, D], F32R)
        tok_l = s1("tok_l", [128, KT, D], F32R)
        pt_h = s1("pt_h", [128, 2, KT, IR], F32R)
        pt_l = s1("pt_l", [128, 2, KT, IR], F32R)
        pos = s1("pos", [IR, GRID * D])
        tok_bias = s1("tok_bias", [IR, D])
        emb = s1("emb", [IR, GRID, D])
        cls = s1("cls", [B, D])
        cls_pos = s1("cls_pos", [B, D])
        bias_raw = s1("bias_raw", [W // 128, 2 * D])
        bias_h = s1("bias_h", [W // 128, 2 * D], F32R)
        bias_l = s1("bias_l", [W // 128, 2 * D], F32R)
        stage1.close()

        q_h = sa("q_h", [128, 2, ROWS + 1], F32R)
        q_l = sa("q_l", [128, ROWS + 1], F32R)
        q_l1 = sa("q_l1", [64, ROWS + 1], F32R)
        k_h = sa("k_h", [128, ROWS + 1], F32R)
        k_l = sa("k_l", [128, ROWS + 1], F32R)
        k_hl = sa("k_hl", [128, ROWS + 1], F32R)
        o_h = sa("o_h", [128, 2, ROWS], F32R)
        o_l = sa("o_l", [128, ROWS], F32R)
        o_l1 = sa("o_l1", [64, ROWS], F32R)
        v_h = sa("v_h", [T0, HEADS, 2, D], F32R)
        v_l = sa("v_l", [T0, HEADS, 2, D], F32R)
        v_out = sa("v_out", [T0, 4, 2 * D])
        probs = sa("probs", [T0, 3, 2, SP])
        pt2_h = sa("pt2_h", [T0, 2, 2, SP], F32R)
        pt2_l = sa("pt2_l", [T0, 2, 2, SP], F32R)
        xt_h = sa("xt_h", [128, 2, SP], F32R)
        xt_l = sa("xt_l", [128, SP], F32R)
        xt_l1 = sa("xt_l1", [128, SP], F32R)
        h_in = sa("h_in", [T0, 2, D])
        h_res = sa("h_res", [T0, 2, D])
        x_norm = sa("x_norm", [T0, 2, D + D1])
        h_mid = sa("h_mid", [T0, 2, D])
        z_row = sa("z_row", [T0, 2, ROW])
        z_t = sa("z_t", [128, 2, S])
        neg_max = sa("neg_max", [T0, HEADS, 2])
        row_sum = sa("row_sum", [T0, HEADS, 2])
        row_inv = sa("row_inv", [T0, HEADS, 2])
        stats = sa("stats", [T0, 2, 2, 6])
        neg_mean = sa("neg_mean", [T0, 2])
        mean_var = sa("mean_var", [T0, 2, 2, 2])
        rs = sa("rs", [T0, 2, 4, 2])
        logits = sa("logits", [T0, 2, E])
        square = sa("square", [T0, D])
        rms = sa("rms", [T0, 5, 2])
        rt = sa("rt", [T0, 12, 2, E])
        picks = sa("picks", [T0, 2, E], F32R)
        r1 = sa("r1", [T0, 8, 2, 1])
        counts = sa("counts", [T0, 3, E])
        base = sa("base", [T0, E])
        slot_of = sa("slot_of", [T0, 2, TOP_K, E])
        slot_f = sa("slot_f", [T0, 2, TOP_K, 1])
        slot_i = sa("slot_i", [T0, 2, TOP_K], I32)
        attention.close()

        experts = ExitStack()

        def se(name, shape, dt=F32):
            return sb(name, shape, dt, experts)

        up_raw = se("up_raw", [128, 2 * HT, D + D1])
        down_raw = se("down_raw", [128, 2, HIDDEN])
        up_w = se("up_w", [128, 2 * HT, 2, 128], F32R)
        up_l = se("up_l", [128, 2 * HT, 128], F32R)
        down_h = se("down_h", [128, HT, D], F32R)
        down_l = se("down_l", [128, HT, D], F32R)
        zs_in = se("zs_in", [TM, CHUNKS, TILES, ROW])
        zs = se("zs", [TM, 2, TILES, D + D1])
        zst_h = se("zst_h", [128, 2, 2, CN], F32R)
        zst_l = se("zst_l", [128, 2, 2, CN], F32R)
        silu = se("silu", [128, HT, CN])
        act = se("act", [128, 2, HT, CN])
        act_h = se("act_h", [128, 2, HT, CN], F32R)
        act_l = se("act_l", [128, 2, HT, CN], F32R)
        y_out = se("y_out", [TM, 2, TILES, D])
        token_f = se("token_f", [TM, CHUNKS, TILES])
        token_i = se("token_i", [TM, CHUNKS, TILES], I32)
        experts.close()

        pads_ready = sem("pads_ready")
        h_loaded = sem("h_loaded")
        res_loaded = sem("res_loaded")
        res_biased = sem("res_biased")
        ln1_stats = sem("ln1_stats")
        x_ready = sem("x_ready")
        ring_full = sem("ring_full")
        ring_act = sem("ring_act")
        ring_dve = sem("ring_dve")
        q_doubled = sem("q_doubled")
        v_stored = [sem(f"v_stored{n}") for n in range(4)]
        v_loaded = [sem(f"v_loaded{n}") for n in range(2)]
        v_high = sem("v_high")
        v_ready = sem("v_ready")
        scores_full = sem("scores_full")
        max_ready = sem("max_ready")
        exp_done = sem("exp_done")
        inv_ready = sem("inv_ready")
        probs_ready = sem("probs_ready")
        probs_t_full = sem("probs_t_full")
        probs_t_high = sem("probs_t_high")
        probs_t_low = sem("probs_t_low")
        h_mid_ready = sem("h_mid_ready")
        h_mid_stored = sem("h_mid_stored")
        ln2_stats = sem("ln2_stats")
        ln2_rs = sem("ln2_rs")
        z_ready = sem("z_ready")
        z_squares = sem("z_squares")
        route_sub = sem("route_sub")
        route_exp = sem("route_exp")
        chosen = sem("chosen")
        counts_ready = sem("counts_ready")
        slots_ranked = sem("slots_ranked")
        slots_ready = sem("slots_ready")
        rows_scattered = sem("rows_scattered")
        dve_step = sem("dve_step")
        stats_step = [sem(f"stats_step{n}") for n in range(2)]
        pool_step = sem("pool_step")
        stage2_done = sem("stage2_done")

        ew_loaded = sem("ew_loaded")
        ew_full = sem("ew_full")
        ew_high = sem("ew_high")
        ew_low = sem("ew_low")
        z_loaded = [sem(f"z_loaded{n}") for n in range(CHUNKS)]
        empty_marked = sem("empty_marked")
        tokens_read = sem("tokens_read")
        z_scaled = sem("z_scaled")
        z_weighted = sem("z_weighted")
        zt_full = sem("zt_full")
        zt_high = sem("zt_high")
        zt_low = sem("zt_low")
        gu_full = sem("gu_full")
        silu_ready = sem("silu_ready")
        act_ready = sem("act_ready")
        act_high = sem("act_high")
        act_low = sem("act_low")
        y_full = sem("y_full")
        y_ready = sem("y_ready")
        y_added = [sem(f"y_added{n}") for n in range(2)]

        block = persistent.enter_context(nc.Block())

        def load_tokens(eng, dst, b, signal):
            eng.dma_start(dst[0:IMG_T, 0, :], images_rows[b]).then_inc(signal, 16)
            eng.dma_start(dst[IMG_T:T0, 0, :], txt[b, 0:T0 - IMG_T, :]).then_inc(signal, 16)
            eng.dma_start(dst[0:T1, 1, :], txt[b, T0 - IMG_T:TXT, :]).then_inc(signal, 16)

        def position(part, turn, name, e=None):
            seq = [n for n in uses.lists[part] if e is None or e in uses.who(n)]
            c = uses.count(e)
            begin = {"before": 0, "after": None}.get(part, c.start(turn))
            if part == "after":
                begin = c.start(LAST) + uses.size("last", e)
            return begin + (seq.index(name) + 1)

        def part_of(turn):
            if not isinstance(turn, int):
                return "mid"
            return "first" if turn == 0 else "last" if turn == LAST else "mid"

        def ring_bank(part, name):
            begin = {"before": 0, "first": uses.size("before")}.get(part)
            if begin is None:
                begin = uses.size("before") + uses.size("first")
            if part == "after":
                begin += uses.size("last")
            return ring[(begin + uses.lists[part].index(name)) % GB]

        def carried(eng, row, carrier):
            cell = 1

            def wait(signal, value):
                nonlocal cell
                eng.wait_ge(signal, value)
                if not isinstance(value, int):
                    at = TICKS * row + cell
                    carrier(tick[0:1, at:at + 1])
                    cell += 1
            return wait

        def step_counter(eng, signal, wait=None):
            class Steps:
                start, n = 0, 0

                def turn(self, start):
                    self.start, self.n = start, 0

                def __call__(self, ins, carry=False):
                    self.n += 1
                    ins.then_inc(signal, 1)
                    (wait if wait and carry else eng.wait_ge)(signal, self.start + self.n)
            return Steps()

        @block.sync
        def _(sp):
            def load_w(dst, src, third, signal):
                if third == 2:
                    sp.dma_start(dst, src).then_inc(signal, 16)
                    return
                to = dst.rearrange("p (n c) -> p n c", c=2 * D)
                of = src.rearrange("p (n k d) -> p n k d", k=2, d=D)
                for k in range(2):
                    sp.dma_start(to[:, :, 128 * k:128 * k + 128], of[:, :, k, 0:128]).then_inc(signal, 16)
                    sp.dma_start(to[:, :, 256 + D1 * k:256 + D1 * k + D1], of[:, :, k, 128:D]).then_inc(signal, 16)

            sp.dma_start(tok_raw[:, 0, :], tok_w[0:128, :]).then_inc(tok_loaded, 16)
            sp.dma_start(tok_raw[0:D1, 1, :], tok_w[128:D, :]).then_inc(tok_loaded, 16)

            def load_images(r):
                src = x[r * SEQS:(r + 1) * SEQS].rearrange("b c (g y) w -> b g c (y w)", y=PATCH)
                for s in range(SEQS):
                    sp.dma_start(img[s * GRID:(s + 1) * GRID, :, :], src[s]).then_inc(images_loaded, 16)

            def load_third(n):
                raw = w_raw[n % 2]
                cols = slice(n * W, (n + 1) * W)
                load_w(raw[:, 0, :], w_qkv[0:128, cols], n, w_loaded[n])
                for half in range(2):
                    load_w(raw[half * D1:(half + 1) * D1, 1, :], w_qkv[128:D, cols], n, w_loaded[n])

            def store_images(r):
                sp.wait_ge(emb_ready, GRID * (r + 1))
                for s in range(SEQS):
                    dst = images_rows[r * SEQS + s, 1:IMG_T, :].rearrange("(h w) d -> h w d", w=GRID)
                    sp.dma_start(dst, emb[s * GRID:(s + 1) * GRID, :, :]).then_inc(emb_stored, 16)

            load_images(0)
            load_third(0)
            sp.dma_start(tok_bias[:], tok_b.rearrange("(a d) -> a d", a=1).to_broadcast([IR, D])).then_inc(image_args_loaded, 16)
            pos_rows = pos_emb[0, 1:IMG_T, :].rearrange("(h w) d -> h (w d)", w=GRID)
            for s in range(SEQS):
                sp.dma_start(pos[s * GRID:(s + 1) * GRID, :], pos_rows).then_inc(image_args_loaded, 16)
            sp.dma_start(cls[:], cls_tok[0].to_broadcast([B, D])).then_inc(image_args_loaded, 16)
            sp.dma_start(cls_pos[:], pos_emb[0, 0:1, :].to_broadcast([B, D])).then_inc(image_args_loaded, 16)
            load_third(1)
            for r in range(1, RT):
                sp.wait_ge(regrouped, GRID * r)
                load_images(r)
            for n in range(3):
                rows = W // (2 * D)
                load_w(bias_raw[n * rows:(n + 1) * rows, :], b_qkv[n * W:(n + 1) * W].rearrange("(n c) -> n c", c=2 * D), n, bias_loaded)
            sp.wait_ge(w_low, 1)
            load_third(2)
            sp.wait_ge(token_bias, 2)
            sp.dma_start(images_rows[:, 0, :], cls[:]).then_inc(emb_stored, 16)
            for r in range(RT - 1):
                store_images(r)
            sp.wait_ge(w_low, 2)
            wp = w_proj.rearrange("(h d) n -> d h n", d=D)
            as_heads = w_raw[1][:].rearrange("p a (h n) -> p a h n", h=HEADS)
            sp.dma_start(as_heads[:, 0], wp[0:128]).then_inc(w_loaded[3], 16)
            for half in range(2):
                sp.dma_start(as_heads[half * D1:(half + 1) * D1, 1], wp[128:D]).then_inc(w_loaded[3], 16)
            sp.wait_ge(w_rows_cleared, 1)
            sp.wait_ge(bias_high, 1)
            sp.dma_start(wq_hb[64:65, :].bitcast(F32), bias_h[:].bitcast(F32)).then_inc(bias_placed, 16)
            sp.wait_ge(bias_low, 1)
            sp.dma_start(wq_hb[96:97, :].bitcast(F32), bias_l[:].bitcast(F32)).then_inc(bias_placed, 16)
            sp.dma_start(proj_bias[:], b_proj.rearrange("(a d) -> a d", a=1).to_broadcast([T0, D])).then_inc(const_loaded, 16)
            with nc.allow_non_contiguous_dma(reason="few small columns"):
                gate_cols = gate_w.rearrange("e d -> d e")
                sp.dma_start(gate_t[:, 0, :], gate_cols[0:128, :]).then_inc(const_loaded, 16)
                sp.dma_start(gate_t[0:D1, 1, :], gate_cols[128:D, :]).then_inc(const_loaded, 16)
                norm_c = norm_w.rearrange("e d -> d e")
                sp.dma_start(norm_cols[:, 0, :], norm_c[0:128, :]).then_inc(const_loaded, 16)
                sp.dma_start(norm_cols[0:D1, 1, :], norm_c[128:D, :]).then_inc(const_loaded, 16)
                sp.dma_start(norm_cols[D1:2 * D1, 1, :], norm_c[128:D, :]).then_inc(const_loaded, 16)
            store_images(RT - 1)
            sp.wait_ge(emb_stored, 16 * (B + 1))
            sp.wait_ge(bias_placed, 32)

            def v_chunk(n):
                t, c = n // 4, n % 4
                rows = v_rows.rearrange("(s h) d -> s (h d)", h=HEADS)
                return rows[t * T0:t * T0 + (T1 if t else T0), c * 2 * D:(c + 1) * 2 * D]

            def store_v(b, turn, part, t):
                for n in range(4 * t, 4 * t + 4):
                    sp.wait_ge(ring_act, position(part, turn, ("v", n), "a"))
                    m = T1 if t else T0
                    sp.dma_start(v_chunk(n), v_out[0:m, n % 4, :]).then_inc(v_stored[n % 4], 16)

            def load_v(b, t):
                for stored in v_stored:
                    sp.wait_ge(stored, b * 32 + 16 * (t + 1))
                heads = v_rows.rearrange("(h s) d -> s h d", h=HEADS)[:, HALF * t:HALF * t + HALF, :]
                dst = v_l[:, HALF * t:HALF * t + HALF].bitcast(F32)
                sp.dma_start(dst[:, :, 0, :], heads[0:T0]).then_inc(v_loaded[t], 16)
                sp.dma_start(dst[0:T1, :, 1, :], heads[T0:S]).then_inc(v_loaded[t], 16)

            def double_q(turn, part):
                sp.wait_ge(ring_dve, position(part, turn, ("q", 3), "d"))
                sp.dma_start(q_h[64:128, 1, 0:ROWS].bitcast(F32), q_h[0:64, 1, 0:ROWS].bitcast(F32)).then_inc(q_doubled, 16)

            def next_h(i):
                sp.wait_ge(x_ready, 2 * i)
                load_tokens(sp, h_in, i, h_loaded)

            def turn(i, part, two_follow=True):
                if part != "first":
                    sp.wait_ge(h_mid_ready, i)
                load_v(i, 1)
                if part == "last":
                    sp.wait_ge(ring_full, position("mid", LAST - 1, ("v", 7)))
                    load_expert(0)
                load_tokens(sp, h_res, i, res_loaded)
                if part != "last":
                    for loaded in v_loaded:
                        sp.wait_ge(loaded, i * 32 + 32)
                    store_v(i + 1, i, part, 0)
                    sp.wait_ge(ring_full, position(part, i, ("pv", HALF - 1)))
                    load_v(i + 1, 0)
                    if two_follow:
                        next_h(i + 2)
                sp.wait_ge(h_mid_ready, i + 1)
                sp.dma_start(out[bass.ds(i * S, T0), :], h_mid[:, 0, :]).then_inc(h_mid_stored, 16)
                sp.dma_start(out[bass.ds(i * S + T0, T1), :], h_mid[0:T1, 1, :]).then_inc(h_mid_stored, 16)
                if part != "last":
                    double_q(i, part)
                    store_v(i + 1, i, part, 1)

            sp.wait_ge(stage1_done, 4)
            sp.wait_ge(pads_ready, 2)
            load_tokens(sp, h_in, 0, h_loaded)
            store_v(0, 0, "before", 0)
            load_v(0, 0)
            store_v(0, 0, "before", 1)
            double_q(0, "before")
            next_h(1)
            def load_expert(e):
                rows = w13[e].rearrange("(t p) d -> p t d", p=128)
                sp.dma_start(up_raw[:, :, 0:D], rows).then_inc(ew_loaded, 16)
                sp.dma_start(up_raw[:, :, D:], rows[:, :, 128:D]).then_inc(ew_loaded, 16)
                sp.dma_start(down_raw[:, 0, :], w2[e, 0:128, :]).then_inc(ew_loaded, 16)
                sp.dma_start(down_raw[0:D1, 1, :], w2[e, 128:D, :]).then_inc(ew_loaded, 16)

            def load_z(e, chunks):
                for c in chunks:
                    src = slot_rows[bass.ds(e * SLOTS + c * CN, CN), :].rearrange("(t p) d -> p t d", p=TM)
                    sp.dma_start(zs_in[:, c, :, :], src).then_inc(z_loaded[c], 16)

            turn(0, "first")
            with sp.Fori(1, LAST - 1) as i:
                turn(i, "mid")
            turn(LAST - 1, "mid", two_follow=False)
            turn(LAST, "last", two_follow=False)
            sp.wait_ge(rows_scattered, 64 * B)
            sp.wait_ge(h_mid_stored, 32 * B)
            sp.wait_ge(stage2_done, 4)

            load_z(0, range(CHUNKS))

            def turn3(e):
                sp.wait_ge(ew_full, e * 6 + 6)
                load_expert(e + 1)
                for c in range(CHUNKS):
                    sp.wait_ge(y_ready, e * CHUNKS + (c + 1))
                    sp.wait_ge(tokens_read, e * CHUNKS + (c + 1))
                    load_z(e + 1, [c])

            turn3(0)
            with sp.Fori(1, E - 1) as e:
                turn3(e)
            for added in y_added:
                sp.wait_ge(added, ADDED * E)

        @block.gpsimd
        def _(pool):
            wait = carried(pool, 0, lambda to: nc.gpsimd.tensor_tensor(to, tick[0:1, 0:1], tick[0:1, 0:1], ALU.add))
            step = step_counter(pool, pool_step, wait)
            nc.gpsimd.memset(ident[:], 0.0).then_inc(const_made, 1)
            nc.gpsimd.memset(earlier[:], 1.0).then_inc(const_made, 1)
            nc.gpsimd.iota(expert_of_real[:], pattern=[[0, 2], [1, E]], base=-E, channel_multiplier=0,
                           allow_small_or_imprecise_dtypes=True).then_inc(const_made, 1)
            nc.gpsimd.memset(tick[:], 0.0).then_inc(const_made, 1)
            nc.gpsimd.memset(empty_row[:], 0.0).then_inc(const_made, 1)
            pool.wait_ge(const_made, 5)
            nc.gpsimd.affine_select(out=ident[:], in_=ident[:], compare_op=ALU.not_equal, fill=1.0, base=0,
                                    pattern=[[-1, 128]], channel_multiplier=1).then_inc(const_ready, 1)
            nc.gpsimd.affine_select(out=earlier[:], in_=earlier[:], compare_op=ALU.is_gt, fill=0.0, base=0,
                                    pattern=[[1, T0]], channel_multiplier=-1).then_inc(const_ready, 1)
            nc.gpsimd.memset(ones_r[:].bitcast(F32), 1.0).then_inc(const_ready, 1)
            nc.gpsimd.memset(minus_half[:], -0.5).then_inc(const_ready, 1)
            nc.gpsimd.iota(expert_no[:], pattern=[[0, 2], [1, E]], base=-E, channel_multiplier=0,
                           allow_small_or_imprecise_dtypes=True).then_inc(const_ready, 1)
            nc.gpsimd.affine_select(out=expert_of_real[:], in_=expert_of_real[:], compare_op=ALU.is_gt, fill=1.0, base=S,
                                    pattern=[[-T0, 2], [0, E]], channel_multiplier=-1).then_inc(const_ready, 1)
            nc.gpsimd.iota(slot_base[:], pattern=[[0, 2], [SLOTS, E]], base=0, channel_multiplier=0,
                           allow_small_or_imprecise_dtypes=True).then_inc(const_ready, 1)
            nc.gpsimd.iota(dump_row[:], pattern=[[2 * T0, 2], [T0, TOP_K]], base=E * SLOTS, channel_multiplier=1,
                           allow_small_or_imprecise_dtypes=True).then_inc(const_ready, 1)
            nc.gpsimd.iota(tile_first[:], pattern=[[TILES * TM, CHUNKS], [TM, TILES]], base=0, channel_multiplier=0,
                           allow_small_or_imprecise_dtypes=True).then_inc(const_ready, 1)
            nc.gpsimd.iota(empty_row[:, D:D + 1], pattern=[[0, 1]], base=N, channel_multiplier=1,
                           allow_small_or_imprecise_dtypes=True).then_inc(const_ready, 1)
            pool.wait_ge(const_ready, 10)
            nc.gpsimd.tensor_copy(earlier_r[:], earlier[:]).then_inc(const_ready, 1)
            pool.wait_ge(emb_stored, 16 * (B + 1))
            pool.wait_ge(bias_placed, 32)
            pool.engine_nop().then_inc(stage1_done, 1)
            pool.wait_ge(stage1_done, 4)
            for e in range(E):
                dst = slot_rows[e * SLOTS:(e + 1) * SLOTS, :].rearrange("(t p) d -> p t d", p=TM)
                pool.dma_start(dst, empty_row[:].unsqueeze(1).to_broadcast([TM, CHUNKS * TILES, ROW])).then_inc(slots_cleared, 16)
            pool.dma_start(out[N:N + SLOTS, :].rearrange("(t p) d -> p t d", p=TM),
                           empty_row[:, 0:D].unsqueeze(1).to_broadcast([TM, CHUNKS * TILES, D])).then_inc(slots_cleared, 16)

            def rs_start(which):
                v, y, t, u = (rs[:, which, k, :] for k in range(4))
                step(nc.gpsimd.tensor_scalar(v, mean_var[:, which, :, 1], LN_EPS, None, ALU.add))
                step(nc.gpsimd.tensor_tensor(y, v, minus_half[0:T0, 0:2], ALU.pow))

            def rs_polish(which):
                v, y, t, u = (rs[:, which, k, :] for k in range(4))
                step(nc.gpsimd.tensor_tensor(t, y, y, ALU.mult))
                step(nc.gpsimd.tensor_tensor(t, t, v, ALU.mult), carry=True)
                step(nc.gpsimd.tensor_scalar(u, t, -0.5, 1.5, ALU.mult, ALU.add))
                return nc.gpsimd.tensor_tensor(y, y, u, ALU.mult)

            def v_low(b, g):
                pool.wait_ge(v_high, b * HALF + (g // 2 + 1))
                nc.gpsimd.tensor_tensor(v_l[:, g], v_l[:, g].bitcast(F32), v_h[:, g].bitcast(F32), ALU.subtract).then_inc(v_ready, 1)

            def ln1_start(b):
                wait(ln1_stats, b + 1)
                nc.gpsimd.tensor_scalar(neg_mean[:], mean_var[:, 0, :, 0], -1.0, 0.0, ALU.mult, ALU.add)
                rs_start(0)

            def ln1_apply(t):
                m, r = neg_mean[:, t:t + 1], rs[:, 0, 1, t:t + 1]
                nc.gpsimd.tensor_scalar(x_norm[:, t, 0:D], h_in[:, t, :], m, r, ALU.add, ALU.mult)
                nc.gpsimd.tensor_scalar(x_norm[:, t, D:], h_in[:, t, 128:D], m, r, ALU.add, ALU.mult).then_inc(x_ready, 1)

            def rms_scale(b):
                wait(z_squares, b + 1)
                ss, v, y, t, u = (rms[:, k, :] for k in range(5))
                step(nc.gpsimd.tensor_scalar(v, ss, 4.0 / D, RMS_EPS, ALU.mult, ALU.add))
                step(nc.gpsimd.tensor_tensor(y, v, minus_half[0:T0, 0:2], ALU.pow))
                step(nc.gpsimd.tensor_tensor(t, y, y, ALU.mult))
                step(nc.gpsimd.tensor_tensor(t, t, v, ALU.mult), carry=True)
                step(nc.gpsimd.tensor_scalar(u, t, -1.0, 3.0, ALU.mult, ALU.add))
                step(nc.gpsimd.tensor_tensor(z_row[:, :, ROW - 1], y, u, ALU.mult), carry=True)

            def rank(b, first):
                pool.wait_ge(counts_ready, b + 1)
                pos_, keep, val = rt[:, 8], rt[:, 9], rt[:, 10]
                step(nc.gpsimd.tensor_tensor(pos_, counts[:, 0:2, :], base[:].unsqueeze(1).to_broadcast([T0, 2, E]), ALU.add))
                step(nc.gpsimd.tensor_tensor(base[:], base[:], counts[:, 2, :], ALU.add), carry=True)
                step(nc.gpsimd.tensor_scalar(keep, pos_, float(CAP), None, ALU.is_lt))
                step(nc.gpsimd.tensor_tensor(val, pos_, slot_base[:], ALU.add))
                for k in range(TOP_K):
                    dump = dump_row[:, :, k:k + 1].to_broadcast([T0, 2, E])
                    a = rt[:, 11]
                    step(nc.gpsimd.tensor_tensor(a, val, dump, ALU.subtract))
                    step(nc.gpsimd.tensor_tensor(a, a, keep, ALU.mult))
                    step(nc.gpsimd.tensor_tensor(a, a, dump, ALU.add))
                    last = nc.gpsimd.tensor_tensor(slot_of[:, :, k, :], a, rt[:, 4 + k], ALU.mult)
                    if k == 0:
                        step(last)
                last.then_inc(slots_ranked, 1)

            def scatter(b):
                wait(slots_ready, b + 1)
                for t in range(2):
                    m = T1 if t else T0
                    for k in range(TOP_K):
                        pool.indirect_dma_start(
                            out=slot_rows, out_offset=bass.IndirectOffsetOnAxis(ap=slot_i[0:m, t, k:k + 1], axis=0),
                            in_=z_row[0:m, t, :], in_offset=None).then_inc(rows_scattered, 16)

            def residual(b):
                pool.wait_ge(res_loaded, b * 48 + 48)
                nc.gpsimd.tensor_tensor(h_res[:], h_res[:], proj_bias[:].unsqueeze(1).to_broadcast([T0, 2, D]),
                                        ALU.add).then_inc(res_biased, 1)

            def normed(g, i):
                pool.wait_ge(inv_ready, i * HEADS + (g + 1))
                p = probs[:, g % 3, :, 0:S]
                nc.gpsimd.tensor_tensor(p, p, row_inv[:, g, :].unsqueeze(2).to_broadcast([T0, 2, S]), ALU.mult).then_inc(probs_ready, 1)

            def turn(i, part, start, two_follow=True):
                step.turn(start)
                for g in range(HEADS):
                    normed(g, i)
                    if g in (2, 3) and part != "last":
                        ln1_apply(g - 2)
                    if g == 4:
                        v_low(i, 4)
                    if g == 5:
                        v_low(i, 5)
                    if g == 6:
                        v_low(i, 6)
                    if g == 7:
                        v_low(i, 7)
                if part != "first":
                    rank(i - 1, False)
                residual(i)
                if part != "first":
                    scatter(i - 1)
                wait(ln2_stats, i + 1)
                rs_start(1)
                rs_polish(1).then_inc(ln2_rs, 1)
                if part != "last":
                    for g in range(HALF):
                        v_low(i + 1, g)
                rms_scale(i)
                if two_follow:
                    ln1_start(i + 2)
                    step(rs_polish(0))
                return step.n

            pads = [q_h[:, :, ROWS:], q_l[:, ROWS:], q_l1[:, ROWS:], k_h[:, ROWS:], k_l[:, ROWS:], k_hl[:, ROWS:],
                    xt_h[:], xt_l[:], xt_l1[0:64, :], h_in[:], h_res[:], base[:], z_row[:]]
            for p in pads:
                step(nc.gpsimd.memset(p.bitcast(F32) if p.dtype == F32R else p, 0.0))
            step(nc.gpsimd.memset(xt_l1[64:128, :].bitcast(F32), 1.0))
            nc.gpsimd.iota(z_row[:, :, D:D + 1], pattern=[[T0, 2], [0, 1]], base=-S, channel_multiplier=1,
                           allow_small_or_imprecise_dtypes=True).then_inc(pads_ready, 1)
            wait(pads_ready, 2)
            at = step.n
            step.turn(at)
            ln1_start(0)
            step(rs_polish(0))
            for t in range(2):
                ln1_apply(t)
            for g in range(HALF):
                v_low(0, g)
            ln1_start(1)
            step(rs_polish(0))
            at += step.n
            n0 = turn(0, "first", at)
            pool.wait_ge(slots_cleared, 16 * (E + 1))
            n_mid = n0 + 11
            with pool.Fori(1, LAST - 1) as i:
                assert turn(i, "mid", (i - 1) * n_mid + (at + n0)) == n_mid, step.n - n0
            at = at + n0 + (LAST - 2) * n_mid
            at += turn(LAST - 1, "mid", at, two_follow=False)
            at += turn(LAST, "last", at, two_follow=False)
            step.turn(at)
            rank(LAST, False)
            scatter(LAST)
            at += step.n
            wait(rows_scattered, 64 * B)
            pool.engine_nop().then_inc(stage2_done, 1)
            wait(stage2_done, 4)

            def act_lows(e, c, h):
                pool.wait_ge(act_high, e * CHUNKS * HT + (c * HT + h + 1))
                nc.gpsimd.tensor_tensor(act_l[:, c % 2, h, :], act[:, c % 2, h, :], act_h[:, c % 2, h, :].bitcast(F32),
                                        ALU.subtract).then_inc(act_low, 1)

            def add_rows(e, c, first):
                if c == 0 and not first:
                    for added in y_added:
                        wait(added, e * ADDED)
                wait(tokens_read, e * CHUNKS + (c + 1))
                wait(y_ready, e * CHUNKS + (c + 1))
                for t in range(TILES):
                    pool.indirect_dma_start(
                        out=out, out_offset=bass.IndirectOffsetOnAxis(ap=token_i[:, c, t:t + 1], axis=0),
                        in_=y_out[:, c % 2, t, :], in_offset=None, compute_op=ALU.add).then_inc(y_added[c % 2], 16)

            def turn3(e, first):
                for c in range(CHUNKS):
                    for h in range(HT):
                        act_lows(e, c, h)
                    if c:
                        add_rows(e, c - 1, first)
                add_rows(e, CHUNKS - 1, first)

            turn3(0, True)
            with pool.Fori(1, E) as e:
                turn3(e, False)

        @block.scalar
        def _(a):
            wait = carried(a, 1, lambda to: nc.scalar.copy(to, tick[0:1, 0:1]))
            def regroup(r, gw):
                src = img[:].rearrange("p c (y g x) -> p (c y) g x", g=GRID, x=PATCH)[:, :, gw, :]
                nc.scalar.copy(img_grouped[:, gw, :].rearrange("p (r x) -> p r x", x=PATCH), src).then_inc(regrouped, 1)

            def third_high(n):
                a.wait_ge(w_loaded[n], 16 * (12, 12, 3)[n])
                cols = slice(n * W, (n + 1) * W)
                nc.scalar.copy(wq_h[:, cols], w_raw[n % 2][:, 0, :])
                nc.scalar.copy(wq_hb[0:D1, cols], w_raw[n % 2][0:D1, 1, :])
                nc.scalar.copy(wq_hl[:, cols], w_raw[n % 2][:, 1, :]).then_inc(w_high, 1)

            def patches_high(g):
                for half in range(2):
                    n = 2 * g + half
                    a.wait_ge(pt_full, n + 1)
                    src = bank[n % 4][:, 0:3 * IR].rearrange("p (k r) -> p k r", k=3)
                    nc.scalar.copy(pt_h[:, g % 2, 3 * half:3 * half + 3, :], src).then_inc(pt_high, 1)

            a.wait_ge(images_loaded, 16 * SEQS)
            for gw in range(GRID):
                regroup(0, gw)
            for k in range(KT):
                a.wait_ge(tok_full, k + 1)
                nc.scalar.copy(tok_h[:, k, :], bank[4 + k % 2][:, 0:D]).then_inc(tok_high, 1)
            for r in range(RT):
                third_high(r)
                for gw in range(GRID):
                    patches_high(r * GRID + gw)
                if r == 0:
                    a.wait_ge(bias_loaded, 16 * 9)
                    nc.scalar.copy(bias_h[:], bias_raw[:]).then_inc(bias_high, 1)
            for n in range(RT, 3):
                third_high(n)
            a.wait_ge(w_loaded[3], 16 * 3)
            as_heads = w_raw[1][:].rearrange("p a (h n) -> p a h n", h=HEADS)
            nc.scalar.copy(wp_h[:], as_heads[:, 0])
            nc.scalar.copy(wp_hl[:], as_heads[:, 1]).then_inc(w_high, 1)
            a.wait_ge(emb_stored, 16 * (B + 1))
            a.wait_ge(bias_placed, 32)
            nc.scalar.copy(minus_half[0:1, 3:4], minus_half[0:1, 3:4]).then_inc(stage1_done, 1)
            a.wait_ge(stage1_done, 4)

            def use(part, i, name):
                a.wait_ge(ring_full, position(part, i, name))
                return ring_bank(part, name)

            def qk_high(i, part, kind, n):
                src = use(part, i, (kind, n))
                src = src[:, 0:3 * SP].rearrange("p (k s) -> p k s", k=3)
                main, pair = (q_h[:, 0, :], q_h[:, 1, :]) if kind == "q" else (k_h, k_hl)
                m = main[:, 0:ROWS].rearrange("p (s j) -> p j s", j=HEADS)
                r = pair[:, 0:ROWS].rearrange("p (s j) -> p j s", j=HEADS)
                nc.scalar.copy(m[:, 2 * n:2 * n + 2, :], src[:, 0:2, 0:S])
                nc.scalar.copy(r[0:64, 2 * n, :], src[0:64, 2, 0:S])
                nc.scalar.copy(r[0:64, 2 * n + 1, :], src[64:128, 2, 0:S]).then_inc(ring_act, 1)

            def xt_high(i, part, b):
                src = use(part, i, ("xt", 0))[:, 0:2 * S].rearrange("p (k s) -> p k s", k=2)
                nc.scalar.copy(xt_h[:, :, 0:S], src).then_inc(ring_act, 1)

            def v_evac(i, part, b, n):
                src = use(part, i, ("v", n))
                m = T1 if n // 4 else T0
                if not (part == "before" and n < 4):
                    a.wait_ge(v_stored[n % 4], b * 32 + 16 * (n // 4))
                nc.scalar.activation(v_out[0:m, n % 4, :], src[0:m, 0:2 * D], ACT.Copy, scale=float(D) ** -0.5).then_inc(ring_act, 1)

            def zt_evac(part, i, b):
                src = use(part, i, ("zt", 0))[:, 0:2 * S].rearrange("p (k s) -> p k s", k=2)
                nc.scalar.copy(z_t[:, 0, :], src[:, 0])
                nc.scalar.copy(z_t[0:D1, 1, :], src[0:D1, 1]).then_inc(ring_act, 1)

            def route_exps(b):
                a.wait_ge(route_sub, b + 1)
                nc.scalar.activation(rt[:, 1], rt[:, 0], ACT.Exp).then_inc(route_exp, 1)

            def exps(i, g):
                a.wait_ge(max_ready, i * HEADS + (g + 1))
                src = score_bank[g % 2][0:T0, 0:2 * SP].rearrange("p (t s) -> p t s", t=2)
                for t in range(2):
                    last = nc.scalar.activation(probs[:, g % 3, t, 0:S], src[:, t, 0:S], ACT.Exp,
                                                bias=neg_max[:, g, t:t + 1], accum_out=row_sum[:, g, t:t + 1])
                last.then_inc(exp_done, 1)

            def probs_t_h(i, g):
                a.wait_ge(probs_t_full, i * HEADS + (g + 1))
                src = probs_t_bank[0:T0, 0:2 * SP].rearrange("p (t s) -> p t s", t=2)
                nc.scalar.copy(pt2_h[:, g % 2], src).then_inc(probs_t_high, 1)

            def o_high(i, part, g):
                src = use(part, i, ("pv", g))
                cols = slice(S * g, S * (g + 1))
                nc.scalar.copy(o_h[:, 0, cols], src[:, 0:S])
                nc.scalar.copy(o_h[0:64, 1, cols], src[0:64, SP:SP + S])
                nc.scalar.copy(o_h[64:128, 1, cols], src[0:64, SP:SP + S]).then_inc(ring_act, 1)

            def v_highs(b, n):
                if n % 2 == 0:
                    wait(v_loaded[n // 2], b * 32 + 32)
                g = slice(2 * n, 2 * n + 2)
                nc.scalar.copy(v_h[:, g], v_l[:, g].bitcast(F32)).then_inc(v_high, 1)

            def turn(i, part):
                nxt = part != "last"
                for s in range(2, HEADS + 3):
                    if 4 <= s <= HEADS:
                        o_high(i, part, s - 4)
                    if s < HEADS + 2:
                        probs_t_h(i, s - 2)
                    if s < HEADS:
                        exps(i, s)
                    if s in (4, 5):
                        v_highs(i, s - 2)
                    if s == XT_STEP and nxt:
                        xt_high(i, part, i + 1)
                    if s >= HEADS:
                        o_high(i, part, s - 3)
                        for n in V_CHUNKS[s - HEADS] if nxt else []:
                            v_evac(i, part, i + 1, n)
                if nxt:
                    for n in range(4):
                        qk_high(i, part, "q", n)
                        if n >= 2:
                            v_highs(i + 1, n - 2)
                    for n in range(4):
                        qk_high(i, part, "k", n)
                zt_evac(part, i, i)
                if nxt:
                    v_evac(i, part, i + 1, 4)
                    v_evac(i, part, i + 1, 5)
                    exps(i + 1, 0)
                route_exps(i)
                if nxt:
                    v_evac(i, part, i + 1, 6)
                    v_evac(i, part, i + 1, 7)
                    exps(i + 1, 1)

            a.wait_ge(pads_ready, 2)
            xt_high(0, "before", 0)
            for n in range(8):
                v_evac(0, "before", 0, n)
            for kind in "qk":
                for n in range(4):
                    qk_high(0, "before", kind, n)
            for n in range(2):
                v_highs(0, n)
            for g in range(2):
                exps(0, g)
            turn(0, "first")
            with a.Fori(1, LAST) as i:
                turn(i, "mid")
            turn(LAST, "last")

            def up_high(e, u):
                a.wait_ge(ew_full, e * 6 + (u + 1))
                nc.scalar.copy(up_w[:, 2 * u:2 * u + 2], bank[u][:].rearrange("p (r k d) -> p r k d", r=2, k=2)).then_inc(ew_high, 1)

            def down_high(e, u):
                a.wait_ge(ew_full, e * 6 + (u + 5))
                nc.scalar.copy(down_h[:, 2 * u:2 * u + 2, :], bank[4 + u][:, 0:2 * D].rearrange("p (h d) -> p h d", h=2)).then_inc(ew_high, 1)

            for u in range(4):
                up_high(0, u)
            for u in range(2):
                down_high(0, u)
            a.wait_ge(rows_scattered, 64 * B)
            nc.scalar.copy(minus_half[0:1, 3:4], minus_half[0:1, 3:4]).then_inc(stage2_done, 1)
            a.wait_ge(stage2_done, 4)

            def zt_h(e, c):
                wait(zt_full, e * CHUNKS + (c + 1))
                for k in range(2):
                    last = nc.scalar.activation(zst_h[:, c % 2, k, :], bank[4 + k][:, 0:CN], ACT.Copy,
                                                scale=norm_cols[:, k, bass.ds(e, 1)])
                last.then_inc(zt_high, 1)

            def z_weights(e, c):
                wait(z_scaled, e * CHUNKS + (c + 1))
                for t in range(TILES):
                    z = zs_in[:, c, t, 0:D]
                    last = nc.scalar.activation(z, z, ACT.Copy, scale=zs_in[:, c, t, bass.ds(e + (D + 1), 1)])
                last.then_inc(z_weighted, 1)

            def silus(e, c, h):
                n = c * 2 * HT + 2 * h
                a.wait_ge(gu_full, e * (2 * HT * CHUNKS) + (n + 1))
                nc.scalar.activation(silu[:, h, :], bank[n % 4][:, 0:CN], ACT.Silu).then_inc(silu_ready, 1)

            def act_highs(e, c, h):
                a.wait_ge(act_ready, e * (HT * CHUNKS) + (c * HT + h + 1))
                nc.scalar.copy(act_h[:, c % 2, h, :], act[:, c % 2, h, :]).then_inc(act_high, 1)

            def turn3(e, nxt):
                for c in range(CHUNKS):
                    silus(e, c, 0)
                    silus(e, c, 1)
                    act_highs(e, c, 0)
                    if c + 1 < CHUNKS:
                        zt_h(e, c + 1)
                    elif nxt:
                        zt_h(e + 1, 0)
                    silus(e, c, 2)
                    act_highs(e, c, 1)
                    silus(e, c, 3)
                    act_highs(e, c, 2)
                    act_highs(e, c, 3)
                    if c < CHUNKS - 1:
                        z_weights(e, c)
                if nxt:
                    for u in range(2):
                        up_high(e + 1, u)
                z_weights(e, CHUNKS - 1)
                if nxt:
                    for u in range(2, 4):
                        up_high(e + 1, u)
                    for u in range(2):
                        down_high(e + 1, u)

            zt_h(0, 0)
            turn3(0, True)
            with a.Fori(1, E - 1) as e:
                turn3(e, True)
            turn3(E - 1, False)

        @block.vector
        def _(v):
            wait = carried(v, 2, lambda to: nc.vector.tensor_copy(to, tick[0:1, 0:1]))
            step = step_counter(v, dve_step)
            alone = [step_counter(v, signal, wait) for signal in stats_step]
            def regroup(r, gw):
                v.wait_ge(pt_full, 2 * ((r - 1) * GRID + gw + 1))
                src = img[:].rearrange("p c (y g x) -> p (c y) g x", g=GRID, x=PATCH)[:, :, gw, :]
                nc.vector.tensor_copy(img_grouped[:, gw, :].rearrange("p (r x) -> p r x", x=PATCH), src).then_inc(regrouped, 1)

            def third_low(n):
                v.wait_ge(w_high, n + 1)
                cols = slice(n * W, (n + 1) * W)
                raw = w_raw[n % 2]
                nc.vector.tensor_tensor(wq_l[:, cols], raw[:, 0, :], wq_h[:, cols].bitcast(F32), ALU.subtract)
                nc.vector.tensor_tensor(wq_hl[64:128, cols], raw[64:128, 1, :], wq_hl[64:128, cols].bitcast(F32),
                                        ALU.subtract).then_inc(w_low, 1)

            def patches_low(g):
                for half in range(2):
                    n = 2 * g + half
                    v.wait_ge(pt_high, n + 1)
                    src = bank[n % 4][:, 0:3 * IR].rearrange("p (k r) -> p k r", k=3)
                    ks = slice(3 * half, 3 * half + 3)
                    nc.vector.tensor_tensor(pt_l[:, g % 2, ks, :], src, pt_h[:, g % 2, ks, :].bitcast(F32), ALU.subtract).then_inc(pt_low, 1)

            def embedded(g):
                r, gw = g // GRID, g % GRID
                if gw == 0 and r:
                    v.wait_ge(emb_stored, 16 * (SEQS * r + 1))
                v.wait_ge(emb_full, g + 1)
                nc.vector.tensor_tensor(emb[:, gw, :], bank[6 + g % 2][0:IR, 0:D], pos_g[:, gw, :], ALU.add).then_inc(emb_ready, 1)

            nc.vector.memset(wq_hb[64:128, :].bitcast(F32), 0.0).then_inc(w_rows_cleared, 1)
            for k in range(KT):
                v.wait_ge(tok_high, k + 1)
                nc.vector.tensor_tensor(tok_l[:, k, :], bank[4 + k % 2][:, 0:D], tok_h[:, k, :].bitcast(F32), ALU.subtract).then_inc(tok_low, 1)
            v.wait_ge(image_args_loaded, 16 * (3 + SEQS))
            pos_g = pos[:].rearrange("p (w d) -> p w d", w=GRID)
            nc.vector.tensor_tensor(pos_g, pos_g, tok_bias[:].unsqueeze(1).to_broadcast([IR, GRID, D]), ALU.add).then_inc(token_bias, 1)
            nc.vector.tensor_tensor(cls[:], cls[:], cls_pos[:], ALU.add).then_inc(token_bias, 1)
            v.wait_ge(token_bias, 2)
            for r in range(RT):
                third_low(r)
                for gw in range(GRID):
                    g = r * GRID + gw
                    patches_low(g)
                    if gw:
                        embedded(g - 1)
                if r + 1 < RT:
                    v.wait_ge(images_loaded, 16 * SEQS * (r + 2))
                    for gw in range(GRID):
                        regroup(r + 1, gw)
                embedded(r * GRID + GRID - 1)
                if r == 0:
                    v.wait_ge(bias_high, 1)
                    nc.vector.tensor_tensor(bias_l[:], bias_raw[:], bias_h[:].bitcast(F32), ALU.subtract).then_inc(bias_low, 1)
            for n in range(RT, 3):
                third_low(n)
            v.wait_ge(w_high, 4)
            as_heads = w_raw[1][:].rearrange("p a (h n) -> p a h n", h=HEADS)
            nc.vector.tensor_tensor(wp_l[:], as_heads[:, 0], wp_h[:].bitcast(F32), ALU.subtract)
            nc.vector.tensor_tensor(wp_hl[64:128], as_heads[64:128, 1], wp_hl[64:128].bitcast(F32), ALU.subtract).then_inc(w_low, 1)
            v.wait_ge(w_low, 4)
            v.wait_ge(emb_stored, 16 * (B + 1))
            v.wait_ge(bias_placed, 32)
            nc.vector.memset(minus_half[0:1, 2:3], -0.5).then_inc(stage1_done, 1)
            v.wait_ge(stage1_done, 4)

            def use(part, i, name):
                e = uses.who(name)
                if "a" in e:
                    v.wait_ge(ring_act, position(part, i, name, "a"))
                else:
                    v.wait_ge(ring_full, position(part, i, name))
                return ring_bank(part, name)

            def qk_low(i, part, kind, n):
                src = use(part, i, (kind, n))
                src = src[:, 0:3 * SP].rearrange("p (k s) -> p k s", k=3)
                hm, lm, pair = (q_h[:, 0, :], q_l, q_h[:, 1, :]) if kind == "q" else (k_h, k_l, k_hl)
                by_chunk = lambda t: t[:, 0:ROWS].rearrange("p (s j) -> p j s", j=HEADS)
                js = slice(2 * n, 2 * n + 2)
                nc.vector.tensor_tensor(by_chunk(lm)[:, js, :], src[:, 0:2, 0:S], by_chunk(hm)[:, js, :].bitcast(F32), ALU.subtract)
                r = by_chunk(pair)
                for k in range(2):
                    j = 2 * n + k
                    dst = by_chunk(q_l1)[:, j, :] if kind == "q" else r[64:128, j, :]
                    last = nc.vector.tensor_tensor(dst, src[64 * k:64 * k + 64, 2, 0:S], r[0:64, j, :].bitcast(F32), ALU.subtract)
                last.then_inc(ring_dve, 1)

            def stat(which, src, b, signal):
                alone[which].turn(b)
                for t in range(2):
                    ins = nc.vector.bn_stats(stats[:, which, t, :], src[:, t, :])
                    if t:
                        alone[which](ins, carry=True)
                for t in range(2):
                    last = nc.vector.bn_aggr(mean_var[:, which, t, :], stats[:, which, t, :])
                last.then_inc(signal, 1)

            def apply(dst, src, which, t):
                return nc.vector.tensor_scalar(dst, src, mean_var[:, which, t, 0:1], rs[:, which, 1, t:t + 1],
                                               ALU.subtract, ALU.mult)

            def ln1_stat(b):
                v.wait_ge(h_loaded, b * 48 + 48)
                stat(0, h_in, b, ln1_stats)

            def xt_low(i, part):
                src = use(part, i, ("xt", 0))[:, 0:2 * S].rearrange("p (k s) -> p k s", k=2)
                nc.vector.tensor_tensor(xt_l[:, 0:S], src[:, 0], xt_h[:, 0, 0:S].bitcast(F32), ALU.subtract)
                nc.vector.tensor_tensor(xt_l1[0:64, 0:S], src[0:64, 1], xt_h[0:64, 1, 0:S].bitcast(F32),
                                        ALU.subtract).then_inc(ring_dve, 1)

            def bc(t):
                return t.to_broadcast([T0, 2, E])

            def route_logits(part, i, b):
                src = use(part, i, ("log", 0))[0:T0, 0:2 * E].rearrange("p (t e) -> p t e", t=2)
                nc.vector.tensor_copy(logits[0:T0, 0, :], src[0:T0, 0, :])
                step(nc.vector.tensor_copy(logits[0:T1, 1, :], src[0:T1, 1, :]))
                nc.vector.tensor_copy(rt[:, 7], logits[:]).then_inc(ring_dve, 1)
                step(nc.vector.tensor_reduce(r1[:, 0], logits[:], AXIS.X, ALU.max))
                nc.vector.tensor_tensor(rt[:, 0], logits[:], bc(r1[:, 0]), ALU.subtract).then_inc(route_sub, 1)

            def choose_likelihood(b):
                v.wait_ge(route_exp, b + 1)
                step(nc.vector.tensor_reduce(r1[:, 1], rt[:, 1], AXIS.X, ALU.add))
                step(nc.vector.reciprocal(r1[:, 2], r1[:, 1]))
                step(nc.vector.tensor_tensor(rt[:, 2], rt[:, 1], bc(r1[:, 2]), ALU.mult))

            def choose_most(k):
                rest, eq = rt[:, 3] if k else rt[:, 2], rt[:, 6]
                step(nc.vector.tensor_reduce(r1[:, 3 + k], rest, AXIS.X, ALU.max))
                step(nc.vector.tensor_tensor(eq, rest, bc(r1[:, 3 + k]), ALU.is_equal))
                step(nc.vector.tensor_tensor(eq, eq, expert_no[:], ALU.mult))

            def choose_first(k):
                p, m, eq, pick = rt[:, 2], rt[:, 3], rt[:, 6], rt[:, 4 + k]
                step(nc.vector.tensor_reduce(r1[:, 5], eq, AXIS.X, ALU.min))
                step(nc.vector.tensor_tensor(pick, expert_of_real[:], bc(r1[:, 5]), ALU.is_equal))
                if k == 0:
                    step(nc.vector.scalar_tensor_tensor(m, pick, -2.0, p, ALU.mult, ALU.add))

            def choose_weights():
                w = r1
                nc.vector.tensor_tensor(w[:, 6], w[:, 3], w[:, 4], ALU.add)
                step(nc.vector.tensor_tensor(picks[:], rt[:, 4], rt[:, 5], ALU.add))
                nc.vector.tensor_tensor(rt[:, 6], picks[:].bitcast(F32), rt[:, 2], ALU.mult)
                step(nc.vector.reciprocal(w[:, 7], w[:, 6]))
                nc.vector.tensor_tensor(z_row[:, :, D + 1:D + 1 + E], rt[:, 6], bc(w[:, 7]), ALU.mult)
                nc.vector.tensor_scalar(z_row[:, :, D:D + 1], z_row[:, :, D:D + 1], float(S), None, ALU.add).then_inc(chosen, 1)

            def route_counts(part, i, b):
                src = use(part, i, ("cnt", 0))[0:T0, 0:3 * E].rearrange("p (t e) -> p t e", t=3)
                nc.vector.tensor_copy(counts[:], src).then_inc(ring_dve, 1)
                v.wait_ge(ring_dve, position(part, i, ("cnt", 0), "d"))
                nc.vector.memset(r1[:, 5], 0.0).then_inc(counts_ready, 1)

            def route_slots(b):
                v.wait_ge(slots_ranked, b + 1)
                step(nc.vector.tensor_reduce(slot_f[:].rearrange("p t k o -> p (t k) o"), slot_of[:].rearrange("p t k e -> p (t k) e"),
                                             AXIS.X, ALU.add))
                nc.vector.tensor_copy(slot_i[:], slot_f[:].rearrange("p t k o -> p t (k o)")).then_inc(slots_ready, 1)

            def maxes(i, g):
                v.wait_ge(scores_full, i * HEADS + (g + 1))
                src = score_bank[g % 2][0:T0, 0:2 * SP].rearrange("p (t s) -> p t s", t=2)
                nc.vector.tensor_reduce(neg_max[:, g, :].unsqueeze(2), src[:, :, 0:S], AXIS.X, ALU.max, negate=True).then_inc(max_ready, 1)

            def invs(i, g):
                v.wait_ge(exp_done, i * HEADS + (g + 1))
                nc.vector.reciprocal(row_inv[:, g, :], row_sum[:, g, :]).then_inc(inv_ready, 1)

            def probs_t_l(i, g):
                v.wait_ge(probs_t_high, i * HEADS + (g + 1))
                src = probs_t_bank[0:T0, 0:2 * SP].rearrange("p (t s) -> p t s", t=2)
                nc.vector.tensor_tensor(pt2_l[:, g % 2], src, pt2_h[:, g % 2].bitcast(F32), ALU.subtract).then_inc(probs_t_low, 1)

            def o_low(i, part, g):
                src = use(part, i, ("pv", g))
                cols = slice(S * g, S * (g + 1))
                nc.vector.tensor_tensor(o_l[:, cols], src[:, 0:S], o_h[:, 0, cols].bitcast(F32), ALU.subtract)
                nc.vector.tensor_tensor(o_l1[:, cols], src[0:64, SP:SP + S], o_h[0:64, 1, cols].bitcast(F32),
                                        ALU.subtract).then_inc(ring_dve, 1)

            def y_evac(i, part):
                v.wait_ge(res_biased, i + 1)
                if part != "first":
                    v.wait_ge(h_mid_stored, i * 32)
                for t in range(2):
                    src = use(part, i, ("y", t))
                    m = T1 if t else T0
                    nc.vector.tensor_tensor(h_mid[0:m, t, :], src[0:m, 0:D], h_res[0:m, t, :], ALU.add).then_inc(ring_dve, 1)
                v.wait_ge(ring_dve, position(part, i, ("y", 1), "d"))
                nc.vector.memset(r1[:, 5], 0.0).then_inc(h_mid_ready, 1)

            def ln2_apply(i, part):
                v.wait_ge(ln2_rs, i + 1)
                if part != "first":
                    v.wait_ge(rows_scattered, i * 64)
                for t in range(2):
                    last = apply(z_row[:, t, 0:D], h_mid[:, t, :], 1, t)
                last.then_inc(z_ready, 1)
                v.wait_ge(z_ready, i + 1)
                for t in range(2):
                    z = z_row[:, t, 0:D]
                    ins = nc.vector.tensor_tensor_reduce(square[:], z, z, 1.0, 0.0, ALU.mult, ALU.add, rms[:, 0, t:t + 1])
                    if t == 0:
                        step(ins)
                ins.then_inc(z_squares, 1)

            def turn(i, part, start, two_follow=True):
                step.turn(start)
                nxt = part != "last"
                for s in range(2, HEADS + 3):
                    if 2 < s < HEADS:
                        maxes(i, s)
                    if 3 <= s <= HEADS:
                        invs(i, s - 1)
                    if 4 <= s <= HEADS:
                        o_low(i, part, s - 4)
                    if s < HEADS + 2:
                        probs_t_l(i, s - 2)
                    if part != "first":
                        if s == 2:
                            choose_first(0)
                        if s == 3:
                            choose_most(1)
                        if s == 4:
                            choose_first(1)
                        if s == 5:
                            choose_weights()
                        if s == COUNT_STEP:
                            route_counts(part, i, i - 1)
                    if s == XT_STEP and nxt:
                        xt_low(i, part)
                    if s >= HEADS:
                        o_low(i, part, s - 3)
                if part != "first":
                    route_slots(i - 1)
                y_evac(i, part)
                stat(1, h_mid, i, ln2_stats)
                if nxt:
                    for n in range(2):
                        qk_low(i, part, "q", n)
                ln2_apply(i, part)
                if nxt:
                    for n in range(2, 4):
                        qk_low(i, part, "q", n)
                    if two_follow:
                        ln1_stat(i + 2)
                    for n in range(4):
                        qk_low(i, part, "k", n)
                if nxt:
                    maxes(i + 1, 0)
                route_logits(part, i, i)
                choose_likelihood(i)
                if nxt:
                    invs(i + 1, 0)
                    maxes(i + 1, 1)
                choose_most(0)
                if nxt:
                    maxes(i + 1, 2)
                    invs(i + 1, 1)
                return step.n

            step(nc.vector.memset(probs[:], 0.0))
            nc.vector.memset(v_l[:].bitcast(F32), 0.0).then_inc(pads_ready, 1)
            v.wait_ge(pads_ready, 2)
            nc.vector.memset(logits[:], 0.0)
            step(nc.vector.memset(h_mid[:], 0.0))
            at = step.n
            step.turn(at)
            ln1_stat(0)
            at += step.n
            xt_low(0, "before")
            for kind in "qk":
                for n in range(4):
                    qk_low(0, "before", kind, n)
            ln1_stat(1)
            for g in range(3):
                maxes(0, g)
            for g in range(2):
                invs(0, g)
            n0 = turn(0, "first", at)
            n_mid = n0 + 11
            with v.Fori(1, LAST - 1) as i:
                assert turn(i, "mid", (i - 1) * n_mid + (at + n0)) == n_mid, step.n - n0
            at = at + n0 + (LAST - 2) * n_mid
            at += turn(LAST - 1, "mid", at, two_follow=False)
            at += turn(LAST, "last", at, two_follow=False)
            step.turn(at)
            choose_first(0)
            choose_most(1)
            choose_first(1)
            choose_weights()
            route_counts("after", 0, LAST)
            route_slots(LAST)
            at += step.n

            def up_low(e, u):
                v.wait_ge(ew_high, e * 6 + (u + 1))
                src = bank[u][:].rearrange("p (r k d) -> p r k d", r=2, k=2)
                w = up_w[:, 2 * u:2 * u + 2]
                nc.vector.tensor_tensor(up_l[:, 2 * u:2 * u + 2, :], src[:, :, 0], w[:, :, 0].bitcast(F32), ALU.subtract)
                nc.vector.tensor_tensor(w[64:128, :, 1], src[64:128, :, 1], w[64:128, :, 1].bitcast(F32), ALU.subtract).then_inc(ew_low, 1)

            def down_low(e, u):
                v.wait_ge(ew_high, e * 6 + (u + 5))
                hs = slice(2 * u, 2 * u + 2)
                nc.vector.tensor_tensor(down_l[:, hs, :], bank[4 + u][:, 0:2 * D].rearrange("p (h d) -> p h d", h=2),
                                        down_h[:, hs, :].bitcast(F32), ALU.subtract).then_inc(ew_low, 1)

            for u in range(4):
                up_low(0, u)
            for u in range(2):
                down_low(0, u)
            v.wait_ge(rows_scattered, 64 * B)
            nc.vector.memset(minus_half[0:1, 2:3], -0.5).then_inc(stage2_done, 1)
            v.wait_ge(stage2_done, 4)

            def z_scale(e, c):
                v.wait_ge(z_loaded[c], e * 16 + 16)
                if not (isinstance(e, int) and e == 0 and c < 2):
                    v.wait_ge(zt_full, e * CHUNKS + (c - 1))
                for t in range(TILES):
                    s_ = zs_in[:, c, t, ROW - 1:ROW]
                    nc.vector.tensor_scalar(zs[:, c % 2, t, 0:D], zs_in[:, c, t, 0:D], s_, None, ALU.mult)
                    last = nc.vector.tensor_scalar(zs[:, c % 2, t, D:], zs_in[:, c, t, 128:D], s_, None, ALU.mult)
                last.then_inc(z_scaled, 1)
                if not (isinstance(e, int) and e == 0):
                    v.wait_ge(y_added[c % 2], e * ADDED - (64 if c < 2 else 0))
                number = zs_in[:, c, :, D]
                nc.vector.scalar_tensor_tensor(token_f[:, c, :], number, float(N), tile_first[:, c, :], ALU.is_ge, ALU.mult).then_inc(empty_marked, 1)
                v.wait_ge(empty_marked, e * CHUNKS + (c + 1))
                nc.vector.tensor_tensor(token_i[:, c, :], token_f[:, c, :], number, ALU.add).then_inc(tokens_read, 1)

            def zt_l(e, c):
                v.wait_ge(zt_high, e * CHUNKS + (c + 1))
                for k in range(2):
                    last = nc.vector.scalar_tensor_tensor(zst_l[:, c % 2, k, :], bank[4 + k][:, 0:CN],
                                                          norm_cols[:, k, bass.ds(e, 1)], zst_h[:, c % 2, k, :].bitcast(F32),
                                                          ALU.mult, ALU.subtract)
                last.then_inc(zt_low, 1)

            def gated(e, c, h):
                n = c * 2 * HT + 2 * h + 1
                v.wait_ge(gu_full, e * (2 * HT * CHUNKS) + (n + 1))
                v.wait_ge(silu_ready, e * (HT * CHUNKS) + (c * HT + h + 1))
                nc.vector.tensor_tensor(act[:, c % 2, h, :], silu[:, h, :], bank[n % 4][:, 0:CN], ALU.mult).then_inc(act_ready, 1)

            def y_rows(e, c, first):
                v.wait_ge(z_weighted, e * CHUNKS + (c + 1))
                if not (first and c < 2):
                    v.wait_ge(y_added[c % 2], e * ADDED + 16 * TILES * (c // 2))
                for u in range(2):
                    v.wait_ge(y_full, e * (2 * CHUNKS) + (2 * c + u + 1))
                    for t in (2 * u, 2 * u + 1):
                        last = nc.vector.scalar_tensor_tensor(y_out[:, c % 2, t, :], bank[6 + u][0:TM, (t % 2) * D:(t % 2) * D + D],
                                                              zs_in[:, c, t, bass.ds(e + (D + 1), 1)], zs_in[:, c, t, 0:D],
                                                              ALU.mult, ALU.add)
                last.then_inc(y_ready, 1)

            def turn3(e, first, nxt):
                for c in range(CHUNKS):
                    gated(e, c, 0)
                    gated(e, c, 1)
                    if c + 1 < CHUNKS:
                        zt_l(e, c + 1)
                    elif nxt:
                        zt_l(e + 1, 0)
                    gated(e, c, 2)
                    gated(e, c, 3)
                    if c + 2 < CHUNKS:
                        z_scale(e, c + 2)
                    elif nxt:
                        z_scale(e + 1, c + 2 - CHUNKS)
                    if 0 < c < CHUNKS - 1:
                        y_rows(e, c - 1, first)
                if nxt:
                    for u in range(2):
                        up_low(e + 1, u)
                y_rows(e, CHUNKS - 2, first)
                if nxt:
                    for u in range(2, 4):
                        up_low(e + 1, u)
                y_rows(e, CHUNKS - 1, first)
                if nxt:
                    for u in range(2):
                        down_low(e + 1, u)

            z_scale(0, 0)
            z_scale(0, 1)
            zt_l(0, 0)
            turn3(0, True, True)
            with v.Fori(1, E - 1) as e:
                turn3(e, False, True)
            turn3(E - 1, False, False)

        @block.tensor
        def _(pe):
            def passes(dst, pairs):
                for n, (lhs, rhs) in enumerate(pairs):
                    last = nc.tensor.matmul(dst, lhs, rhs, start=(n == 0), stop=(n == len(pairs) - 1))
                return last

            def turn_patches(g):
                r, gw = g // GRID, g % GRID
                pe.wait_ge(regrouped, g + 1)
                for half in range(2):
                    n = 2 * g + half
                    if n >= 4:
                        pe.wait_ge(pt_low, n - 3)
                    for k in range(3):
                        kk = 3 * half + k
                        last = nc.tensor.transpose(bank[n % 4][:, k * IR:(k + 1) * IR],
                                                   img_grouped[:, gw, 128 * kk:128 * kk + 128], ident[0:IR, 0:IR])
                    last.then_inc(pt_full, 1)

            def embed(g):
                if g >= 2:
                    pe.wait_ge(emb_ready, g - 1)
                pe.wait_ge(pt_low, 2 * g + 2)
                pairs = []
                for k in range(KT):
                    ph, pl = pt_h[:, g % 2, k, :], pt_l[:, g % 2, k, :]
                    pairs += [(ph, tok_h[:, k, :]), (ph, tok_l[:, k, :]), (pl, tok_h[:, k, :])]
                passes(bank[6 + g % 2][0:IR, 0:D], pairs).then_inc(emb_full, 1)

            pe.wait_ge(const_ready, 11)
            pe.wait_ge(tok_loaded, 32)
            for k in range(KT):
                if k >= 2:
                    pe.wait_ge(tok_low, k - 1)
                nc.tensor.transpose(bank[4 + k % 2][:, 0:128], tok_raw[:, 0, 128 * k:128 * k + 128], ident[:])
                nc.tensor.transpose(bank[4 + k % 2][:, 128:D], tok_raw[0:D1, 1, 128 * k:128 * k + 128], ident[0:D1, 0:D1]).then_inc(tok_full, 1)
            turn_patches(0)
            pe.wait_ge(tok_low, KT)
            for g in range(RT * GRID):
                if g + 1 < RT * GRID and (g + 1) % GRID:
                    turn_patches(g + 1)
                embed(g)
                if g + 1 < RT * GRID and (g + 1) % GRID == 0:
                    turn_patches(g + 1)
            pe.wait_ge(emb_stored, 16 * (B + 1))
            nc.tensor.transpose(bank[0][0:1, 0:1], ident[0:1, 0:1], ident[0:1, 0:1]).then_inc(stage1_done, 1)
            pe.wait_ge(stage1_done, 4)
            pe.wait_ge(const_loaded, 16 * 6)

            def use(part, i, name):
                here = uses.lists[part].index(name)
                back = here - GB
                if back >= 0:
                    old_part, old = part, uses.lists[part][back]
                    old_turn = i
                elif part == "before":
                    return ring_bank(part, name)
                else:
                    old_part = {"first": "before", "mid": "mid", "last": "mid", "after": "last"}[part]
                    old = uses.lists[old_part][back]
                    old_turn = {"before": 0, "mid": i - 1 if part != "last" else LAST - 1, "last": LAST}[old_part]
                e = "d" if "d" in uses.who(old) else "a"
                c = uses.count(e)
                seq = [n for n in uses.lists[old_part] if e in uses.who(n)]
                if part == "mid" and back < 0:
                    value = c.start(i) - (len(seq) - seq.index(old) - 1)
                elif old_part == "before":
                    value = seq.index(old) + 1
                else:
                    value = position(old_part, old_turn, old, e)
                pe.wait_ge(ring_dve if e == "d" else ring_act, value)
                return ring_bank(part, name)

            def x_side(t=None):
                cols = slice(0, SP) if t is None else slice(t * T0, t * T0 + (T1 if t else T0))
                return xt_h[:, 0, cols], xt_l[:, cols], xt_h[:, 1, cols], xt_l1[:, cols]

            def w_side(cols):
                return wq_h[:, cols], wq_l[:, cols], wq_hl[:, cols], wq_hb[:, cols]

            def products(x_, w_):
                (xh, xl, xhh, xl1), (wh, wl, whl, whb) = x_, w_
                return [(xh, wh), (xh, wl), (xl, wh), (xhh, whl), (xl1, whb)]

            def turned(pairs):
                return [(b_, a_) for a_, b_ in pairs]

            def qk(i, part, kind, n):
                dst = use(part, i, (kind, n))
                first = (0 if kind == "q" else W) + 2 * n * D
                for k in range(3):
                    cols = slice(first + 128 * k, first + 128 * k + 128)
                    last = passes(dst[:, k * SP:(k + 1) * SP], turned(products(x_side(), w_side(cols))))
                last.then_inc(ring_full, 1)

            def xt(i, part, b):
                dst = use(part, i, ("xt", 0))
                pe.wait_ge(x_ready, 2 * b + 2)
                for t in range(2):
                    m = T1 if t else T0
                    for k in range(2):
                        last = nc.tensor.transpose(dst[:, k * S + t * T0:k * S + t * T0 + m],
                                                   x_norm[0:m, t, 128 * k:128 * k + 128], ident[0:m, 0:m])
                last.then_inc(ring_full, 1)

            def v_product(i, part, n):
                dst = use(part, i, ("v", n))
                if n == 0:
                    pe.wait_ge(ring_dve, position(part, i, ("xt", 0), "d"))
                t, c = n // 4, n % 4
                m = T1 if t else T0
                cols = slice(2 * W + c * 2 * D, 2 * W + (c + 1) * 2 * D)
                passes(dst[0:m, 0:2 * D], products(x_side(t), w_side(cols))).then_inc(ring_full, 1)

            def zt(part, i, b):
                dst = use(part, i, ("zt", 0))
                pe.wait_ge(z_ready, b + 1)
                for t in range(2):
                    m = T1 if t else T0
                    nc.tensor.transpose(dst[:, t * T0:t * T0 + m], z_row[0:m, t, 0:128], ident[0:m, 0:m])
                    last = nc.tensor.transpose(dst[0:D1, S + t * T0:S + t * T0 + m], z_row[0:m, t, 128:D], ident[0:m, 0:m])
                last.then_inc(ring_full, 1)

            def gate(part, i, b):
                dst = use(part, i, ("log", 0))
                pe.wait_ge(ring_act, position(part, i, ("zt", 0), "a"))
                for t in range(2):
                    m = T1 if t else T0
                    cols = slice(t * T0, t * T0 + m)
                    last = passes(dst[0:m, t * E:(t + 1) * E], [(z_t[:, 0, cols], gate_t[:, 0, :]), (z_t[0:D1, 1, cols], gate_t[0:D1, 1, :])])
                last.then_inc(ring_full, 1)

            def counting(part, i, b):
                dst = use(part, i, ("cnt", 0))
                pe.wait_ge(chosen, b + 1)
                m0, m1 = picks[:, 0, :], picks[:, 1, :]
                passes(dst[0:T0, 0:E], [(earlier_r[:], m0)])
                passes(dst[0:T0, E:2 * E], [(ones_r[:], m0), (earlier_r[:], m1)])
                passes(dst[0:T0, 2 * E:3 * E], [(ones_r[:], m0), (ones_r[:], m1)]).then_inc(ring_full, 1)

            def scores(i, g):
                if g < 2:
                    if not (isinstance(i, int) and i == 0):
                        pe.wait_ge(exp_done, i * HEADS + (g - 1))
                else:
                    pe.wait_ge(exp_done, i * HEADS + (g - 1))
                dst = score_bank[g % 2]
                keys = slice(S * g, S * g + SP)
                for t in range(2):
                    rows = slice(S * g + T0 * t, S * g + T0 * (t + 1))
                    last = passes(dst[0:T0, t * SP:(t + 1) * SP], [
                        (q_h[:, 0, rows], k_h[:, keys]), (q_h[:, 0, rows], k_l[:, keys]), (q_l[:, rows], k_h[:, keys]),
                        (q_h[:, 1, rows], k_hl[:, keys]), (q_l1[:, rows], k_hl[0:64, keys])])
                last.then_inc(scores_full, 1)

            def probs_turn(i, g):
                if not (isinstance(i, int) and i == 0 and g == 0):
                    pe.wait_ge(probs_t_low, i * HEADS + g)
                pe.wait_ge(probs_ready, i * HEADS + (g + 1))
                for kt in range(2):
                    for t in range(2):
                        last = nc.tensor.transpose(probs_t_bank[0:T0, kt * SP + t * T0:kt * SP + (t + 1) * T0],
                                                   probs[:, g % 3, t, kt * T0:(kt + 1) * T0], ident[0:T0, 0:T0])
                last.then_inc(probs_t_full, 1)

            def pv(i, part, g):
                dst = use(part, i, ("pv", g))
                pe.wait_ge(probs_t_low, i * HEADS + (g + 1))
                pe.wait_ge(v_ready, i * HEADS + (g + 1))
                for d0, d1, col in ((0, 128, 0), (128, D, SP)):
                    pairs = []
                    for kt in range(2):
                        ph, pl = pt2_h[:, g % 2, kt, :], pt2_l[:, g % 2, kt, :]
                        vh, vl = v_h[:, g, kt, d0:d1], v_l[:, g, kt, d0:d1]
                        pairs += [(vh, ph), (vh, pl), (vl, ph)]
                    last = passes(dst[0:d1 - d0, col:col + SP], pairs)
                last.then_inc(ring_full, 1)

            def project(i, part):
                pe.wait_ge(ring_dve, position(part, i, ("pv", HEADS - 1), "d"))
                for t in range(2):
                    dst = use(part, i, ("y", t))
                    m = T1 if t else T0
                    pairs = []
                    for j in range(HEADS):
                        first = HEADS * T0 * t + j
                        rows = slice(first, first + HEADS * (m - 1) + 1, HEADS)
                        oh, ol, ohh, ol1 = o_h[:, 0, rows], o_l[:, rows], o_h[:, 1, rows], o_l1[:, rows]
                        pairs += [(oh, wp_h[:, j, :]), (oh, wp_l[:, j, :]), (ol, wp_h[:, j, :]),
                                  (ohh, wp_hl[:, j, :]), (ol1, wp_hl[0:64, j, :])]
                    passes(dst[0:m, 0:D], pairs).then_inc(ring_full, 1)

            def turn(i, part):
                nxt = part != "last"
                for s in range(2, HEADS + 3):
                    if s < HEADS:
                        scores(i, s)
                    if s < HEADS + 2:
                        probs_turn(i, s - 2)
                    if s == COUNT_STEP and part != "first":
                        counting(part, i, i - 1)
                    if s == XT_STEP and nxt:
                        xt(i, part, i + 1)
                    if 0 <= s - 3:
                        pv(i, part, s - 3)
                    for n in V_CHUNKS[s - HEADS] if nxt and s >= HEADS else []:
                        v_product(i, part, n)
                project(i, part)
                if nxt:
                    for n in range(4):
                        qk(i, part, "q", n)
                    for n in range(4):
                        qk(i, part, "k", n)
                zt(part, i, i)
                if nxt:
                    v_product(i, part, 4)
                    v_product(i, part, 5)
                    pe.wait_ge(q_doubled, i * 16 + 32)
                    pe.wait_ge(ring_dve, position(part, i, ("k", 3), "d"))
                    scores(i + 1, 0)
                gate(part, i, i)
                if nxt:
                    v_product(i, part, 6)
                    scores(i + 1, 1)
                    v_product(i, part, 7)

            xt(0, "before", 0)
            for n in range(8):
                v_product(0, "before", n)
            for kind in "qk":
                for n in range(4):
                    qk(0, "before", kind, n)
            pe.wait_ge(q_doubled, 16)
            pe.wait_ge(ring_dve, position("before", 0, ("k", 3), "d"))
            for g in range(2):
                scores(0, g)
            turn(0, "first")
            with pe.Fori(1, LAST) as i:
                turn(i, "mid")
            turn(LAST, "last")
            counting("after", LAST, LAST)

            def up_turn(e, u):
                for k in range(2):
                    r = 2 * u + k
                    nc.tensor.transpose(bank[u][:, 256 * k:256 * k + 128], up_raw[:, r, 0:128], ident[:])
                    last = nc.tensor.transpose(bank[u][:, 256 * k + 128:256 * k + 256], up_raw[:, r, 128:256], ident[:])
                last.then_inc(ew_full, 1)

            def down_turn(e, u):
                for k in range(2):
                    cols = slice(128 * (2 * u + k), 128 * (2 * u + k) + 128)
                    nc.tensor.transpose(bank[4 + u][:, D * k:D * k + 128], down_raw[:, 0, cols], ident[:])
                    last = nc.tensor.transpose(bank[4 + u][:, D * k + 128:D * k + D], down_raw[0:D1, 1, cols], ident[0:D1, 0:D1])
                last.then_inc(ew_full, 1)

            pe.wait_ge(ring_dve, position("after", LAST, ("cnt", 0), "d"))
            pe.wait_ge(ring_act, uses.count("a").start(LAST) + uses.size("last", "a"))
            pe.wait_ge(ew_loaded, 64)
            for u in range(4):
                up_turn(0, u)
            for u in range(2):
                down_turn(0, u)
            pe.wait_ge(rows_scattered, 64 * B)
            nc.tensor.transpose(bank[7][0:1, 0:1], ident[0:1, 0:1], ident[0:1, 0:1]).then_inc(stage2_done, 1)
            pe.wait_ge(stage2_done, 4)

            def zs_turn(e, c):
                pe.wait_ge(z_scaled, e * CHUNKS + (c + 1))
                if c == 1 or (isinstance(e, int) and e == 0 and c == 0):
                    pe.wait_ge(ew_low, e * 6 + 6)
                else:
                    pe.wait_ge(zt_low, e * CHUNKS + c)
                for k in range(2):
                    for t in range(TILES):
                        last = nc.tensor.transpose(bank[4 + k][:, t * TM:(t + 1) * TM], zs[:, c % 2, t, 128 * k:128 * k + 128],
                                                   ident[0:TM, 0:TM])
                last.then_inc(zt_full, 1)

            def gate_up(e, c, ns):
                b = c % 2
                for n in ns:
                    r = n // 2 + HT * (n % 2)
                    if c or n >= 4:
                        pe.wait_ge(act_ready, e * (HT * CHUNKS) + (c * HT + n // 2 - 1))
                    passes(bank[n % 4][:, 0:CN], [
                        (up_w[:, r, 0, :], zst_h[:, b, 0, :]), (up_l[:, r, :], zst_h[:, b, 0, :]), (up_w[:, r, 0, :], zst_l[:, b, 0, :]),
                        (up_w[:, r, 1, :], zst_h[:, b, 1, :]), (up_w[0:64, r, 1, :], zst_l[0:64, b, 1, :])]).then_inc(gu_full, 1)

            def down(e, c, first):
                if c == 0:
                    pe.wait_ge(ew_low, e * 6 + 6)
                pe.wait_ge(act_low, e * (HT * CHUNKS) + HT * (c + 1))
                if not (first and c == 0):
                    pe.wait_ge(y_ready, e * CHUNKS + c)
                for t in range(TILES):
                    rows = slice(t * TM, (t + 1) * TM)
                    pairs = []
                    for h in range(HT):
                        ah, al = act_h[:, c % 2, h, rows], act_l[:, c % 2, h, rows]
                        pairs += [(ah, down_h[:, h, :]), (ah, down_l[:, h, :]), (al, down_h[:, h, :])]
                    last = passes(bank[6 + t // 2][0:TM, (t % 2) * D:(t % 2) * D + D], pairs)
                    if t % 2:
                        last.then_inc(y_full, 1)

            def turn3(e, first, nxt):
                pe.wait_ge(ew_low, e * 6 + 4)
                for c in range(CHUNKS):
                    pe.wait_ge(zt_low, e * CHUNKS + (c + 1))
                    gate_up(e, c, range(HT))
                    if c + 1 < CHUNKS:
                        zs_turn(e, c + 1)
                    elif nxt:
                        zs_turn(e + 1, 0)
                    gate_up(e, c, range(HT, 2 * HT))
                    if 0 < c < CHUNKS - 1:
                        down(e, c - 1, first)
                if nxt:
                    pe.wait_ge(ew_loaded, e * 64 + 128)
                    pe.wait_ge(act_ready, (e + 1) * (HT * CHUNKS) - 1)
                    for u in range(2):
                        up_turn(e + 1, u)
                down(e, CHUNKS - 2, first)
                if nxt:
                    pe.wait_ge(act_ready, (e + 1) * (HT * CHUNKS))
                    for u in range(2, 4):
                        up_turn(e + 1, u)
                down(e, CHUNKS - 1, first)
                if nxt:
                    pe.wait_ge(zt_low, (e + 1) * CHUNKS + 1)
                    for u in range(2):
                        down_turn(e + 1, u)

            zs_turn(0, 0)
            turn3(0, True, True)
            with pe.Fori(1, E - 1) as e:
                turn3(e, False, True)
            turn3(E - 1, False, False)


_INS = ["x", "txt", "L0_tok_W", "L0_tok_b", "L0_tok_cls_tok", "L0_tok_pos_emb", "L0_attn_W_qkv", "L0_attn_b_qkv",
        "L0_attn_W_proj", "L0_attn_b_proj", "L0_ffn_gate_w", "L0_ffn_w13", "L0_ffn_w2", "L0_ffn_norm_w"]


def slots_of(tokens, experts):
    capacity = -(-5 * TOP_K * tokens // (4 * experts))
    tile = -(-capacity // (CHUNKS * TILES))
    return CHUNKS * TILES * (tile + tile % 2)


def kernel(**inputs):
    import numpy as np
    import concourse.bacc as bacc
    from concourse.bass_utils import run_bass_kernel_spmd

    nc = bacc.Bacc("TRN2", target_bir_lowering=False, num_devices=1)
    arrays, args = {}, []
    for name in _INS:
        a = np.ascontiguousarray(inputs[name])
        arrays[f"in_{name}"] = a
        args.append(nc.dram_tensor(f"in_{name}", a.shape, mybir.dt.from_np(a.dtype), kind="ExternalInput").ap())
    batch, text, width = arrays["in_txt"].shape
    grid = arrays["in_x"].shape[2] // PATCH
    tokens = batch * (grid * grid + 1 + text)
    rows = tokens + slots_of(tokens, arrays["in_L0_ffn_gate_w"].shape[0])
    out = nc.dram_tensor("out_rows", (rows, width), F32, kind="ExternalOutput").ap()
    build(nc, *args, out)
    r = run_bass_kernel_spmd(nc, [arrays], core_ids=[0])
    return r.results[0]["out_rows"][:tokens].reshape(batch, -1, width)
```
